# Optimizing a Trainium2 kernel written in Bass

```python
import numpy as np
import jax
import jax.numpy as jnp

def _softmax(x, axis=-1):
    return jax.nn.softmax(x, axis=axis)

def _gelu(x):
    return jax.nn.gelu(x, approximate=True)

def _silu(x):
    return jax.nn.silu(x)

def _sigmoid(x):
    return jax.nn.sigmoid(x)

def _layernorm(x, axis=-1, eps=1e-05):
    m = jnp.mean(x, axis=axis, keepdims=True)
    v = jnp.var(x, axis=axis, keepdims=True)
    return (x - m) / jnp.sqrt(v + eps)

def _scatter_add(tgt, idx, src, axis=0):
    return tgt.at[idx].add(src)

def _segment_sum(src, seg, n):
    return jax.ops.segment_sum(src, seg, n)
kernel_name = 'mk_gnn_ffn_d2_gnn_r32_c98422'

def setup_inputs(seed: int=0):
    np.random.seed(seed)
    _w = jnp.asarray

    def _rec_inputs():
        import jax
        import jax.numpy as jnp
        _gk = jax.random.key(seed)
        x = -0.0003713 + 1 * jax.random.normal(jax.random.fold_in(_gk, 1), (3125, 256), jnp.float32)
        src = jax.random.randint(jax.random.fold_in(_gk, 2), (50000,), 0, 3125, jnp.int32)
        dst = jax.random.randint(jax.random.fold_in(_gk, 3), (50000,), 0, 3125, jnp.int32)
        _o = jnp.argsort(dst, stable=True)
        src = src[_o]
        dst = dst[_o]
        edge_weight = jax.random.uniform(jax.random.fold_in(_gk, 12), (50000,), jnp.float32, 0.0, 0.999999)
        return (x, src, dst, edge_weight)
    x, src, dst, edge_weight = _rec_inputs()

    def _L0_gnn_setup():
        import jax, jax.numpy as jnp
        import numpy as np
        N = 50000
        E = 50000
        D = 256
        P = 64
        K = 3

        def _gcn_conv(h, src, dst, W, b):
            n = h.shape[0]
            loops = jnp.arange(n, dtype=src.dtype)
            row = jnp.concatenate([src, loops])
            col = jnp.concatenate([dst, loops])
            deg = jax.ops.segment_sum(jnp.ones_like(col, dtype=h.dtype), col, num_segments=n)
            dinv = jax.lax.rsqrt(jnp.maximum(deg, 1e-12))
            norm = dinv[row] * dinv[col]
            hw = h @ W
            msg = hw[row] * norm[:, None]
            return jax.ops.segment_sum(msg, col, num_segments=n) + b
        key = jax.random.key(seed)
        ks = jax.random.split(key, 12)
        s = 0.05
        return {'x': jax.random.normal(ks[0], (N, D), jnp.float32), 'edge_index': jax.random.randint(ks[1], (2, E), 0, N, dtype=jnp.int64), 'W_static': jax.random.normal(ks[2], (K, P, P), jnp.float32) * s, 'b_static': jax.random.normal(ks[3], (K, P), jnp.float32) * s, 'W1': jax.random.normal(ks[4], (D, D // 2), jnp.float32) * s, 'b1': jax.random.normal(ks[5], (D // 2,), jnp.float32) * s, 'W2': jax.random.normal(ks[6], (D // 2, P), jnp.float32) * s, 'b2': jax.random.normal(ks[7], (P,), jnp.float32) * s, 'W_aggr': jax.random.normal(ks[8], (D, D), jnp.float32) * s, 'b_aggr': jax.random.normal(ks[9], (D,), jnp.float32) * s}
    _L0_gnn_all = _L0_gnn_setup()
    _L0_gnn_in = {k: v for k, v in _L0_gnn_all.items() if k in ('W_static', 'b_static', 'W1', 'b1', 'W2', 'b2', 'W_aggr', 'b_aggr')}
    del _L0_gnn_all

    def _L0_ffn_setup():
        import math
        import jax, jax.numpy as jnp
        import numpy as np
        CAPACITY_FACTOR = 1.25
        key = jax.random.key(seed)
        ks = jax.random.split(key, 5)
        B, L, D, F, E = (8, 256, 256, 1024, 8)
        h = jax.random.normal(ks[0], (B, L, D), dtype=jnp.float32)
        gate_w = jax.random.normal(ks[1], (D, E), dtype=jnp.float32) * 0.02
        gate_b = jnp.zeros((E,), dtype=jnp.float32)
        w1 = jax.random.normal(ks[2], (E, D, F), dtype=jnp.float32) * (1.0 / math.sqrt(D))
        b1 = jnp.zeros((E, F), dtype=jnp.float32)
        w2 = jax.random.normal(ks[3], (E, F, D), dtype=jnp.float32) * (1.0 / math.sqrt(F))
        b2 = jnp.zeros((E, D), dtype=jnp.float32)
        return {'h': h, 'gate_w': gate_w, 'gate_b': gate_b, 'w1': w1, 'b1': b1, 'w2': w2, 'b2': b2}
    _L0_ffn_all = _L0_ffn_setup()
    _L0_ffn_in = {k: v for k, v in _L0_ffn_all.items() if k in ('gate_w', 'gate_b', 'w1', 'b1', 'w2', 'b2')}
    del _L0_ffn_all

    def _L1_gnn_setup():
        import jax, jax.numpy as jnp
        import numpy as np
        N = 50000
        D = 256
        E = 50000
        BN_EPS = 1e-05

        def gcn_conv(x, src, dst, w, W, b, n):
            xw = x @ W
            deg = jax.ops.segment_sum(w, dst, num_segments=n)
            dinv = jnp.where(deg > 0, jax.lax.rsqrt(deg), 0.0)
            norm = dinv[src] * w * dinv[dst]
            out = jax.ops.segment_sum(xw[src] * norm[:, None], dst, num_segments=n)
            return out + b
        key = jax.random.key(seed)
        ks = jax.random.split(key, 9)
        x = jax.random.normal(ks[0], (N, D), dtype=jnp.float32)
        edge_index = jax.random.randint(ks[1], (2, E), 0, N, dtype=jnp.int64)
        edge_weight = jax.random.uniform(ks[2], (E,), dtype=jnp.float32)
        s = 1.0 / np.sqrt(D)
        W1 = jax.random.uniform(ks[3], (D, D), minval=-s, maxval=s, dtype=jnp.float32)
        b1 = jnp.zeros((D,), dtype=jnp.float32)
        W2 = jax.random.uniform(ks[4], (D, D), minval=-s, maxval=s, dtype=jnp.float32)
        b2 = jnp.zeros((D,), dtype=jnp.float32)
        gamma = jnp.ones((D,), dtype=jnp.float32)
        beta = jnp.zeros((D,), dtype=jnp.float32)
        return {'x': x, 'edge_index': edge_index, 'edge_weight': edge_weight, 'W1': W1, 'b1': b1, 'W2': W2, 'b2': b2, 'gamma': gamma, 'beta': beta}
    _L1_gnn_all = _L1_gnn_setup()
    _L1_gnn_in = {k: v for k, v in _L1_gnn_all.items() if k in ('W1', 'b1', 'W2', 'b2', 'gamma', 'beta')}
    del _L1_gnn_all

    def _L1_ffn_setup():
        import jax, jax.numpy as jnp
        import numpy as np
        E = 8
        K = 2
        D = 256
        H = 512
        DOUT = 256
        EPS = 1e-05
        key = jax.random.key(seed)
        ks = jax.random.split(key, 9)
        s = 0.02
        return {'x': jax.random.normal(ks[0], (4, 256, D), jnp.float32), 'gamma': 1.0 + 0.05 * jax.random.normal(ks[1], (D,), jnp.float32), 'beta': 0.05 * jax.random.normal(ks[2], (D,), jnp.float32), 'Wr': 0.01 * jax.random.normal(ks[3], (D, E), jnp.float32), 'br': jnp.zeros((E,), jnp.float32), 'W1': s * jax.random.normal(ks[4], (E, D, H), jnp.float32), 'b1': s * jax.random.normal(ks[5], (E, H), jnp.float32), 'W2': s * jax.random.normal(ks[6], (E, H, DOUT), jnp.float32), 'b2': s * jax.random.normal(ks[7], (E, DOUT), jnp.float32)}
    _L1_ffn_all = _L1_ffn_setup()
    _L1_ffn_in = {k: v for k, v in _L1_ffn_all.items() if k in ('gamma', 'beta', 'Wr', 'br', 'W1', 'b1', 'W2', 'b2')}
    del _L1_ffn_all
    return {'x': x, 'src': src, 'dst': dst, 'edge_weight': edge_weight, 'L0_gnn_W_static': _L0_gnn_in['W_static'], 'L0_gnn_b_static': _L0_gnn_in['b_static'], 'L0_gnn_W1': _L0_gnn_in['W1'], 'L0_gnn_b1': _L0_gnn_in['b1'], 'L0_gnn_W2': _L0_gnn_in['W2'], 'L0_gnn_b2': _L0_gnn_in['b2'], 'L0_gnn_W_aggr': _L0_gnn_in['W_aggr'], 'L0_gnn_b_aggr': _L0_gnn_in['b_aggr'], 'L0_ffn_gate_w': _L0_ffn_in['gate_w'], 'L0_ffn_gate_b': _L0_ffn_in['gate_b'], 'L0_ffn_w1': _L0_ffn_in['w1'], 'L0_ffn_b1': _L0_ffn_in['b1'], 'L0_ffn_w2': _L0_ffn_in['w2'], 'L0_ffn_b2': _L0_ffn_in['b2'], 'L1_gnn_W1': _L1_gnn_in['W1'], 'L1_gnn_b1': _L1_gnn_in['b1'], 'L1_gnn_W2': _L1_gnn_in['W2'], 'L1_gnn_b2': _L1_gnn_in['b2'], 'L1_gnn_gamma': _L1_gnn_in['gamma'], 'L1_gnn_beta': _L1_gnn_in['beta'], 'L1_ffn_gamma': _L1_ffn_in['gamma'], 'L1_ffn_beta': _L1_ffn_in['beta'], 'L1_ffn_Wr': _L1_ffn_in['Wr'], 'L1_ffn_br': _L1_ffn_in['br'], 'L1_ffn_W1': _L1_ffn_in['W1'], 'L1_ffn_b1': _L1_ffn_in['b1'], 'L1_ffn_W2': _L1_ffn_in['W2'], 'L1_ffn_b2': _L1_ffn_in['b2']}

def reference(x, src, dst, edge_weight, L0_gnn_W_static, L0_gnn_b_static, L0_gnn_W1, L0_gnn_b1, L0_gnn_W2, L0_gnn_b2, L0_gnn_W_aggr, L0_gnn_b_aggr, L0_ffn_gate_w, L0_ffn_gate_b, L0_ffn_w1, L0_ffn_b1, L0_ffn_w2, L0_ffn_b2, L1_gnn_W1, L1_gnn_b1, L1_gnn_W2, L1_gnn_b2, L1_gnn_gamma, L1_gnn_beta, L1_ffn_gamma, L1_ffn_beta, L1_ffn_Wr, L1_ffn_br, L1_ffn_W1, L1_ffn_b1, L1_ffn_W2, L1_ffn_b2):
    import jax
    import jax.numpy as jnp

    def _L0_gnn_ref(x, W_static, b_static, W1, b1, W2, b2, W_aggr, b_aggr, edge_index):
        import jax, jax.numpy as jnp
        import numpy as np
        N = 50000
        E = 50000
        D = 256
        P = 64
        K = 3

        def _gcn_conv(h, src, dst, W, b):
            n = h.shape[0]
            loops = jnp.arange(n, dtype=src.dtype)
            row = jnp.concatenate([src, loops])
            col = jnp.concatenate([dst, loops])
            deg = jax.ops.segment_sum(jnp.ones_like(col, dtype=h.dtype), col, num_segments=n)
            dinv = jax.lax.rsqrt(jnp.maximum(deg, 1e-12))
            norm = dinv[row] * dinv[col]
            hw = h @ W
            msg = hw[row] * norm[:, None]
            return jax.ops.segment_sum(msg, col, num_segments=n) + b
        src, dst = (edge_index[0], edge_index[1])
        x_conv = x[:, :P]
        x_skip = x[:, P:]
        x_static = x_conv
        for i in range(K):
            x_static = jax.nn.relu(_gcn_conv(x_static, src, dst, W_static[i], b_static[i]))
        ew = jax.nn.gelu(x @ W1 + b1, approximate=False) @ W2 + b2
        x_dyn = x_conv[dst] * ew[src]
        x_dyn_agg = jax.ops.segment_sum(x_dyn, src, num_segments=x.shape[0])
        x_out = x_static + x_dyn_agg
        x_full = jnp.concatenate([x_out, x_skip], axis=-1)
        return x_full @ W_aggr + b_aggr

    def _L0_ffn_ref(h, gate_w, gate_b, w1, b1, w2, b2):
        import math
        import jax, jax.numpy as jnp
        import numpy as np
        CAPACITY_FACTOR = 1.25
        B, L, D = h.shape
        E = gate_w.shape[1]
        T = B * L
        C = max(1, math.ceil(CAPACITY_FACTOR * T / E))
        x = h.reshape(T, D)
        logits = x @ gate_w + gate_b
        probs = jax.nn.softmax(logits, axis=-1)
        idx = jnp.argmax(probs, axis=-1)
        prb = jnp.take_along_axis(probs, idx[:, None], axis=1)[:, 0]
        one_hot = jax.nn.one_hot(idx, E, dtype=jnp.float32)
        pos = (jnp.cumsum(one_hot, axis=0) * one_hot).sum(-1).astype(jnp.int32) - 1
        kept = pos < C
        pos_safe = jnp.where(kept, pos, C)
        buf = jnp.zeros((E, C, D), dtype=h.dtype).at[idx, pos_safe].set(x, mode='drop')
        hmid = jax.nn.relu(jnp.einsum('ecd,edf->ecf', buf, w1) + b1[:, None, :])
        ybuf = jnp.einsum('ecf,efd->ecd', hmid, w2) + b2[:, None, :]
        pos_g = jnp.minimum(pos, C - 1)
        y_tok = ybuf[idx, pos_g] * (prb * kept)[:, None]
        y = y_tok.reshape(B, L, D)
        y = jnp.nan_to_num(y, nan=0.0, posinf=10000.0, neginf=-10000.0)
        return y

    def _L1_gnn_ref(x, edge_index, edge_weight, W1, b1, W2, b2, gamma, beta):
        import jax, jax.numpy as jnp
        import numpy as np
        N = 50000
        D = 256
        E = 50000
        BN_EPS = 1e-05

        def gcn_conv(x, src, dst, w, W, b, n):
            xw = x @ W
            deg = jax.ops.segment_sum(w, dst, num_segments=n)
            dinv = jnp.where(deg > 0, jax.lax.rsqrt(deg), 0.0)
            norm = dinv[src] * w * dinv[dst]
            out = jax.ops.segment_sum(xw[src] * norm[:, None], dst, num_segments=n)
            return out + b
        n = x.shape[0]
        loop = jnp.arange(n, dtype=edge_index.dtype)
        src = jnp.concatenate([edge_index[0], loop])
        dst = jnp.concatenate([edge_index[1], loop])
        w = jnp.concatenate([edge_weight, jnp.ones((n,), dtype=edge_weight.dtype)])
        identity = x
        out = gcn_conv(x, src, dst, w, W1, b1, n)
        out = jax.nn.relu(out)
        out = gcn_conv(out, src, dst, w, W2, b2, n)
        mean = out.mean(axis=0)
        var = out.var(axis=0)
        out = (out - mean) * jax.lax.rsqrt(var + BN_EPS) * gamma + beta
        out = out + identity
        return jax.nn.relu(out)

    def _L1_ffn_ref(x, gamma, beta, Wr, br, W1, b1, W2, b2):
        import jax, jax.numpy as jnp
        import numpy as np
        E = 8
        K = 2
        D = 256
        H = 512
        DOUT = 256
        EPS = 1e-05
        mu = jnp.mean(x, axis=-1, keepdims=True)
        var = jnp.mean(jnp.square(x - mu), axis=-1, keepdims=True)
        xn = (x - mu) * jax.lax.rsqrt(var + EPS) * gamma + beta
        logits = jnp.einsum('bsd,de->bse', xn, Wr) + br
        top_vals, top_idx = jax.lax.top_k(logits, K)
        w = jax.nn.softmax(top_vals, axis=-1)
        w_full = jnp.einsum('bsk,bske->bse', w, jax.nn.one_hot(top_idx, E, dtype=w.dtype))
        y = jnp.zeros(x.shape[:-1] + (DOUT,), x.dtype)
        for e in range(E):
            h = jax.nn.gelu(jnp.einsum('bsd,dh->bsh', xn, W1[e]) + b1[e], approximate=False)
            y_e = jnp.einsum('bsh,hd->bsd', h, W2[e]) + b2[e]
            y = y + y_e * w_full[..., e, None]
        return y
    edge_index = jnp.stack([src, dst])
    x = x + _L0_gnn_ref(_layernorm(x, axis=-1), L0_gnn_W_static, L0_gnn_b_static, L0_gnn_W1, L0_gnn_b1, L0_gnn_W2, L0_gnn_b2, L0_gnn_W_aggr, L0_gnn_b_aggr, edge_index)
    x = x + _L0_ffn_ref(_layernorm(x, axis=-1)[None], L0_ffn_gate_w, L0_ffn_gate_b, L0_ffn_w1, L0_ffn_b1, L0_ffn_w2, L0_ffn_b2)[0]
    x = x + _L1_gnn_ref(_layernorm(x, axis=-1), edge_index, edge_weight, L1_gnn_W1, L1_gnn_b1, L1_gnn_W2, L1_gnn_b2, L1_gnn_gamma, L1_gnn_beta)
    x = x + _L1_ffn_ref(_layernorm(x, axis=-1)[None], L1_ffn_gamma, L1_ffn_beta, L1_ffn_Wr, L1_ffn_br, L1_ffn_W1, L1_ffn_b1, L1_ffn_W2, L1_ffn_b2)[0]
    return x

_drawn_inputs = setup_inputs


def setup_inputs(seed=0):
    import zlib

    import numpy as np

    out = dict(_drawn_inputs(seed))
    spreads = {'L0_ffn_gate_b': (0.0, 0.1),
     'L0_ffn_b1': (0.0, 0.719),
     'L0_ffn_b2': (0.0, 0.508),
     'L1_gnn_b1': (0.0, 0.1),
     'L1_gnn_b2': (0.0, 2.0),
     'L1_gnn_gamma': (1.0, 0.2),
     'L1_gnn_beta': (0.0, 0.1),
     'L1_ffn_br': (0.0, 0.393)}
    factors = {'L0_gnn_W_static': 8.0,
     'L0_gnn_b_static': 3.367,
     'L1_ffn_gamma': 8.0,
     'L1_ffn_beta': 8.0,
     'L1_ffn_b1': 24.628,
     'L1_ffn_b2': 8.0}
    for name, (base, spread) in spreads.items():
        noise = np.random.default_rng([zlib.crc32(name.encode()), seed]).standard_normal(out[name].shape)
        drawn = base * np.exp(spread * noise) if base else spread * noise
        out[name] = jnp.asarray(drawn.astype(out[name].dtype))
    for name, factor in factors.items():
        out[name] = (out[name] * factor).astype(out[name].dtype)
    return out
```

```python
from contextlib import ExitStack, contextmanager

import concourse.bass as bass
from concourse import mybir

F32 = mybir.dt.float32
BF16 = mybir.dt.bfloat16
F16 = mybir.dt.float16
I32 = mybir.dt.int32
U32 = mybir.dt.uint32
ALU = mybir.AluOpType
ACT = mybir.ActivationFunctionType
AX = mybir.AxisListType

N, D, E = 3125, 256, 50000
P = 125
T = N // P
NB = T * T
EC = E // P
C0 = 64
NO_LANE = 127
EMPTY = float(NO_LANE * 128 + NO_LANE)
PAST = float(1 << 20)
ROUND = float(3 << 22)


class Step:

    def __init__(self, engine, semaphore):
        self.engine, self.semaphore, self.count = engine, semaphore, 0

    def __call__(self, instruction):
        self.count += 1
        instruction.then_inc(self.semaphore, 1)
        self.engine.wait_ge(self.semaphore, self.count)


@contextmanager
def stage(nc):
    sems = []

    def sem(name):
        sems.append(nc.alloc_semaphore(name=name))
        return sems[-1]

    with ExitStack() as ctx:
        yield ctx, sem
    nc.all_engine_barrier()
    nc.clear_and_free_semaphores(sems)
    nc.all_engine_barrier()


def sort_edges(nc, g):
    G = 16
    TRIPS = EC // G
    Q = G // 4
    HB = (NB + 1) // 2
    with stage(nc) as (ctx, sem):
        sb = lambda n, s, d: ctx.enter_context(nc.sbuf_tensor(n, s, d))
        src_i, dst_i = sb("src_i", [P, EC], I32), sb("dst_i", [P, EC], I32)
        local = sb("local", [P, 2, EC], F32)
        tile_of = sb("tile_of", [P, 2, EC], F32)
        tmp = sb("tmp_edge", [P, EC], F32)
        key = sb("key", [P, EC], F32)
        keyp = sb("keyp", [P, EC], F32)
        rec = sb("rec", [P, EC, 2], F32)
        blank = sb("blank", [P, NB, 2], F32)
        iota_nb = sb("iota_nb", [P, 2, HB], F16)
        ones_nb = sb("ones_nb", [P, P], BF16)
        before = sb("before", [P, P], BF16)
        rest = sb("rest", [P, P], BF16)
        hot = sb("hot", [P, G, 2, HB], BF16)
        junk = sb("junk", [P, 2, 2, HB], BF16)
        rank = sb("rank_ring", [P, G], F32)
        over = sb("over", [P, 4], F32)
        pos = sb("pos", [P, 4], F32)
        idx = sb("idx", [P, Q, 4], U32)
        staged = sb("staged", [P, Q, 4, 2], F32)
        count = [ctx.enter_context(nc.psum_tensor(f"count{b}", [P, 2, 512], F32)) for b in range(2)]

        edges_in, blank_out = sem("edges_in"), sem("blank_out")
        consts, prep, w_placed = sem("consts"), sem("prep"), sem("w_placed")
        dve_step, pos_step = sem("dve_step_a"), sem("pos_step")
        hot_ready, counted, rank_read = sem("hot_ready"), sem("counted"), sem("rank_read")
        idx_ready, stage_ready = sem("idx_ready"), sem("stage_ready")
        pool_read, scatter_go = sem("pool_read"), sem("scatter_go")
        scattered = [sem(f"scattered{h}") for h in range(Q)]

        with nc.Block() as block:
            @block.sync
            def _(sp):
                sp.dma_start(src_i[:], g.src.rearrange("(p t) -> p t", p=P)).then_inc(edges_in, 16)
                sp.dma_start(dst_i[:], g.dst.rearrange("(p t) -> p t", p=P)).then_inc(edges_in, 16)
                sp.dma_start(tmp[:], g.edge_weight.rearrange("(p t) -> p t", p=P)).then_inc(edges_in, 16)
                sp.wait_ge(consts, 1)
                sp.dma_start(g.slots.rearrange("(p n) k -> p (n k)", p=P),
                             blank[:].rearrange("p n k -> p (n k)")).then_inc(blank_out, 16)
                sp.wait_ge(blank_out, 16)

            @block.gpsimd
            def _(pool):
                pool.memset(blank[:, :, 0], 0.0)
                pool.memset(blank[:, :, 1], EMPTY).then_inc(consts, 1)
                pool.iota(iota_nb[:], pattern=[[HB, 2], [1, HB]], base=0, channel_multiplier=0,
                          allow_small_or_imprecise_dtypes=True).then_inc(consts, 1)
                pool.memset(ones_nb[:], 1.0).then_inc(pool_read, 1)
                pool.wait_ge(pool_read, 1)
                pool.affine_select(out=before[:], in_=ones_nb[:], compare_op=ALU.is_gt, fill=0.0, base=0,
                                   pattern=[[1, P]], channel_multiplier=-1)
                pool.affine_select(out=rest[:], in_=ones_nb[:], compare_op=ALU.is_ge, fill=0.0, base=0,
                                   pattern=[[-1, P]], channel_multiplier=1).then_inc(consts, 1)
                pool.wait_ge(blank_out, 16)

                bound = pool.to_reg(NB * P - 1)

                def scatter(i, h):
                    pool.wait_ge(idx_ready, i * Q + h + 1)
                    pool.wait_ge(stage_ready, i * Q + h + 1)
                    pool.sem_inc(scatter_go)
                    for u in range(4):
                        pool.indirect_dma_start(
                            out=g.slots, out_offset=bass.IndirectOffsetOnAxis(ap=idx[:, h, u:u + 1], axis=0),
                            in_=staged[:, h, u, :], in_offset=None, bounds_check=bound,
                            oob_is_err=False).then_inc(scattered[h], 16)

                with pool.Fori(0, TRIPS) as i:
                    for h in range(Q):
                        scatter(i, h)
                for h in range(Q):
                    pool.wait_ge(scattered[h], TRIPS * 64)

            @block.scalar
            def _(act):
                act.wait_ge(edges_in, 48)
                nc.scalar.copy(rec[:, :, 0], tmp[:]).then_inc(w_placed, 1)
                act.wait_ge(prep, 1)
                act.wait_ge(w_placed, 1)

                def fill_stage(i, h, first):
                    if not first:
                        act.wait_ge(scattered[h], i * 64)
                    nc.scalar.copy(staged[:, h, :, :], rec[:, bass.ds(i * G + 4 * h, 4), :]).then_inc(stage_ready, 1)

                for h in range(Q):
                    fill_stage(0, h, True)
                with act.Fori(1, TRIPS) as i:
                    for h in range(Q):
                        fill_stage(i, h, False)

            @block.vector
            def _(dve):
                step = Step(dve, dve_step)
                dve.wait_ge(edges_in, 48)
                dve.wait_ge(w_placed, 1)
                for k, ids in enumerate((src_i, dst_i)):
                    step(nc.vector.tensor_copy(local[:, k, :], ids[:]))
                    step(nc.vector.tensor_scalar(tmp[:], local[:, k, :], 1.0 / P, -(P // 2) / P, ALU.mult, ALU.add))
                    step(nc.vector.tensor_scalar_add(tile_of[:, k, :], tmp[:], ROUND))
                    step(nc.vector.tensor_scalar_add(tmp[:], tile_of[:, k, :], -ROUND))
                    step(nc.vector.tensor_copy(tile_of[:, k, :], tmp[:]))
                    step(nc.vector.scalar_tensor_tensor(out=tmp[:], in0=tile_of[:, k, :], scalar=float(-P),
                                                        in1=local[:, k, :], op0=ALU.mult, op1=ALU.add))
                    step(nc.vector.tensor_copy(local[:, k, :], tmp[:]))
                step(nc.vector.scalar_tensor_tensor(out=key[:], in0=tile_of[:, 1, :], scalar=float(T),
                                                    in1=tile_of[:, 0, :], op0=ALU.mult, op1=ALU.add))
                step(nc.vector.tensor_scalar_mul(keyp[:], key[:], float(P)))
                step(nc.vector.scalar_tensor_tensor(out=rec[:, :, 1], in0=local[:, 0, :], scalar=128.0,
                                                    in1=local[:, 1, :], op0=ALU.mult, op1=ALU.add))
                nc.vector.tensor_copy(g.spare[:P, 0:1], key[:, 0:1]).then_inc(prep, 1)
                dve.wait_ge(consts, 3)

                def one_hot(t, slot):
                    nc.vector.tensor_scalar(hot[:, slot, :, :], iota_nb[:], key[:, bass.ds(t, 1)], None,
                                            ALU.is_equal).then_inc(hot_ready, 1)

                def read_rank(t, u, t_before):
                    dve.wait_ge(counted, t + 1)
                    if t_before is not None:
                        dve.wait_ge(rank_read, t_before)
                    nc.vector.tensor_tensor_reduce(
                        out=junk[:, u % 2], in0=hot[:, u], in1=count[u % 2][:, :, 0:HB], scale=1.0,
                        scalar=0.0, op0=ALU.mult, op1=ALU.add, accum_out=rank[:, u:u + 1]).then_inc(rank_read, 1)

                def positions(i, h, first):
                    dve.wait_ge(rank_read, i * G + 4 * h + 4)
                    nc.vector.tensor_copy(g.ranks[:, bass.ds(i * G + 4 * h, 4)], rank[:, 4 * h:4 * h + 4])
                    nc.vector.tensor_scalar(over[:], rank[:, 4 * h:4 * h + 4], float(P), PAST, ALU.is_ge,
                                            ALU.mult).then_inc(pos_step, 1)
                    nc.vector.tensor_tensor(pos[:], rank[:, 4 * h:4 * h + 4], keyp[:, bass.ds(i * G + 4 * h, 4)],
                                            ALU.add).then_inc(pos_step, 1)
                    dve.wait_ge(pos_step, (i * Q + h) * 2 + 2)
                    if not first:
                        dve.wait_ge(scattered[h], i * 64)
                    nc.vector.tensor_tensor(idx[:, h, :], pos[:], over[:], ALU.add).then_inc(idx_ready, 1)

                def trip(i, first=False, last=False):
                    for u in range(G):
                        if not (last and u >= G - 2):
                            one_hot(i * G + u + 2, (u + 2) % G)
                        read_rank(i * G + u, u, None if first and u < 2 else i * G + u - 1)
                        if u % 4 == 3:
                            positions(i, u // 4, first)

                one_hot(0, 0)
                one_hot(1, 1)
                trip(0, first=True)
                with dve.Fori(1, TRIPS - 1) as i:
                    trip(i)
                trip(TRIPS - 1, last=True)

            @block.tensor
            def _(pe):
                pe.wait_ge(consts, 3)

                def add(b, what, slot, start=False, inc=None):
                    for c in range(2):
                        mm = nc.tensor.matmul(count[b][:, c, 0:HB], what, hot[:, slot, c, :], start=start,
                                              stop=True, skip_group_check=True)
                    if inc is not None:
                        mm.then_inc(inc, 1)

                def tally(t, u, old=True, older=True):
                    if older:
                        pe.wait_ge(rank_read, t - 1)
                        add(u % 2, rest[:], (u - 2) % G)
                    if old:
                        add(u % 2, ones_nb[:], (u - 1) % G, start=not older)
                    pe.wait_ge(hot_ready, t + 1)
                    add(u % 2, before[:], u, start=not old, inc=counted)

                for u in range(G):
                    tally(u, u, old=u >= 1, older=u >= 2)
                with pe.Fori(1, TRIPS) as i:
                    for u in range(G):
                        tally(i * G + u, u)

GROUPS = [4, 3, 3, 3, 3, 3, 3, 3]
BASES = [sum(GROUPS[:j]) for j in range(len(GROUPS))]
NG = len(GROUPS)
EPS = 1e-5


def root(nc, act, value, out, ready, done):
    act.wait_ge(ready, 1)
    nc.scalar.activation(out, value, ACT.Sqrt).then_inc(done, 1)


def inverse_root(nc, dve, step, value, rooted, tmp, done):
    dve.wait_ge(done, 1)
    step(nc.vector.reciprocal(tmp, rooted))
    step(nc.vector.tensor_tensor(tmp, tmp, value, ALU.mult))
    step(nc.vector.tensor_tensor(tmp, tmp, rooted, ALU.add))
    step(nc.vector.tensor_scalar_mul(tmp, tmp, 0.5))
    step(nc.vector.reciprocal(value, tmp))


def layer_norm(nc, dve, step, x, xn, stats, small, rows_done, var_ready, rstd_ready):
    with dve.Fori(0, T) as t:
        nc.vector.bn_stats(stats[:, bass.ds(t, 1), :].rearrange("p a k -> p (a k)"),
                           x[:, bass.ds(t, 1), :].rearrange("p a k -> p (a k)")).then_inc(rows_done, 1)
    dve.wait_ge(rows_done, T)
    mean, var, dif, mean2 = (small[:, k, :] for k in range(4))
    step(nc.vector.tensor_tensor(mean, stats[:, :, 1], stats[:, :, 4], ALU.add))
    step(nc.vector.tensor_tensor(dif, stats[:, :, 1], stats[:, :, 4], ALU.subtract))
    step(nc.vector.tensor_tensor(var, stats[:, :, 2], stats[:, :, 5], ALU.add))
    step(nc.vector.tensor_scalar_mul(mean, mean, 0.5))
    step(nc.vector.tensor_tensor(dif, dif, dif, ALU.mult))
    step(nc.vector.tensor_scalar(dif, dif, 0.25, EPS, ALU.mult, ALU.add))
    nc.vector.scalar_tensor_tensor(out=var, in0=var, scalar=1.0 / D, in1=dif, op0=ALU.mult,
                                   op1=ALU.add).then_inc(var_ready, 1)
    inverse_root(nc, dve, step, var, mean2, dif, rstd_ready)
    with dve.Fori(0, T) as t:
        one = lambda a: a[:, bass.ds(t, 1), :].rearrange("p a k -> p (a k)")
        nc.vector.tensor_scalar(one(xn), one(x), mean[:, bass.ds(t, 1)], var[:, bass.ds(t, 1)], ALU.subtract,
                                ALU.mult).then_inc(rows_done, 1)
    dve.wait_ge(rows_done, 2 * T)


def split3(nc, step, whole, parts, left):
    step(nc.vector.tensor_copy(parts(0), whole))
    step(nc.vector.tensor_tensor(left, whole, parts(0), ALU.subtract))
    step(nc.vector.tensor_copy(parts(1), left))
    step(nc.vector.tensor_tensor(left, left, parts(1), ALU.subtract))
    step(nc.vector.tensor_copy(parts(2), left))


def normalise_input(nc, g):
    with stage(nc) as (ctx, sem):
        sb = lambda n, s, d: ctx.enter_context(nc.sbuf_tensor(n, s, d))
        x, xn = sb("x_in", [P, T, D], F32), sb("xn_in", [P, T, D], F32)
        stats, small = sb("stats0", [P, T, 6], F32), sb("small0", [P, 4, T], F32)
        left = sb("left0", [P, T, C0], F32)
        x_in, xn_ready, xn_out = sem("x_in_done"), sem("xn_ready"), sem("xn_out")
        rows_done, dve_step = sem("rows_done0"), sem("dve_step0")
        var_ready, rstd_ready = sem("var_ready0"), sem("rstd_ready0")
        with nc.Block() as block:
            @block.scalar
            def _(act):
                root(nc, act, small[:, 1, :], small[:, 3, :], var_ready, rstd_ready)

            @block.sync
            def _(sp):
                sp.dma_start(x[:], g.x.rearrange("(t p) d -> p t d", p=P)).then_inc(x_in, 16)
                sp.wait_ge(xn_ready, 1)
                sp.dma_start(g.xn.rearrange("(t p) d -> p t d", p=P), xn[:]).then_inc(xn_out, 16)
                sp.wait_ge(xn_out, 16)

            @block.vector
            def _(dve):
                step = Step(dve, dve_step)
                dve.wait_ge(x_in, 16)
                layer_norm(nc, dve, step, x, xn, stats, small, rows_done, var_ready, rstd_ready)
                split3(nc, step, xn[:, :, 0:C0], lambda k: g.xparts[:, :, k, :], left[:])
                nc.vector.tensor_copy(g.spare[:P, 0:1], left[:, 0, 0:1]).then_inc(xn_ready, 1)


def load_slots(nc, g):
    CH = NB // P
    with stage(nc) as (ctx, sem):
        sb = lambda n, s, d: ctx.enter_context(nc.sbuf_tensor(n, s, d))
        raw = sb("raw_slots", [P, CH, P, 2], F32)
        turned = [ctx.enter_context(nc.psum_tensor(f"turned{k}", [P, 2, 512], F32)) for k in range(2)]
        code = sb("code", [P, NB], I32)
        field = sb("field", [P, 2, NB], I32)
        left = sb("left1", [P, NB], F32)
        part = sb("wpart", [P, NB], BF16)
        slots_in, turned_done, dve_step = sem("slots_in"), sem("turned_done"), sem("dve_step1")
        with nc.Block() as block:
            @block.sync
            def _(sp):
                sp.dma_start(raw[:].rearrange("q c e k -> q c (e k)"),
                             g.slots.rearrange("(c q e) k -> q c (e k)", c=CH, q=P)).then_inc(slots_in, 16)

            @block.tensor
            def _(pe):
                pe.wait_ge(slots_in, 16)
                for k in range(2):
                    for c in range(CH):
                        out = turned[k][:, c // 4, (c % 4) * P:(c % 4 + 1) * P]
                        nc.tensor.transpose(out, raw[:, c, :, k], g.ident[0:P, 0:P]).then_inc(turned_done, 1)

            @block.vector
            def _(dve):
                step = Step(dve, dve_step)
                dve.wait_ge(turned_done, 2 * CH)
                for c, (lo, hi) in enumerate(((0, 4 * P), (4 * P, NB))):
                    step(nc.vector.tensor_copy(g.slot_w[:, lo:hi], turned[0][:, c, 0:hi - lo]))
                    step(nc.vector.tensor_copy(code[:, lo:hi], turned[1][:, c, 0:hi - lo]))
                step(nc.vector.tensor_scalar(field[:, 0, :], code[:], 7, None, ALU.logical_shift_right))
                step(nc.vector.tensor_scalar(field[:, 1, :], code[:], 127, None, ALU.bitwise_and))
                step(nc.vector.tensor_copy(g.slot_ids[:], field[:]))
                step(nc.vector.memset(g.slot_deg[:, :, 0:1], 1.0))
                split3(nc, step, g.slot_w[:], lambda k: g.slot_deg[:, :, 1 + k], left[:])


def build_blocks(nc, g):
    R = 2
    with stage(nc) as (ctx, sem):
        sb = lambda n, s, d: ctx.enter_context(nc.sbuf_tensor(n, s, d))
        ps = lambda n: ctx.enter_context(nc.psum_tensor(n, [P, 512], F32))
        src16, dst16 = sb("src16", [P, R, 4, P], BF16), sb("dst16", [P, R, 4, P], BF16)
        src32, dst32 = sb("src32", [P, R, 4, P], F32), sb("dst32", [P, R, 4, P], F32)
        turned = sb("countT", [P, R, 4, P], BF16)
        strip = sb("strip", [P, R, 4 * P], F32)
        zero = sb("zero_deg", [P, T * 4], BF16)
        p_w, p_c, p_t = ([ps(f"p_{k}{r}") for r in range(R)] for k in "wct")
        p_deg, p_dyn = ps("p_deg"), ps("p_dyn")

        zeroed = sem("zeroed")
        hot16, hot_s32, hot_d32 = sem("hot16"), sem("hot_s32"), sem("hot_d32")
        blocks = sem("blocks")
        ev_c, ev_w, ev_t = sem("ev_c"), sem("ev_w"), sem("ev_t")
        spread = sem("spread")
        dyn_read = sem("dyn_read")
        strip_out = [sem(f"strip_out{r}") for r in range(R)]
        slot = lambda k, b, s: g.slot_ids[:, k, bass.ds(s + b * T, 1)]

        with nc.Block() as block:
            @block.vector
            def _(dve):
                nc.vector.memset(zero[:], 0.0).then_inc(zeroed, 1)

                def make(s, j, n, first):
                    r = j % R
                    if not (first and j < R):
                        dve.wait_ge(blocks, n - R + 1)
                        dve.wait_ge(hot_s32, n - R + 1)
                    for u in range(GROUPS[j]):
                        d = BASES[j] + u
                        nc.vector.tensor_scalar(src16[:, r, u, :], g.iota[:P, 0:P], slot(0, d, s), None, ALU.is_equal)
                        ins = nc.vector.tensor_scalar(dst16[:, r, u, :], g.iota[:P, 0:P], slot(1, d, s), None,
                                                      ALU.is_equal)
                    ins.then_inc(hot16, 1)

                def evacuate(s, j, n, first):
                    w = GROUPS[j] * P
                    dve.wait_ge(blocks, n + 1)
                    if not (first and j < R):
                        dve.wait_ge(spread, n - R + 1)
                    nc.vector.tensor_copy(turned[:, j % R, 0:GROUPS[j], :].rearrange("p u e -> p (u e)"),
                                          p_t[j % R][:P, 0:w]).then_inc(ev_t, 1)

                def read_dyn(s, count):
                    dve.wait_ge(spread, count * NG)
                    nc.vector.tensor_copy(g.dyn[:, bass.ds(s, 1), :].rearrange("p a k -> p (a k)"),
                                          p_dyn[:P, 0:C0]).then_inc(dyn_read, 1)

                def whole(s, first=False):
                    for j in range(NG):
                        n = s * NG + j
                        make(s, j, n, first)
                        if j == 0 and not first:
                            evacuate(s - 1, NG - 1, n - 1, False)
                        elif j > 0:
                            evacuate(s, j - 1, n - 1, first)
                        if j == 2 and not first:
                            read_dyn(s - 1, s)

                whole(0, first=True)
                with dve.Fori(1, T) as s:
                    whole(s)
                evacuate(T - 1, NG - 1, T * NG - 1, False)
                read_dyn(T - 1, T)
                dve.wait_ge(blocks, T * NG)
                nc.vector.tensor_copy(g.deg[:].rearrange("p t k -> p (t k)"), p_deg[:P, 0:T * 4])

            @block.scalar
            def _(act):
                def weigh(s, j, n, first):
                    r, k = j % R, GROUPS[j]
                    act.wait_ge(hot16, n + 1)
                    if not (first and j < R):
                        act.wait_ge(blocks, n - R + 1)
                    for u in range(k):
                        d = BASES[j] + u
                        ins = nc.scalar.activation(dst32[:, r, u, :], dst16[:, r, u, :], ACT.Copy,
                                                   scale=g.slot_w[:, bass.ds(s + d * T, 1)])
                    ins.then_inc(hot_d32, 1)
                    nc.scalar.copy(src32[:, r, 0:k, :], src16[:, r, 0:k, :]).then_inc(hot_s32, 1)

                def evacuate(s, j, n, first):
                    r, w, lo = j % R, GROUPS[j] * P, BASES[j] * P
                    act.wait_ge(blocks, n + 1)
                    nc.scalar.copy(g.counts[:, bass.ds(s, 1), lo:lo + w].rearrange("p a e -> p (a e)"),
                                   p_c[r][:P, 0:w]).then_inc(ev_c, 1)
                    if not (first and j < R):
                        act.wait_ge(strip_out[r], (s * (NG // R) + j // R) * 16)
                    nc.scalar.copy(strip[:, r, 0:w], p_w[r][:P, 0:w]).then_inc(ev_w, 1)

                def whole(s, first=False):
                    for j in range(NG):
                        weigh(s, j, s * NG + j, first)
                        if j > 0:
                            evacuate(s, j - 1, s * NG + j - 1, first)
                        elif not first:
                            evacuate(s - 1, NG - 1, s * NG - 1, False)

                whole(0, first=True)
                with act.Fori(1, T) as s:
                    whole(s)
                evacuate(T - 1, NG - 1, T * NG - 1, False)

            @block.sync
            def _(sp):
                with sp.Fori(0, T) as s:
                    for j in range(NG):
                        r, w, lo = j % R, GROUPS[j] * P, BASES[j] * P
                        sp.wait_ge(ev_w, s * NG + j + 1)
                        sp.dma_start(g.weights[bass.ds(s * P, P), lo:lo + w], strip[:, r, 0:w]).then_inc(strip_out[r], 16)
                for r in range(R):
                    sp.wait_ge(strip_out[r], T * NG // R * 16)

            @block.tensor
            def _(pe):
                pe.wait_ge(zeroed, 1)
                nc.tensor.matmul(p_deg[:P, 0:T * 4], g.iota[:P, 0:P], zero[:], start=True, stop=True,
                                 skip_group_check=True)

                def products(s, j, n, first):
                    r = j % R
                    pe.wait_ge(hot16, n + 1)
                    pe.wait_ge(hot_d32, n + 1)
                    pe.wait_ge(hot_s32, n + 1)
                    if not (first and j < R):
                        pe.wait_ge(ev_c, n - R + 1)
                        pe.wait_ge(ev_w, n - R + 1)
                        pe.wait_ge(ev_t, n - R + 1)
                    for u in range(GROUPS[j]):
                        d = BASES[j] + u
                        o = slice(u * P, (u + 1) * P)
                        nc.tensor.matmul(p_deg[:P, d * 4:d * 4 + 4], dst16[:, r, u, :],
                                         g.slot_deg[:, bass.ds(s + d * T, 1), :].rearrange("p a k -> p (a k)"),
                                         start=False, stop=True, skip_group_check=True)
                        nc.tensor.matmul(p_t[r][:P, o], dst16[:, r, u, :], src16[:, r, u, :], start=True, stop=True)
                        nc.tensor.matmul(p_c[r][:P, o], src16[:, r, u, :], dst16[:, r, u, :], start=True, stop=True)
                        mm = nc.tensor.matmul(p_w[r][:P, o], src32[:, r, u, :], dst32[:, r, u, :], start=True,
                                              stop=True)
                    mm.then_inc(blocks, 1)

                def spread_group(j, n, wait_dyn):
                    pe.wait_ge(ev_t, n + 1)
                    if wait_dyn is not None:
                        pe.wait_ge(dyn_read, wait_dyn)
                    for u in range(GROUPS[j]):
                        d = BASES[j] + u
                        for k in range(3):
                            mm = nc.tensor.matmul(p_dyn[:P, 0:C0], turned[:, j % R, u, :], g.xparts[:, d, k, :],
                                                  start=(d == 0 and k == 0), stop=(d == T - 1 and k == 2))
                    mm.then_inc(spread, 1)

                def whole(s, first=False):
                    for j in range(NG):
                        n = s * NG + j
                        products(s, j, n, first)
                        if j == 0 and not first:
                            spread_group(NG - 1, n - 1, None)
                        elif j > 0:
                            spread_group(j - 1, n - 1, s if j == 1 and not first else None)

                whole(0, first=True)
                with pe.Fori(1, T) as s:
                    whole(s)
                spread_group(NG - 1, T * NG - 1, None)

F = D // 128
QUADS = [(t, min(4, T - t)) for t in range(0, T, 4)]


def turn_tiles(nc, pe, rows, width, psum, ident, wait_free, turned):
    n = 0
    for t0, k in QUADS:
        for lo in range(0, width, 128):
            m = min(128, width - lo)
            if n >= len(psum):
                pe.wait_ge(wait_free, n - len(psum) + 1)
            for u in range(k):
                mm = nc.tensor.transpose(psum[n % len(psum)][0:m, u * P:(u + 1) * P], rows[:, t0 + u, lo:lo + m],
                                         ident[0:P, 0:P])
            mm.then_inc(turned, 1)
            n += 1


def static_convs(nc, g):
    with stage(nc) as (ctx, sem):
        sb = lambda n, s, d: ctx.enter_context(nc.sbuf_tensor(n, s, d))
        ps = lambda n: ctx.enter_context(nc.psum_tensor(n, [128, 512], F32))
        hT = sb("hT", [C0, 2, 4 * P], F32)
        scaled = sb("scaled", [P, T, C0], F32)
        parts = sb("hparts", [P, T, 3, C0], BF16)
        own = sb("own", [P, T, C0], F32)
        left = own
        summed = sb("summed", [P, 2, 2, C0], F32)
        w = sb("w_static", [C0, 3, C0], F32)
        bias = sb("b_static", [P, 3, C0], F32)
        dinv, rooted, tmp = sb("dinv_s", [P, T], F32), sb("rooted_s", [P, T], F32), sb("tmp_s", [P, T], F32)
        p_turn, p_mul = [ps(f"p_turn{b}") for b in range(2)], [ps(f"p_mul{b}") for b in range(2)]
        p_agg = [ps(f"p_agg{b}") for b in range(2)]
        loaded, deg_ready, root_done, dve_step = sem("loaded_s"), sem("deg_ready"), sem("root_done_s"), sem("dve_step_s")
        turned, turn_read, multiplied, mul_read = sem("turned_s"), sem("turn_read"), sem("multiplied"), sem("mul_read")
        parts_ready, aggregated, agg_read, h_ready = sem("parts_ready"), sem("aggregated"), sem("agg_read"), sem("h_ready")
        before_relu = sem("before_relu")
        NQ = len(QUADS)

        with nc.Block() as block:
            @block.sync
            def _(sp):
                sp.dma_start(g.h[:], g.xn.rearrange("(t p) d -> p t d", p=P)[:, :, 0:C0]).then_inc(loaded, 16)
                sp.dma_start(w[:], g.L0_gnn_W_static.rearrange("k i o -> i k o")).then_inc(loaded, 16)
                sp.dma_start(bias[:], g.L0_gnn_b_static[None, :, :].to_broadcast([P, 3, C0])).then_inc(loaded, 16)

            @block.scalar
            def _(act):
                root(nc, act, dinv[:], rooted[:], deg_ready, root_done)
                act.wait_ge(loaded, 48)
                for i in range(3):
                    for q, (t0, k) in enumerate(QUADS):
                        n = i * NQ + q
                        act.wait_ge(turned, n + 1)
                        if n >= 2:
                            act.wait_ge(multiplied, n - 1)
                        nc.scalar.copy(hT[:, n % 2, 0:k * P], p_turn[n % 2][0:C0, 0:k * P]).then_inc(turn_read, 1)

            @block.tensor
            def _(pe):
                pe.wait_ge(loaded, 48)
                for i in range(3):
                    if i > 0:
                        pe.wait_ge(h_ready, i * T)
                    def turn(q):
                        t0, k = QUADS[q]
                        n = i * NQ + q
                        if n >= 2:
                            pe.wait_ge(turn_read, n - 1)
                        for u in range(k):
                            mm = nc.tensor.transpose(p_turn[n % 2][0:C0, u * P:(u + 1) * P], g.h[:, t0 + u, :],
                                                     g.ident[0:P, 0:P])
                        mm.then_inc(turned, 1)

                    def multiply(q):
                        t0, k = QUADS[q]
                        n = i * NQ + q
                        pe.wait_ge(turn_read, n + 1)
                        if n >= 2:
                            pe.wait_ge(mul_read, n - 1)
                        for u in range(k):
                            mm = nc.tensor.matmul(p_mul[n % 2][0:P, u * C0:(u + 1) * C0], hT[:, n % 2, u * P:(u + 1) * P],
                                                  w[:, i, :], start=True, stop=True)
                        mm.then_inc(multiplied, 1)

                    turn(0)
                    for q in range(NQ):
                        if q + 1 < NQ:
                            turn(q + 1)
                        multiply(q)
                    pe.wait_ge(parts_ready, i + 1)

                    def aggregate(d, n, par, first=False):
                        if not first:
                            pe.wait_ge(agg_read, n)
                        for s in range(T):
                            mm = nc.tensor.matmul(p_agg[par][0:P, 0:3 * C0], g.counts[:, s, bass.ds(d * P, P)],
                                                  parts[:, s, :, :].rearrange("p k c -> p (k c)"),
                                                  start=(s == 0), stop=(s == T - 1))
                        mm.then_inc(aggregated, 1)

                    o = i % 2
                    aggregate(0, i * T, o, first=(i == 0))
                    with pe.Fori(0, T // 2) as m:
                        for b in (1, 2):
                            d = m * 2 + b
                            aggregate(d, d + i * T, (o + b) % 2)

            @block.vector
            def _(dve):
                step = Step(dve, dve_step)
                dve.sem_inc(agg_read)
                nc.vector.tensor_scalar(dinv[:], g.deg[:, :, 0], 1.0, 1e-12, ALU.add, ALU.max).then_inc(deg_ready, 1)
                inverse_root(nc, dve, step, dinv[:], rooted[:], tmp[:], root_done)
                dve.wait_ge(loaded, 48)
                for i in range(3):
                    for q, (t0, k) in enumerate(QUADS):
                        n = i * NQ + q
                        dve.wait_ge(multiplied, n + 1)
                        if i and q == 0:
                            dve.wait_ge(aggregated, i * T)
                        nc.vector.tensor_tensor(
                            scaled[:, t0:t0 + k, :], p_mul[n % 2][0:P, 0:k * C0].rearrange("p (u c) -> p u c", u=k),
                            dinv[:, t0:t0 + k, None].to_broadcast([P, k, C0]), ALU.mult).then_inc(mul_read, 1)
                    dve.wait_ge(mul_read, (i + 1) * NQ)
                    split3(nc, step, scaled[:], lambda k: parts[:, :, k, :], left[:])
                    dve.sem_inc(parts_ready)
                    step(nc.vector.tensor_tensor(own[:], scaled[:], dinv[:, :, None].to_broadcast([P, T, C0]), ALU.mult))
                    step(nc.vector.tensor_tensor(own[:], own[:], bias[:, i:i + 1, :].to_broadcast([P, T, C0]), ALU.add))

                    def update(d, n, par):
                        row = lambda a: a[:, bass.ds(d, 1), :].rearrange("p a c -> p (a c)")
                        dve.wait_ge(aggregated, n + 1)
                        nc.vector.tensor_reduce(summed[:, par, 0, :],
                                                p_agg[par][0:P, 0:3 * C0].rearrange("p (k c) -> p c k", k=3), AX.X,
                                                ALU.add).then_inc(agg_read, 1)
                        dve.wait_ge(agg_read, n + 2)
                        nc.vector.scalar_tensor_tensor(out=summed[:, par, 1, :], in0=summed[:, par, 0, :],
                                                       scalar=dinv[:, bass.ds(d, 1)], in1=row(own), op0=ALU.mult,
                                                       op1=ALU.add).then_inc(before_relu, 1)
                        dve.wait_ge(before_relu, n + 1)
                        nc.vector.tensor_scalar_max(row(g.h), summed[:, par, 1, :], 0.0).then_inc(h_ready, 1)

                    o = i % 2
                    update(0, i * T, o)
                    with dve.Fori(0, T // 2) as m:
                        for b in (1, 2):
                            d = m * 2 + b
                            update(d, d + i * T, (o + b) % 2)
                dve.wait_ge(h_ready, 3 * T)


def first_gnn_out(nc, g):
    with stage(nc) as (ctx, sem):
        sb = lambda n, s, d: ctx.enter_context(nc.sbuf_tensor(n, s, d))
        ps = lambda n: ctx.enter_context(nc.psum_tensor(n, [128, 512], F32))
        xn, xT = sb("xn_g", [P, T, D], F32), sb("xT_g", [128, F, N], F32)
        HID = 128
        hid = sb("hid_g", [HID, N], F32)
        x = g.xr
        w1, w2, wa = sb("w1_g", [128, F, HID], F32), sb("w2_g", [HID, C0], F32), sb("wa_g", [128, F, D], F32)
        b1, b2, ba = sb("b1_g", [HID, 1], F32), sb("b2_g", [P, C0], F32), sb("ba_g", [P, D], F32)
        factor = sb("factor_g", [P, T, C0], F32)
        psum = [ps(f"p_g{b}") for b in range(8)]
        loaded, x_in, w_in = sem("xn_in_g"), sem("x_in_g"), sem("w_in_g")
        turned, turn_read = sem("turned_g"), sem("turn_read_g")
        hid_done, hid_ready = sem("hid_done"), sem("hid_ready")
        ew_done, ew_read, dve_step = sem("ew_done"), sem("ew_read"), sem("dve_step_g")
        summed_ready, turned2, turn2_read = sem("summed_ready"), sem("turned2_g"), sem("turn2_read_g")
        out_done, out_read = sem("out_done_g"), sem("out_read_g")
        NQ = len(QUADS)
        PAIRS = [(t, min(2, T - t)) for t in range(0, T, 2)]

        with nc.Block() as block:
            @block.sync
            def _(sp):
                sp.dma_start(xn[:], g.xn.rearrange("(t p) d -> p t d", p=P)).then_inc(loaded, 16)
                sp.dma_start(w1[:], g.L0_gnn_W1.rearrange("(f i) o -> i f o", i=128)).then_inc(w_in, 16)
                sp.dma_start(b1[:], g.L0_gnn_b1[:, None]).then_inc(w_in, 16)
                sp.dma_start(w2[:], g.L0_gnn_W2).then_inc(w_in, 16)
                sp.dma_start(b2[:], g.L0_gnn_b2[None, :].to_broadcast([P, C0])).then_inc(w_in, 16)
                sp.dma_start(wa[:], g.L0_gnn_W_aggr.rearrange("(f i) o -> i f o", i=128)).then_inc(w_in, 16)
                sp.dma_start(ba[:], g.L0_gnn_b_aggr[None, :].to_broadcast([P, D])).then_inc(w_in, 16)
                sp.dma_start(x[:], g.x.rearrange("(t p) d -> p t d", p=P)).then_inc(x_in, 16)

            @block.tensor
            def _(pe):
                pe.wait_ge(loaded, 16)
                turn_tiles(nc, pe, xn, D, psum[0:4], g.ident, turn_read, turned)
                pe.wait_ge(w_in, 96)
                for q, (t0, k) in enumerate(QUADS):
                    cols = slice(t0 * P, (t0 + k) * P)
                    pe.wait_ge(turn_read, 2 * q + 2)
                    if q >= 2:
                        pe.wait_ge(hid_ready, q - 1)
                    for f in range(F):
                        mm = nc.tensor.matmul(psum[4 + q % 2][0:HID, 0:k * P], w1[:, f, :], xT[:, f, cols],
                                              start=(f == 0), stop=(f == F - 1))
                    mm.then_inc(hid_done, 1)
                for q, (t0, k) in enumerate(QUADS):
                    pe.wait_ge(hid_ready, q + 1)
                    if q >= 2:
                        pe.wait_ge(ew_read, q - 1)
                    for u in range(k):
                        mm = nc.tensor.matmul(psum[6 + q % 2][0:P, u * C0:(u + 1) * C0],
                                              hid[:, (t0 + u) * P:(t0 + u + 1) * P], w2[:], start=True, stop=True)
                    mm.then_inc(ew_done, 1)
                pe.wait_ge(summed_ready, 1)
                turn_tiles(nc, pe, g.h, C0, psum[0:2], g.ident, turn2_read, turned2)
                pe.wait_ge(turn2_read, NQ)
                for n, (t0, k) in enumerate(PAIRS):
                    if n >= 4:
                        pe.wait_ge(out_read, n - 3)
                    for u in range(k):
                        for f in range(F):
                            mm = nc.tensor.matmul(psum[2 + n % 4][0:P, u * D:(u + 1) * D],
                                                  xT[:, f, (t0 + u) * P:(t0 + u + 1) * P], wa[:, f, :],
                                                  start=(f == 0), stop=(f == F - 1))
                    mm.then_inc(out_done, 1)

            @block.scalar
            def _(act):
                n = 0
                for t0, k in QUADS:
                    for f in range(F):
                        act.wait_ge(turned, n + 1)
                        nc.scalar.copy(xT[:, f, t0 * P:(t0 + k) * P], psum[n % 4][:, 0:k * P]).then_inc(turn_read, 1)
                        n += 1
                act.wait_ge(w_in, 96)
                for q, (t0, k) in enumerate(QUADS):
                    act.wait_ge(hid_done, q + 1)
                    nc.scalar.activation(hid[:, t0 * P:(t0 + k) * P], psum[4 + q % 2][0:HID, 0:k * P], ACT.Gelu,
                                         bias=b1[:, 0:1]).then_inc(hid_ready, 1)
                for q, (t0, k) in enumerate(QUADS):
                    act.wait_ge(turned2, q + 1)
                    nc.scalar.copy(xT[0:C0, 0, t0 * P:(t0 + k) * P], psum[q % 2][0:C0, 0:k * P]).then_inc(turn2_read, 1)

            @block.vector
            def _(dve):
                step = Step(dve, dve_step)
                dve.wait_ge(w_in, 96)
                for q, (t0, k) in enumerate(QUADS):
                    dve.wait_ge(ew_done, q + 1)
                    nc.vector.tensor_tensor(factor[:, t0:t0 + k, :],
                                            psum[6 + q % 2][0:P, 0:k * C0].rearrange("p (u c) -> p u c", u=k),
                                            b2[:, None, :].to_broadcast([P, k, C0]), ALU.add).then_inc(ew_read, 1)
                dve.wait_ge(ew_read, NQ)
                step(nc.vector.tensor_tensor(factor[:], factor[:], g.dyn[:], ALU.mult))
                nc.vector.tensor_tensor(g.h[:], g.h[:], factor[:], ALU.add).then_inc(summed_ready, 1)
                dve.wait_ge(x_in, 16)
                step(nc.vector.tensor_tensor(x[:], x[:], ba[:, None, :].to_broadcast([P, T, D]), ALU.add))
                for n, (t0, k) in enumerate(PAIRS):
                    dve.wait_ge(out_done, n + 1)
                    nc.vector.tensor_tensor(x[:, t0:t0 + k, :],
                                            psum[2 + n % 4][0:P, 0:k * D].rearrange("p (u c) -> p u c", u=k),
                                            x[:, t0:t0 + k, :], ALU.add).then_inc(out_read, 1)

NE = 8
CAP = -(-5 * N // (4 * NE))
CT = -(-CAP // P)
CP = CT * P
F1 = 1024
LARGEST = 1e4


def route_first(nc, g):
    with stage(nc) as (ctx, sem):
        sb = lambda n, s, d: ctx.enter_context(nc.sbuf_tensor(n, s, d))
        ps = lambda n: ctx.enter_context(nc.psum_tensor(n, [128, 512], F32))
        xn, xT = sb("xn_r", [P, T, D], F32), sb("xT_r", [128, F, N], F32)
        stats, small = sb("stats_r", [P, T, 6], F32), sb("small_r", [P, 4, T], F32)
        zero = sb("zero_r", [P, 1, D], F32)
        gate, gate_b = sb("gate_r", [128, F, NE], F32), sb("gate_b_r", [P, NE], F32)
        tri = sb("tri_r", [P, P], F32)
        number, rev = sb("number_r", [P, NE], F32), sb("rev_r", [P, NE], F32)
        logits, a, b = sb("logits_r", [P, T, NE], F32), sb("a_r", [P, T, NE], F32), sb("b_r", [P, T, NE], F32)
        hot, totals = sb("hot_r", [P, T, NE], F32), sb("totals_r", [P, 2, T, NE], F32)
        top, total, place, kept = (sb(f"{k}_r", [P, T], F32) for k in ("top", "total", "place", "kept"))
        where = sb("where_r", [P, T], F32)
        scatter_at = sb("scatter_at_r", [P, T], U32)
        psum = [ps(f"p_r{k}") for k in range(4)]
        p_gate, p_count, p_total = ps("p_gate"), ps("p_count"), ps("p_total")
        cleared, clear_out, w_in = sem("cleared_r"), sem("clear_out_r"), sem("w_in_r")
        rows_done, var_ready, root_done = sem("rows_done_r"), sem("var_ready_r"), sem("root_done_r")
        xn_ready, dve_step = sem("xn_ready_r"), sem("dve_step_r")
        turned, turn_read, gated = sem("turned_r"), sem("turn_read_r"), sem("gated_r")
        exp_asked, exp_done, hot_ready, counted = sem("exp_asked"), sem("exp_done"), sem("hot_ready_r"), sem("counted_r")
        places_ready, consts, scattered = sem("places_ready"), sem("consts_r"), sem("scattered_r")

        with nc.Block() as block:
            @block.sync
            def _(sp):
                sp.dma_start(gate[:], g.L0_ffn_gate_w.rearrange("(f i) e -> i f e", i=128)).then_inc(w_in, 16)
                sp.dma_start(gate_b[:], g.L0_ffn_gate_b[None, :].to_broadcast([P, NE])).then_inc(w_in, 16)
                sp.wait_ge(cleared, 1)
                sp.dma_start(g.placed.rearrange("(p n) d -> p n d", p=P),
                             zero[:].to_broadcast([P, NE * CP // P, D])).then_inc(clear_out, 16)

            @block.gpsimd
            def _(pool):
                pool.memset(zero[:], 0.0).then_inc(cleared, 1)
                pool.iota(number[:], pattern=[[1, NE]], base=0, channel_multiplier=0,
                          allow_small_or_imprecise_dtypes=True).then_inc(consts, 1)
                pool.iota(rev[:], pattern=[[-1, NE]], base=NE, channel_multiplier=0,
                          allow_small_or_imprecise_dtypes=True).then_inc(consts, 1)
                pool.affine_select(out=tri[:], in_=g.ones[0:P, 0:P], compare_op=ALU.is_gt, fill=0.0, base=0,
                                   pattern=[[1, P]], channel_multiplier=-1).then_inc(consts, 1)
                bound = pool.to_reg(NE * CP - 1)
                pool.wait_ge(clear_out, 16)
                pool.wait_ge(places_ready, 1)
                for t in range(T):
                    pool.indirect_dma_start(
                        out=g.placed, out_offset=bass.IndirectOffsetOnAxis(ap=scatter_at[:, t:t + 1], axis=0),
                        in_=xn[:, t, :], in_offset=None, bounds_check=bound, oob_is_err=False).then_inc(scattered, 16)
                pool.wait_ge(scattered, 16 * T)

            @block.scalar
            def _(act):
                root(nc, act, small[:, 1, :], small[:, 3, :], var_ready, root_done)
                n = 0
                for t0, k in QUADS:
                    for f in range(F):
                        act.wait_ge(turned, n + 1)
                        nc.scalar.copy(xT[:, f, t0 * P:(t0 + k) * P], psum[n % 4][:, 0:k * P]).then_inc(turn_read, 1)
                        n += 1
                act.wait_ge(exp_asked, 1)
                nc.scalar.activation(b[:], a[:], ACT.Exp).then_inc(exp_done, 1)

            @block.tensor
            def _(pe):
                pe.wait_ge(xn_ready, 1)
                turn_tiles(nc, pe, xn, D, psum, g.ident, turn_read, turned)
                pe.wait_ge(w_in, 32)
                pe.wait_ge(turn_read, F * len(QUADS))
                for t in range(T):
                    for f in range(F):
                        mm = nc.tensor.matmul(p_gate[0:P, t * NE:(t + 1) * NE], xT[:, f, t * P:(t + 1) * P],
                                              gate[:, f, :], start=(f == 0), stop=(f == F - 1))
                mm.then_inc(gated, 1)
                pe.wait_ge(hot_ready, 1)
                pe.wait_ge(consts, 3)
                flat = hot[:].rearrange("p t e -> p (t e)")
                nc.tensor.matmul(p_total[0:P, 0:T * NE], g.ones[0:P, 0:P], flat, start=True, stop=True).then_inc(counted, 1)
                nc.tensor.matmul(p_count[0:P, 0:T * NE], tri[:], flat, start=True, stop=True).then_inc(counted, 1)

            @block.vector
            def _(dve):
                step = Step(dve, dve_step)
                bc = lambda v: v[:, :, None].to_broadcast([P, T, NE])
                layer_norm(nc, dve, step, g.xr, xn, stats, small, rows_done, var_ready, root_done)
                dve.sem_inc(xn_ready)
                dve.wait_ge(gated, 1)
                dve.wait_ge(w_in, 32)
                dve.wait_ge(consts, 3)
                V = nc.vector
                step(V.tensor_tensor(logits[:], p_gate[0:P, 0:T * NE].rearrange("p (t e) -> p t e", e=NE),
                                     gate_b[:, None, :].to_broadcast([P, T, NE]), ALU.add))
                step(V.tensor_reduce(top[:], logits[:], AX.X, ALU.max))
                V.tensor_tensor(a[:], logits[:], bc(top), ALU.subtract).then_inc(exp_asked, 1)
                step(V.tensor_tensor(hot[:], logits[:], bc(top), ALU.is_equal))
                step(V.tensor_tensor(hot[:], hot[:], rev[:, None, :].to_broadcast([P, T, NE]), ALU.mult))
                step(V.tensor_reduce(top[:], hot[:], AX.X, ALU.max))
                step(V.tensor_tensor(hot[:], hot[:], bc(top), ALU.is_equal))
                dve.sem_inc(hot_ready)
                dve.wait_ge(exp_done, 1)
                step(V.tensor_reduce(total[:], b[:], AX.X, ALU.add))
                step(V.reciprocal(g.chance[:], total[:]))
                step(V.tensor_scalar(top[:], top[:], -float(CP), float(NE * CP), ALU.mult, ALU.add))
                dve.wait_ge(counted, 2)
                step(V.tensor_copy(totals[:, 0], p_total[0:P, 0:T * NE].rearrange("p (t e) -> p t e", e=NE)))
                now, hop = 0, 1
                while hop < T:
                    step(V.tensor_copy(totals[:, 1 - now, 0:hop, :], totals[:, now, 0:hop, :]))
                    step(V.tensor_tensor(totals[:, 1 - now, hop:T, :], totals[:, now, hop:T, :],
                                         totals[:, now, 0:T - hop, :], ALU.add))
                    now, hop = 1 - now, hop * 2
                step(V.tensor_tensor(a[:], totals[:, now], p_total[0:P, 0:T * NE].rearrange("p (t e) -> p t e", e=NE),
                                     ALU.subtract))
                step(V.tensor_tensor(a[:], a[:], p_count[0:P, 0:T * NE].rearrange("p (t e) -> p t e", e=NE), ALU.add))
                step(V.tensor_tensor(a[:], a[:], hot[:], ALU.mult))
                step(V.tensor_reduce(place[:], a[:], AX.X, ALU.add))
                step(V.tensor_scalar(kept[:], place[:], float(CAP), None, ALU.is_lt))
                step(V.tensor_tensor(g.chance[:], g.chance[:], kept[:], ALU.mult))
                step(V.tensor_scalar(kept[:], kept[:], -PAST, PAST, ALU.mult, ALU.add))
                step(V.tensor_tensor(where[:], top[:], place[:], ALU.add))
                step(V.tensor_tensor(scatter_at[:], where[:], kept[:], ALU.add))
                step(V.tensor_scalar_min(place[:], place[:], float(CAP - 1)))
                step(V.tensor_tensor(g.gather_at[:], top[:], place[:], ALU.add))
                dve.sem_inc(places_ready)


def first_experts(nc, g):
    M1 = F1 // 128
    with stage(nc) as (ctx, sem):
        sb = lambda n, s, d: ctx.enter_context(nc.sbuf_tensor(n, s, d))
        ps = lambda n: ctx.enter_context(nc.psum_tensor(n, [128, 512], F32))
        rows = sb("rows_f", [P, 2, CT, D], F32)
        xT = sb("xT_f", [128, 2, F, CP], F32)
        w1, w2 = sb("w1_f", [128, 2, F, F1], F32), sb("w2_f", [128, 2, M1, D], F32)
        b1, b2 = sb("b1_f", [128, NE, M1], F32), sb("b2_f", [P, NE, D], F32)
        b1_rows = sb("b1_rows_f", [NE * M1, 128], F32)
        hid = sb("hid_f", [128, 2, M1, CP], F32)
        y = sb("y_f", [P, 2, CT, D], F32)
        p_turn = [ps(f"p_turn_f{k}") for k in range(2)]
        p_hid = [ps(f"p_hid_f{k}") for k in range(3)]
        p_out = [ps(f"p_out_f{k}") for k in range(2)]
        biases, rows_in = sem("biases_f"), [sem(f"rows_in_f{k}") for k in range(2)]
        w_in, y_out = [sem(f"w_in_f{k}") for k in range(2)], [sem(f"y_out_f{k}") for k in range(2)]
        turned, turn_read = sem("turned_f"), sem("turn_read_f")
        b1_turned, b1_ready = sem("b1_turned_f"), sem("b1_ready_f")
        hid_done, hid_ready = sem("hid_done_f"), sem("hid_ready_f")
        out_done, out_read = sem("out_done_f"), sem("out_read_f")

        with nc.Block() as block:
            @block.sync
            def _(sp):
                sp.dma_start(b1_rows[:], g.L0_ffn_b1.rearrange("e (m i) -> (e m) i", i=128)).then_inc(biases, 16)
                sp.dma_start(b2[:], g.L0_ffn_b2[None, :, :].to_broadcast([P, NE, D])).then_inc(biases, 16)
                for e in range(NE):
                    k = e % 2
                    if e >= 2:
                        sp.wait_ge(hid_done, (e - 1) * M1)
                    sp.dma_start(rows[:, k], g.placed[e * CP:(e + 1) * CP, :].rearrange("(u p) d -> p u d", p=P)
                                 ).then_inc(rows_in[k], 16)
                    sp.dma_start(w1[:, k], g.L0_ffn_w1[e].rearrange("(f i) o -> i f o", i=128)).then_inc(w_in[k], 16)
                    if e >= 2:
                        sp.wait_ge(out_done, (e - 1) * CT)
                    sp.dma_start(w2[:, k], g.L0_ffn_w2[e].rearrange("(m i) o -> i m o", i=128)).then_inc(w_in[k], 16)

            @block.gpsimd
            def _(pool):
                for e in range(NE):
                    pool.wait_ge(out_read, (e + 1) * CT)
                    pool.dma_start(g.results[e * CP:(e + 1) * CP, :].rearrange("(u p) d -> p u d", p=P),
                                   y[:, e % 2]).then_inc(y_out[e % 2], 16)
                for k in range(2):
                    pool.wait_ge(y_out[k], 16 * NE // 2)

            @block.tensor
            def _(pe):
                def turn(e):
                    k = e % 2
                    pe.wait_ge(rows_in[k], 16 * (e // 2 + 1))
                    for f in range(F):
                        n = e * F + f
                        if n >= 2:
                            pe.wait_ge(turn_read, n - 1)
                        for u in range(CT):
                            mm = nc.tensor.transpose(p_turn[f][:, u * P:(u + 1) * P],
                                                     rows[:, k, u, f * 128:(f + 1) * 128], g.ident[0:P, 0:P])
                        mm.then_inc(turned, 1)

                pe.wait_ge(biases, 32)
                nc.tensor.transpose(p_hid[0][:, 0:NE * M1], b1_rows[:], g.ident[0:NE * M1, 0:NE * M1]).then_inc(b1_turned, 1)
                turn(0)
                pe.wait_ge(b1_ready, 1)
                for e in range(NE):
                    k = e % 2
                    pe.wait_ge(turn_read, (e + 1) * F)
                    pe.wait_ge(w_in[k], 32 * (e // 2 + 1))
                    for m in range(M1):
                        n = e * M1 + m
                        if n >= 3:
                            pe.wait_ge(hid_ready, n - 2)
                        for f in range(F):
                            mm = nc.tensor.matmul(p_hid[n % 3][:, 0:CP], w1[:, k, f, m * 128:(m + 1) * 128],
                                                  xT[:, k, f, :], start=(f == 0), stop=(f == F - 1))
                        mm.then_inc(hid_done, 1)
                    if e + 1 < NE:
                        turn(e + 1)
                    pe.wait_ge(hid_ready, (e + 1) * M1)
                    for u in range(CT):
                        n = e * CT + u
                        if n >= 2:
                            pe.wait_ge(out_read, n - 1)
                        for m in range(M1):
                            mm = nc.tensor.matmul(p_out[n % 2][0:P, 0:D], hid[:, k, m, u * P:(u + 1) * P],
                                                  w2[:, k, m, :], start=(m == 0), stop=(m == M1 - 1))
                        mm.then_inc(out_done, 1)

            @block.scalar
            def _(act):
                act.wait_ge(b1_turned, 1)
                nc.scalar.copy(b1[:].rearrange("p e m -> p (e m)"), p_hid[0][:, 0:NE * M1]).then_inc(b1_ready, 1)
                act.wait_ge(b1_ready, 1)
                for e in range(NE):
                    k = e % 2
                    if e >= 2:
                        act.wait_ge(out_done, (e - 1) * CT)
                    for m in range(M1):
                        n = e * M1 + m
                        act.wait_ge(hid_done, n + 1)
                        nc.scalar.activation(hid[:, k, m, :], p_hid[n % 3][:, 0:CP], ACT.Relu,
                                             bias=b1[:, e, m:m + 1]).then_inc(hid_ready, 1)

            @block.vector
            def _(dve):
                dve.wait_ge(biases, 32)

                def take_turned(e):
                    k = e % 2
                    if e >= 2:
                        dve.wait_ge(hid_done, (e - 1) * M1)
                    for f in range(F):
                        dve.wait_ge(turned, e * F + f + 1)
                        nc.vector.tensor_copy(xT[:, k, f, :], p_turn[f][:, 0:CP]).then_inc(turn_read, 1)

                take_turned(0)
                for e in range(NE):
                    k = e % 2
                    if e + 1 < NE:
                        take_turned(e + 1)
                    if e >= 2:
                        dve.wait_ge(y_out[k], 16 * (e // 2))
                    for u in range(CT):
                        dve.wait_ge(out_done, e * CT + u + 1)
                        nc.vector.tensor_tensor(y[:, k, u, :], p_out[(e * CT + u) % 2][0:P, 0:D], b2[:, e, :],
                                                ALU.add).then_inc(out_read, 1)


def combine_first(nc, g):
    with stage(nc) as (ctx, sem):
        sb = lambda n, s, d: ctx.enter_context(nc.sbuf_tensor(n, s, d))
        y = sb("y_c", [P, T, D], F32)
        z = sb("z_c", [P, T, D], F32)
        high, low = sb("high_c", [P, D], F32), sb("low_c", [P, D], F32)
        mask = sb("mask_c", [P, 2, 3, D], U32)
        gathered = [sem(f"gathered{k}") for k in range(5)]
        consts, scaled, masked, kept, added = sem("consts_c"), sem("scaled_c"), sem("masked_c"), sem("kept_c"), sem("added_c")

        with nc.Block() as block:
            @block.gpsimd
            def _(pool):
                pool.memset(high[:], LARGEST)
                pool.memset(low[:], -LARGEST)
                pool.memset(z[:], 0.0).then_inc(consts, 1)
                for t in range(T):
                    if t >= 5:
                        pool.wait_ge(gathered[t % 5], 16 * (t // 5))
                    pool.indirect_dma_start(
                        out=y[:, t, :], out_offset=None, in_=g.results,
                        in_offset=bass.IndirectOffsetOnAxis(ap=g.gather_at[:, t:t + 1], axis=0)
                    ).then_inc(gathered[t % 5], 16)

            @block.scalar
            def _(act):
                for t in range(T):
                    act.wait_ge(gathered[t % 5], 16 * (t // 5 + 1))
                    nc.scalar.activation(y[:, t, :], y[:, t, :], ACT.Copy, scale=g.chance[:, t:t + 1]).then_inc(scaled, 1)

            @block.vector
            def _(dve):
                V = nc.vector
                INF = float("inf")
                dve.wait_ge(consts, 1)
                for t in range(T):
                    k = t % 2
                    dve.wait_ge(scaled, t + 1)
                    if t >= 2:
                        dve.wait_ge(kept, 3 * (t - 1))
                    V.tensor_tensor(mask[:, k, 0, :], y[:, t, :], y[:, t, :], ALU.is_equal)
                    V.tensor_scalar(mask[:, k, 1, :], y[:, t, :], LIMIT, None, ALU.is_gt)
                    V.tensor_scalar(mask[:, k, 2, :], y[:, t, :], -LIMIT, None, ALU.is_lt).then_inc(masked, 1)
                    dve.wait_ge(masked, t + 1)
                    V.copy_predicated(z[:, t, :], mask[:, k, 0, :], y[:, t, :]).then_inc(kept, 1)
                    dve.wait_ge(kept, 3 * t + 1)
                    V.copy_predicated(z[:, t, :], mask[:, k, 1, :], high[:]).then_inc(kept, 1)
                    dve.wait_ge(kept, 3 * t + 2)
                    V.copy_predicated(z[:, t, :], mask[:, k, 2, :], low[:]).then_inc(kept, 1)
                    dve.wait_ge(kept, 3 * t + 3)
                    V.tensor_tensor(g.xr[:, t, :], g.xr[:, t, :], z[:, t, :], ALU.add).then_inc(added, 1)
                dve.wait_ge(added, T)


LIMIT = 3.4028234663852886e38

WINDOWS = [(0, [(0, 4), (4, 4), (8, 4), (12, 4)]), (16, [(16, 4), (20, 4), (24, 1)])]
PAIRS = [(t, min(2, T - t)) for t in range(0, T, 2)]


def second_gnn(nc, g):
    RING = 5
    with stage(nc) as (ctx, sem):
        sb = lambda n, s, d: ctx.enter_context(nc.sbuf_tensor(n, s, d))
        msg = sb("msg_w", [P, T, D], F32)
        xT, outT = sb("xT_w", [128, F, N], F32), sb("outT_w", [128, F, N], F32)
        strips = sb("strips_w", [P, RING, 16 * P], F32)
        msg_now = sb("msg_now", [P, RING, D], F32)
        dinv_row = sb("dinv_row", [128, N], F32)
        stats, small = sb("stats_w", [P, T, 6], F32), sb("small_w", [P, 4, T], F32)
        dinv, rooted, tmp, mask = (sb(f"{k}_w", [P, T], F32) for k in ("dinv", "rooted", "tmp", "mask"))
        dinv_t = sb("dinv_t", [T, P], F32)
        w = [sb(f"w{i}_w", [128, F, D], F32) for i in range(2)]
        cols = sb("cols_w", [128, 4, F], F32)
        bn = sb("bn_w", [128, F, 7, 6], F32)
        agg = sb("agg_w", [128, F, 2], F32)
        norm = sb("norm_w", [128, 4, F], F32)
        bank = [ctx.enter_context(nc.psum_tensor(f"bank_w{k}", [128, 512], F32)) for k in range(8)]

        w_in, rows_done, var_ready, root_done = sem("w_in_w"), sem("rows_done_w"), sem("var_ready_w"), sem("root_done_w")
        dve_step, xn_ready, turned, turn_read = sem("dve_step_w"), sem("xn_ready_w"), sem("turned_w"), sem("turn_read_w")
        deg_ready, deg_rooted = sem("deg_ready_w"), sem("deg_rooted_w")
        dinv_ready, dinv_turned, dinv_read, dinv_out, row_in = (
            sem(k) for k in ("dinv_ready", "dinv_turned", "dinv_read", "dinv_out", "row_in"))
        multiplied, msg_ready = sem("multiplied_w"), sem("msg_ready")
        strip_in = [sem(f"strip_in{k}") for k in range(RING)]
        now_ready = sem("now_ready")
        strip_used, scaled, out_ready = sem("strip_used"), sem("scaled_w"), sem("out_ready_w")
        bn_ready, bn_rooted, norm_ready = sem("bn_ready"), sem("bn_rooted"), sem("norm_ready")
        mixed, final_ready, back, added = sem("mixed"), sem("final_ready"), sem("back"), sem("added_w")
        NQ, NP, NCH = len(QUADS), len(PAIRS), 7
        BIG = 2 * NCH

        with nc.Block() as block:
            @block.sync
            def _(sp):
                for i, name in enumerate((g.L1_gnn_W1, g.L1_gnn_W2)):
                    sp.dma_start(w[i][:], name.rearrange("(f i) o -> i f o", i=128)).then_inc(w_in, 16)
                for i, name in enumerate((g.L1_gnn_b1, g.L1_gnn_b2, g.L1_gnn_gamma, g.L1_gnn_beta)):
                    for f in range(F):
                        sp.dma_start(cols[:, i, f:f + 1], name[f * 128:(f + 1) * 128, None]).then_inc(w_in, 16)
                sp.wait_ge(dinv_read, 1)
                sp.dma_start(g.dinv.rearrange("(t p) -> t p", p=P), dinv_t[:]).then_inc(dinv_out, 16)
                sp.wait_ge(dinv_out, 16)
                sp.dma_start(dinv_row[:], g.dinv[None, :].to_broadcast([128, N])).then_inc(row_in, 16)
                for i in range(2):
                    for v, (first, chunks) in enumerate(WINDOWS):
                        lo, width = first * P, sum(k for _, k in chunks) * P
                        trip = (i * 2 + v) * (T // RING)

                        def load(m, fresh):
                            for r in range(RING):
                                s = m * RING + r
                                if not fresh:
                                    sp.wait_ge(strip_used, (m + trip - 1) * RING + r + 1)
                                sp.dma_start(strips[:, r, 0:width], g.weights[bass.ds(s * P, P), lo:lo + width]
                                             ).then_inc(strip_in[r], 16)

                        load(0, i == 0 and v == 0)
                        with sp.Fori(1, T // RING) as m:
                            load(m, False)

            @block.scalar
            def _(act):
                root(nc, act, dinv[:], rooted[:], deg_ready, deg_rooted)
                root(nc, act, small[:, 1, :], small[:, 3, :], var_ready, root_done)
                n = 0
                for t0, k in QUADS:
                    for f in range(F):
                        act.wait_ge(turned, n + 1)
                        nc.scalar.copy(xT[:, f, t0 * P:(t0 + k) * P], bank[n % 4][:, 0:k * P]).then_inc(turn_read, 1)
                        n += 1
                act.wait_ge(w_in, 160)
                for i, func in enumerate((ACT.Relu, ACT.Identity)):
                    n = 0
                    act.wait_ge(msg_ready, (i + 1) * NP)
                    for v, (_, chunks) in enumerate(WINDOWS):
                        trip = (i * 2 + v) * (T // RING)

                        def take(m, fresh):
                            for r in range(RING):
                                if not fresh:
                                    act.wait_ge(strip_used, (m + trip - 1) * RING + r + 1)
                                nc.scalar.copy(msg_now[:, r, :], msg[:, bass.ds(m * RING + r, 1), :].rearrange(
                                    "p a c -> p (a c)")).then_inc(now_ready, 1)

                        take(0, i == 0 and v == 0)
                        with act.Fori(1, T // RING) as m:
                            take(m, False)
                        for t0, k in chunks:
                            for f in range(F):
                                act.wait_ge(scaled, i * BIG + n + 1)
                                o = outT[:, f, t0 * P:(t0 + k) * P]
                                nc.scalar.activation(o, o, func, bias=cols[:, i, f:f + 1]).then_inc(out_ready, 1)
                                n += 1
                root(nc, act, norm[:, 0, :], norm[:, 1, :], bn_ready, bn_rooted)
                act.wait_ge(norm_ready, 1)
                n = 0
                for t0, k in QUADS:
                    for f in range(F):
                        act.wait_ge(mixed, n + 1)
                        o = outT[:, f, t0 * P:(t0 + k) * P]
                        nc.scalar.activation(o, o, ACT.Relu, bias=norm[:, 3, f:f + 1]).then_inc(final_ready, 1)
                        n += 1

            @block.tensor
            def _(pe):
                pe.wait_ge(dinv_ready, 1)
                nc.tensor.transpose(bank[7][0:T, 0:P], dinv[:], g.ident[0:P, 0:P]).then_inc(dinv_turned, 1)
                pe.wait_ge(xn_ready, 1)
                turn_tiles(nc, pe, msg, D, bank[0:4], g.ident, turn_read, turned)
                pe.wait_ge(w_in, 160)
                pe.wait_ge(turn_read, F * NQ)
                pe.wait_ge(dinv_read, 1)
                for i in range(2):
                    rows = xT if i == 0 else outT
                    for n, (t0, k) in enumerate(PAIRS):
                        if i and n == 0:
                            pe.wait_ge(out_ready, BIG)
                        if n >= 8:
                            pe.wait_ge(msg_ready, i * NP + n - 7)
                        for u in range(k):
                            for f in range(F):
                                mm = nc.tensor.matmul(bank[n % 8][0:P, u * D:(u + 1) * D],
                                                      rows[:, f, (t0 + u) * P:(t0 + u + 1) * P], w[i][:, f, :],
                                                      start=(f == 0), stop=(f == F - 1))
                        mm.then_inc(multiplied, 1)
                    pe.wait_ge(msg_ready, (i + 1) * NP)
                    before = 0
                    for v, (first, chunks) in enumerate(WINDOWS):
                        if v:
                            pe.wait_ge(scaled, i * BIG + before)
                        for c, (t0, k) in enumerate(chunks):
                            for f in range(F):
                                for u in range(k):
                                    nc.tensor.matmul(bank[2 * c + f][:, u * P:(u + 1) * P],
                                                     msg[:, t0 + u, f * 128:(f + 1) * 128], g.ident[0:P, 0:P],
                                                     start=(u == 0), stop=False, skip_group_check=True)

                        trip = (i * 2 + v) * (T // RING)
                        with pe.Fori(0, T // RING) as m:
                            for r in range(RING):
                                pe.wait_ge(strip_in[r], (m + trip + 1) * 16)
                                pe.wait_ge(now_ready, (m + trip) * RING + r + 1)
                                for f in range(F):
                                    for c, (t0, k) in enumerate(chunks):
                                        mm = nc.tensor.matmul(
                                            bank[2 * c + f][:, 0:k * P],
                                            msg_now[:, r, f * 128:(f + 1) * 128],
                                            strips[:, r, (t0 - first) * P:(t0 - first + k) * P], start=False,
                                            stop=True, skip_group_check=True)
                                mm.then_inc(strip_used, 1)
                        before += 2 * len(chunks)
                for n, (t0, k) in enumerate(PAIRS):
                    if n == 0:
                        pe.wait_ge(scaled, 2 * BIG)
                    pe.wait_ge(final_ready, F * ((t0 + k - 1) // 4 + 1))
                    if n >= 8:
                        pe.wait_ge(added, n - 7)
                    for u in range(k):
                        for f in range(F):
                            mm = nc.tensor.transpose(bank[n % 8][0:P, u * D + f * 128:u * D + (f + 1) * 128],
                                                     outT[:, f, (t0 + u) * P:(t0 + u + 1) * P], g.ident[:, :])
                    mm.then_inc(back, 1)

            @block.vector
            def _(dve):
                step = Step(dve, dve_step)
                V = nc.vector
                step(V.tensor_reduce(dinv[:], g.deg[:, :, 1:4], AX.X, ALU.add))
                step(V.tensor_scalar_add(dinv[:], dinv[:], 1.0))
                step(V.tensor_scalar(mask[:], dinv[:], 0.0, None, ALU.is_gt))
                V.tensor_scalar_max(dinv[:], dinv[:], 1e-30).then_inc(deg_ready, 1)
                inverse_root(nc, dve, step, dinv[:], rooted[:], tmp[:], deg_rooted)
                V.tensor_tensor(dinv[:], dinv[:], mask[:], ALU.mult).then_inc(dinv_ready, 1)
                dve.wait_ge(dinv_turned, 1)
                V.tensor_copy(dinv_t[:], bank[7][0:T, 0:P]).then_inc(dinv_read, 1)
                layer_norm(nc, dve, step, g.xr, msg, stats, small, rows_done, var_ready, root_done)
                dve.sem_inc(xn_ready)
                dve.wait_ge(w_in, 160)
                dve.wait_ge(turned, F * NQ)
                for i in range(2):
                    if i:
                        dve.wait_ge(strip_used, 2 * T)
                    for n, (t0, k) in enumerate(PAIRS):
                        dve.wait_ge(multiplied, i * NP + n + 1)
                        V.tensor_tensor(msg[:, t0:t0 + k, :],
                                        bank[n % 8][0:P, 0:k * D].rearrange("p (u c) -> p u c", u=k),
                                        dinv[:, t0:t0 + k, None].to_broadcast([P, k, D]), ALU.mult).then_inc(msg_ready, 1)
                    if i == 0:
                        dve.wait_ge(row_in, 16)
                    for v, (first, chunks) in enumerate(WINDOWS):
                        dve.wait_ge(strip_used, (i * 2 + v + 1) * T)
                        for c, (t0, k) in enumerate(chunks):
                            for f in range(F):
                                at = slice(t0 * P, (t0 + k) * P)
                                V.tensor_tensor(outT[:, f, at], bank[2 * c + f][:, 0:k * P], dinv_row[:, at],
                                                ALU.mult).then_inc(scaled, 1)
                dve.wait_ge(out_ready, 2 * BIG)
                for f in range(F):
                    for q, (t0, k) in enumerate(QUADS):
                        ins = V.bn_stats(bn[:, f, q, :], outT[:, f, t0 * P:(t0 + k) * P])
                step(ins)
                for f in range(F):
                    step(V.bn_aggr(agg[:, f, :], bn[:, f, :, :].rearrange("p q k -> p (q k)")))
                V.tensor_scalar_add(norm[:, 0, :], agg[:, :, 1], EPS).then_inc(bn_ready, 1)
                inverse_root(nc, dve, step, norm[:, 0, :], norm[:, 1, :], norm[:, 2, :], bn_rooted)
                step(V.tensor_tensor(norm[:, 0, :], norm[:, 0, :], cols[:, 2, :], ALU.mult))
                step(V.tensor_tensor(norm[:, 2, :], norm[:, 0, :], agg[:, :, 0], ALU.mult))
                step(V.tensor_tensor(norm[:, 3, :], cols[:, 3, :], norm[:, 2, :], ALU.subtract))
                dve.sem_inc(norm_ready)
                for t0, k in QUADS:
                    for f in range(F):
                        at = slice(t0 * P, (t0 + k) * P)
                        V.scalar_tensor_tensor(out=outT[:, f, at], in0=outT[:, f, at], scalar=norm[:, 0, f:f + 1],
                                               in1=xT[:, f, at], op0=ALU.mult, op1=ALU.add).then_inc(mixed, 1)
                for n, (t0, k) in enumerate(PAIRS):
                    dve.wait_ge(back, n + 1)
                    V.tensor_tensor(g.xr[:, t0:t0 + k, :], g.xr[:, t0:t0 + k, :],
                                    bank[n % 8][0:P, 0:k * D].rearrange("p (u c) -> p u c", u=k),
                                    ALU.add).then_inc(added, 1)
                dve.wait_ge(added, NP)

F2 = 512
FAR = -1e30


def second_ffn(nc, g):
    M2 = F2 // 128
    with stage(nc) as (ctx, sem):
        sb = lambda n, s, d: ctx.enter_context(nc.sbuf_tensor(n, s, d))
        ps = lambda n: ctx.enter_context(nc.psum_tensor(n, [128, 512], F32))
        xn, xT = sb("xn_z", [P, T, D], F32), sb("xT_z", [128, F, N], F32)
        stats, small = sb("stats_z", [P, T, 6], F32), sb("small_z", [P, 4, T], F32)
        gb = sb("gb_z", [P, 2, D], F32)
        wr, br = sb("wr_z", [128, F, NE], F32), sb("br_z", [P, NE], F32)
        rev = sb("rev_z", [P, NE], F32)
        logits, a, share = sb("logits_z", [P, T, NE], F32), sb("a_z", [P, T, NE], F32), sb("share_z", [P, T, NE], F32)
        hot = sb("hot_z", [P, 2, T, NE], F32)
        top, pick = sb("top_z", [P, 2, T], F32), sb("pick_z", [P, T], F32)
        ratio, first_share = sb("ratio_z", [P, T], F32), sb("first_share_z", [P, T], F32)
        shareT = sb("shareT_z", [NE, N], F32)
        w1, w2 = sb("w1_z", [128, 2, F, F2], F32), sb("w2_z", [128, 2, M2, D], F32)
        b1_rows, b1 = sb("b1_rows_z", [NE * M2, 128], F32), sb("b1_z", [128, NE * M2], F32)
        b2 = sb("b2_z", [NE, D], F32)
        hid = sb("hid_z", [128, 2, M2, 4 * P], F32)
        bank = [ps(f"bank_z{k}") for k in range(8)]
        small_in, w_in = sem("small_in_z"), [sem(f"w_in_z{k}") for k in range(2)]
        rows_done, var_ready, root_done = sem("rows_done_z"), sem("var_ready_z"), sem("root_done_z")
        dve_step, xn_ready, turned, turn_read = sem("dve_step_z"), sem("xn_ready_z"), sem("turned_z"), sem("turn_read_z")
        consts, gated, asked, answered = sem("consts_z"), sem("gated_z"), sem("asked_z"), sem("answered_z")
        share_ready, share_turned, share_read = sem("share_ready"), sem("share_turned"), sem("share_read")
        b1_turned, b1_ready, biased, bias_read = sem("b1_turned_z"), sem("b1_ready_z"), sem("biased"), sem("bias_read")
        hid_done, hid_ready, out_done, out_read = sem("hid_done_z"), sem("hid_ready_z"), sem("out_done_z"), sem("out_read_z")
        x_out = sem("x_out_z")
        NQ, NP = len(QUADS), len(PAIRS)

        with nc.Block() as block:
            @block.sync
            def _(sp):
                for k, v in enumerate((g.L1_ffn_gamma, g.L1_ffn_beta)):
                    sp.dma_start(gb[:, k, :], v[None, :].to_broadcast([P, D])).then_inc(small_in, 16)
                sp.dma_start(wr[:], g.L1_ffn_Wr.rearrange("(f i) e -> i f e", i=128)).then_inc(small_in, 16)
                sp.dma_start(br[:], g.L1_ffn_br[None, :].to_broadcast([P, NE])).then_inc(small_in, 16)
                sp.dma_start(b1_rows[:], g.L1_ffn_b1.rearrange("e (m i) -> (e m) i", i=128)).then_inc(small_in, 16)
                sp.dma_start(b2[:], g.L1_ffn_b2).then_inc(small_in, 16)
                for e in range(NE):
                    k = e % 2
                    if e >= 2:
                        sp.wait_ge(out_done, (e - 1) * T)
                        sp.wait_ge(w_in[k], 32 * (e // 2))
                    sp.dma_start(w1[:, k], g.L1_ffn_W1[e].rearrange("(f i) o -> i f o", i=128)).then_inc(w_in[k], 16)
                    sp.dma_start(w2[:, k], g.L1_ffn_W2[e].rearrange("(m i) o -> i m o", i=128)).then_inc(w_in[k], 16)
                sp.wait_ge(out_read, NE * T)
                sp.dma_start(g.out.rearrange("(t p) d -> p t d", p=P), g.xr[:]).then_inc(x_out, 16)
                sp.wait_ge(x_out, 16)

            @block.gpsimd
            def _(pool):
                pool.iota(rev[:], pattern=[[-1, NE]], base=NE, channel_multiplier=0,
                          allow_small_or_imprecise_dtypes=True).then_inc(consts, 1)

            @block.scalar
            def _(act):
                root(nc, act, small[:, 1, :], small[:, 3, :], var_ready, root_done)
                n = 0
                for t0, k in QUADS:
                    for f in range(F):
                        act.wait_ge(turned, n + 1)
                        nc.scalar.copy(xT[:, f, t0 * P:(t0 + k) * P], bank[n % 4][:, 0:k * P]).then_inc(turn_read, 1)
                        n += 1
                act.wait_ge(b1_turned, 1)
                nc.scalar.copy(b1[:], bank[4][:, 0:NE * M2]).then_inc(b1_ready, 1)
                act.wait_ge(asked, 1)
                nc.scalar.activation(ratio[:], ratio[:], ACT.Exp).then_inc(answered, 1)
                act.wait_ge(b1_ready, 1)
                for e in range(NE):
                    for q, (t0, k) in enumerate(QUADS):
                        n = e * NQ + q
                        if n >= 2:
                            act.wait_ge(out_done, (e * T + t0) - (QUADS[q - 1][1] if q else QUADS[-1][1]))
                        for m in range(M2):
                            act.wait_ge(hid_done, n * M2 + m + 1)
                            nc.scalar.activation(hid[:, n % 2, m, 0:k * P], bank[(n * M2 + m) % 4][:, 0:k * P], ACT.Gelu,
                                                 bias=b1[:, e * M2 + m:e * M2 + m + 1]).then_inc(hid_ready, 1)

            @block.tensor
            def _(pe):
                pe.wait_ge(xn_ready, 1)
                turn_tiles(nc, pe, xn, D, bank[0:4], g.ident, turn_read, turned)
                pe.wait_ge(small_in, 96)
                nc.tensor.transpose(bank[4][:, 0:NE * M2], b1_rows[:], g.ident[0:NE * M2, 0:NE * M2]).then_inc(b1_turned, 1)
                pe.wait_ge(turn_read, F * NQ)
                for t in range(T):
                    for f in range(F):
                        mm = nc.tensor.matmul(bank[5][0:P, t * NE:(t + 1) * NE], xT[:, f, t * P:(t + 1) * P],
                                              wr[:, f, :], start=(f == 0), stop=(f == F - 1))
                mm.then_inc(gated, 1)
                pe.wait_ge(share_ready, 1)
                for q, (t0, k) in enumerate(QUADS):
                    if q >= 2:
                        pe.wait_ge(share_read, q - 1)
                    for u in range(k):
                        mm = nc.tensor.transpose(bank[6 + q % 2][0:NE, u * P:(u + 1) * P], share[:, t0 + u, :],
                                                 g.ident[0:P, 0:P])
                    mm.then_inc(share_turned, 1)
                pe.wait_ge(share_read, NQ)
                for n, (t0, k) in enumerate(PAIRS):
                    if n >= 4:
                        pe.wait_ge(bias_read, n - 3)
                    for u in range(k):
                        mm = nc.tensor.matmul(bank[4 + n % 4][0:P, u * D:(u + 1) * D],
                                              shareT[:, (t0 + u) * P:(t0 + u + 1) * P], b2[:], start=True, stop=True)
                    mm.then_inc(biased, 1)
                pe.wait_ge(bias_read, NP)
                pe.wait_ge(b1_ready, 1)

                def up(n):
                    e, q = n // NQ, n % NQ
                    t0, k = QUADS[q]
                    pe.wait_ge(w_in[e % 2], 32 * (e // 2 + 1))
                    for m in range(M2):
                        if n * M2 + m >= 4:
                            pe.wait_ge(hid_ready, n * M2 + m - 3)
                        for f in range(F):
                            mm = nc.tensor.matmul(bank[(n * M2 + m) % 4][:, 0:k * P],
                                                  w1[:, e % 2, f, m * 128:(m + 1) * 128],
                                                  xT[:, f, t0 * P:(t0 + k) * P], start=(f == 0), stop=(f == F - 1))
                        mm.then_inc(hid_done, 1)

                def down(n):
                    e, q = n // NQ, n % NQ
                    t0, k = QUADS[q]
                    pe.wait_ge(hid_ready, (n + 1) * M2)
                    for u in range(k):
                        c = e * T + t0 + u
                        if c >= 4:
                            pe.wait_ge(out_read, c - 3)
                        for m in range(M2):
                            mm = nc.tensor.matmul(bank[4 + c % 4][0:P, 0:D], hid[:, n % 2, m, u * P:(u + 1) * P],
                                                  w2[:, e % 2, m, :], start=(m == 0), stop=(m == M2 - 1))
                        mm.then_inc(out_done, 1)

                up(0)
                for n in range(1, NE * NQ):
                    if n % NQ:
                        up(n)
                        down(n - 1)
                    else:
                        down(n - 1)
                        up(n)
                down(NE * NQ - 1)

            @block.vector
            def _(dve):
                step = Step(dve, dve_step)
                V = nc.vector
                bc = lambda v: v[:, :, None].to_broadcast([P, T, NE])
                layer_norm(nc, dve, step, g.xr, xn, stats, small, rows_done, var_ready, root_done)
                dve.wait_ge(small_in, 96)
                step(V.tensor_tensor(xn[:], xn[:], gb[:, 0:1, :].to_broadcast([P, T, D]), ALU.mult))
                V.tensor_tensor(xn[:], xn[:], gb[:, 1:2, :].to_broadcast([P, T, D]), ALU.add).then_inc(xn_ready, 1)
                dve.wait_ge(gated, 1)
                dve.wait_ge(consts, 1)
                step(V.tensor_tensor(logits[:], bank[5][0:P, 0:T * NE].rearrange("p (t e) -> p t e", e=NE),
                                     br[:, None, :].to_broadcast([P, T, NE]), ALU.add))
                for k in range(2):
                    step(V.tensor_reduce(top[:, k, :], logits[:], AX.X, ALU.max))
                    step(V.tensor_tensor(a[:], logits[:], bc(top[:, k, :]), ALU.is_equal))
                    step(V.tensor_tensor(a[:], a[:], rev[:, None, :].to_broadcast([P, T, NE]), ALU.mult))
                    step(V.tensor_reduce(pick[:], a[:], AX.X, ALU.max))
                    step(V.tensor_tensor(hot[:, k], a[:], bc(pick[:]), ALU.is_equal))
                    if k == 0:
                        step(V.scalar_tensor_tensor(out=logits[:], in0=hot[:, 0], scalar=FAR, in1=logits[:],
                                                    op0=ALU.mult, op1=ALU.add))
                V.tensor_tensor(ratio[:], top[:, 1, :], top[:, 0, :], ALU.subtract).then_inc(asked, 1)
                dve.wait_ge(answered, 1)
                step(V.tensor_scalar_add(first_share[:], ratio[:], 1.0))
                step(V.reciprocal(first_share[:], first_share[:]))
                step(V.tensor_tensor(ratio[:], ratio[:], first_share[:], ALU.mult))
                step(V.tensor_tensor(share[:], hot[:, 0], bc(first_share[:]), ALU.mult))
                step(V.tensor_tensor(a[:], hot[:, 1], bc(ratio[:]), ALU.mult))
                V.tensor_tensor(share[:], share[:], a[:], ALU.add).then_inc(share_ready, 1)
                for q, (t0, k) in enumerate(QUADS):
                    dve.wait_ge(share_turned, q + 1)
                    V.tensor_copy(shareT[:, t0 * P:(t0 + k) * P], bank[6 + q % 2][0:NE, 0:k * P]).then_inc(share_read, 1)
                for n, (t0, k) in enumerate(PAIRS):
                    dve.wait_ge(biased, n + 1)
                    V.tensor_tensor(g.xr[:, t0:t0 + k, :], g.xr[:, t0:t0 + k, :],
                                    bank[4 + n % 4][0:P, 0:k * D].rearrange("p (u c) -> p u c", u=k),
                                    ALU.add).then_inc(bias_read, 1)
                dve.wait_ge(bias_read, NP)
                for e in range(NE):
                    if e:
                        dve.wait_ge(out_read, e * T)
                    for t in range(T):
                        c = e * T + t
                        dve.wait_ge(out_done, c + 1)
                        V.scalar_tensor_tensor(out=g.xr[:, t, :], in0=bank[4 + c % 4][0:P, 0:D],
                                               scalar=share[:, t, e:e + 1], in1=g.xr[:, t, :], op0=ALU.mult,
                                               op1=ALU.add).then_inc(out_read, 1)


def prepare(nc, g):
    with stage(nc) as (_, sem):
        ones_ready, ready = sem("ones_ready"), sem("consts_ready")
        with nc.Block() as block:
            @block.gpsimd
            def _(pool):
                pool.iota(g.iota[:], pattern=[[1, 128]], base=0, channel_multiplier=0,
                          allow_small_or_imprecise_dtypes=True).then_inc(ready, 1)
                pool.memset(g.ones[:], 1.0).then_inc(ones_ready, 1)
                pool.wait_ge(ones_ready, 1)
                pool.affine_select(out=g.ident[:], in_=g.ones[:], compare_op=ALU.is_equal, fill=0.0, base=0,
                                   pattern=[[-1, 128]], channel_multiplier=1).then_inc(ready, 1)
                pool.wait_ge(ready, 2)


def program(nc, g):
    dram = lambda n, s: nc.dram_tensor(n, s, F32).ap()
    g.slots = dram("slots", (NB * P, 2))
    g.xn, g.weights, g.dinv = dram("xn_dram", (N, D)), dram("weights_dram", (N, N)), dram("dinv_dram", (N,))
    g.placed, g.results = dram("placed_dram", (NE * CP, D)), dram("results_dram", (NE * CP, D))
    with ExitStack() as whole:
        keep = lambda ctx, n, s, d: ctx.enter_context(nc.sbuf_tensor(n, s, d))
        g.spare = keep(whole, "spare", [128, 4], F32)
        g.ident, g.ones = keep(whole, "ident", [128, 128], F32), keep(whole, "ones", [128, 128], F32)
        g.iota = keep(whole, "iota", [128, 128], BF16)
        g.deg = keep(whole, "deg", [P, T, 4], F32)
        prepare(nc, g)
        g.dyn, g.h = keep(whole, "dyn", [P, T, C0], F32), keep(whole, "h", [P, T, C0], F32)
        with ExitStack() as ctx:
            g.ranks = keep(ctx, "ranks", [P, EC], F32)
            sort_edges(nc, g)
        with ExitStack() as graph:
            g.xparts = keep(graph, "xparts", [P, T, 3, C0], BF16)
            normalise_input(nc, g)
            g.counts = keep(graph, "counts", [P, T, N], BF16)
            with ExitStack() as build:
                g.slot_w, g.slot_ids = keep(build, "slot_w", [P, NB], F32), keep(build, "slot_ids", [P, 2, NB], F32)
                g.slot_deg = keep(build, "slot_deg", [P, NB, 4], BF16)
                load_slots(nc, g)
                build_blocks(nc, g)
            static_convs(nc, g)
        g.xr = keep(whole, "xr", [P, T, D], F32)
        first_gnn_out(nc, g)
        g.chance, g.gather_at = keep(whole, "chance", [P, T], F32), keep(whole, "gather_at", [P, T], U32)
        route_first(nc, g)
        first_experts(nc, g)
        combine_first(nc, g)
        second_gnn(nc, g)
        second_ffn(nc, g)


_INS = ["x", "src", "dst", "edge_weight", "L0_gnn_W_static", "L0_gnn_b_static", "L0_gnn_W1", "L0_gnn_b1", "L0_gnn_W2",
        "L0_gnn_b2", "L0_gnn_W_aggr", "L0_gnn_b_aggr", "L0_ffn_gate_w", "L0_ffn_gate_b", "L0_ffn_w1", "L0_ffn_b1",
        "L0_ffn_w2", "L0_ffn_b2", "L1_gnn_W1", "L1_gnn_b1", "L1_gnn_W2", "L1_gnn_b2", "L1_gnn_gamma", "L1_gnn_beta",
        "L1_ffn_gamma", "L1_ffn_beta", "L1_ffn_Wr", "L1_ffn_br", "L1_ffn_W1", "L1_ffn_b1", "L1_ffn_W2", "L1_ffn_b2"]


class Tensors:
    pass


def kernel(**inputs):
    import numpy as _np
    import concourse.bacc as _bacc
    from concourse import mybir as _mybir
    from concourse.bass_utils import run_bass_kernel_spmd as _run

    nc = _bacc.Bacc("TRN2", target_bir_lowering=False, num_devices=1)
    arrays, g = {}, Tensors()
    for name in _INS:
        a = _np.ascontiguousarray(inputs[name])
        arrays[f"in_{name}_dram"] = a
        g.__dict__[name] = nc.dram_tensor(f"in_{name}_dram", a.shape, _mybir.dt.from_np(a.dtype),
                                          kind="ExternalInput").ap()
    g.out = nc.dram_tensor("out_0_dram", (N, D), _mybir.dt.float32, kind="ExternalOutput").ap()
    program(nc, g)
    r = _run(nc, [arrays], core_ids=[0])
    return r.results[0]["out_0_dram"]
```

```python
from contextlib import ExitStack, contextmanager

import concourse.bass as bass
from concourse import mybir

F32 = mybir.dt.float32
BF16 = mybir.dt.bfloat16
F16 = mybir.dt.float16
I32 = mybir.dt.int32
U32 = mybir.dt.uint32
ALU = mybir.AluOpType
ACT = mybir.ActivationFunctionType
AX = mybir.AxisListType

N, D, E = 3125, 256, 50000
P = 125
T = N // P
NB = T * T
EC = E // P
C0 = 64
NO_LANE = 127
EMPTY = float(NO_LANE * 128 + NO_LANE)
PAST = float(1 << 20)
ROUND = float(3 << 22)


class Step:

    def __init__(self, engine, semaphore):
        self.engine, self.semaphore, self.count = engine, semaphore, 0

    def __call__(self, instruction):
        self.count += 1
        instruction.then_inc(self.semaphore, 1)
        self.engine.wait_ge(self.semaphore, self.count)


_uses = {}


def unique(name):
    _uses[name] = _uses.get(name, 0) + 1
    return f"{name}_{_uses[name]}"


@contextmanager
def stage(nc):
    sems = []

    def sem(name):
        sems.append(nc.alloc_semaphore(name=unique(name)))
        return sems[-1]

    with ExitStack() as ctx:
        yield ctx, sem
    nc.all_engine_barrier()
    nc.clear_and_free_semaphores(sems)
    nc.all_engine_barrier()


def sort_edges(nc, g):
    G = 16
    TRIPS = EC // G
    Q = G // 4
    HB = (NB + 1) // 2
    with stage(nc) as (ctx, sem):
        sb = lambda n, s, d: ctx.enter_context(nc.sbuf_tensor(unique(n), s, d))
        src_i, dst_i = sb("src_i", [P, EC], I32), sb("dst_i", [P, EC], I32)
        local = sb("local", [P, 2, EC], F32)
        tile_of = sb("tile_of", [P, 2, EC], F32)
        tmp = sb("tmp_edge", [P, EC], F32)
        key = sb("key", [P, EC], F32)
        keyp = sb("keyp", [P, EC], F32)
        rec = sb("rec", [P, EC, 2], F32)
        blank = sb("blank", [P, NB, 2], F32)
        iota_nb = sb("iota_nb", [P, 2, HB], F16)
        ones_nb = sb("ones_nb", [P, P], BF16)
        before = sb("before", [P, P], BF16)
        rest = sb("rest", [P, P], BF16)
        hot = sb("hot", [P, G, 2, HB], BF16)
        junk = sb("junk", [P, 2, 2, HB], BF16)
        rank = sb("rank_ring", [P, G], F32)
        over = sb("over", [P, 4], F32)
        pos = sb("pos", [P, 4], F32)
        idx = sb("idx", [P, Q, 4], U32)
        staged = sb("staged", [P, Q, 4, 2], F32)
        count = [ctx.enter_context(nc.psum_tensor(unique(f"count{b}"), [P, 2, 512], F32)) for b in range(2)]

        edges_in, blank_out = sem("edges_in"), sem("blank_out")
        consts, prep, w_placed = sem("consts"), sem("prep"), sem("w_placed")
        dve_step, pos_step = sem("dve_step_a"), sem("pos_step")
        hot_ready, counted, rank_read = sem("hot_ready"), sem("counted"), sem("rank_read")
        idx_ready, stage_ready = sem("idx_ready"), sem("stage_ready")
        ranks_kept, ranked, edges_out = sem("ranks_kept"), sem("ranked"), sem("edges_out")
        pool_read, scatter_go = sem("pool_read"), sem("scatter_go")
        scattered = [sem(f"scattered{h}") for h in range(Q)]

        with nc.Block() as block:
            @block.sync
            def _(sp):
                sp.dma_start(src_i[:], g.src.rearrange("(p t) -> p t", p=P)).then_inc(edges_in, 16)
                sp.dma_start(dst_i[:], g.dst.rearrange("(p t) -> p t", p=P)).then_inc(edges_in, 16)
                sp.dma_start(tmp[:], g.edge_weight.rearrange("(p t) -> p t", p=P)).then_inc(edges_in, 16)
                sp.wait_ge(consts, 1)
                sp.dma_start(g.slots.rearrange("(p n) k -> p (n k)", p=P),
                             blank[:].rearrange("p n k -> p (n k)")).then_inc(blank_out, 16)
                sp.wait_ge(blank_out, 16)
                sp.wait_ge(ranked, 1)
                sp.dma_start(g.edge_rec, rec[:].rearrange("p t k -> p (t k)")).then_inc(edges_out, 16)
                sp.dma_start(g.edge_key, keyp[:]).then_inc(edges_out, 16)
                sp.dma_start(g.edge_rank, g.ranks[:]).then_inc(edges_out, 16)
                sp.wait_ge(edges_out, 48)

            @block.gpsimd
            def _(pool):
                pool.memset(blank[:, :, 0], 0.0)
                pool.memset(blank[:, :, 1], EMPTY).then_inc(consts, 1)
                pool.iota(iota_nb[:], pattern=[[HB, 2], [1, HB]], base=0, channel_multiplier=0,
                          allow_small_or_imprecise_dtypes=True).then_inc(consts, 1)
                pool.memset(ones_nb[:], 1.0).then_inc(pool_read, 1)
                pool.wait_ge(pool_read, 1)
                pool.affine_select(out=before[:], in_=ones_nb[:], compare_op=ALU.is_gt, fill=0.0, base=0,
                                   pattern=[[1, P]], channel_multiplier=-1)
                pool.affine_select(out=rest[:], in_=ones_nb[:], compare_op=ALU.is_ge, fill=0.0, base=0,
                                   pattern=[[-1, P]], channel_multiplier=1).then_inc(consts, 1)
                pool.wait_ge(blank_out, 16)

                bound = pool.to_reg(NB * P - 1)

                def scatter(i, h):
                    pool.wait_ge(idx_ready, i * Q + h + 1)
                    pool.wait_ge(stage_ready, i * Q + h + 1)
                    pool.sem_inc(scatter_go)
                    for u in range(4):
                        pool.indirect_dma_start(
                            out=g.slots, out_offset=bass.IndirectOffsetOnAxis(ap=idx[:, h, u:u + 1], axis=0),
                            in_=staged[:, h, u, :], in_offset=None, bounds_check=bound,
                            oob_is_err=False).then_inc(scattered[h], 16)

                with pool.Fori(0, TRIPS) as i:
                    for h in range(Q):
                        scatter(i, h)
                for h in range(Q):
                    pool.wait_ge(scattered[h], TRIPS * 64)

            @block.scalar
            def _(act):
                act.wait_ge(edges_in, 48)
                nc.scalar.copy(rec[:, :, 0], tmp[:]).then_inc(w_placed, 1)
                act.wait_ge(prep, 1)
                act.wait_ge(w_placed, 1)

                def fill_stage(i, h, first):
                    if not first:
                        act.wait_ge(scattered[h], i * 64)
                    nc.scalar.copy(staged[:, h, :, :], rec[:, bass.ds(i * G + 4 * h, 4), :]).then_inc(stage_ready, 1)

                for h in range(Q):
                    fill_stage(0, h, True)
                with act.Fori(1, TRIPS) as i:
                    for h in range(Q):
                        fill_stage(i, h, False)

            @block.vector
            def _(dve):
                step = Step(dve, dve_step)
                dve.wait_ge(edges_in, 48)
                dve.wait_ge(w_placed, 1)
                for k, ids in enumerate((src_i, dst_i)):
                    step(nc.vector.tensor_copy(local[:, k, :], ids[:]))
                    step(nc.vector.tensor_scalar(tmp[:], local[:, k, :], 1.0 / P, -(P // 2) / P, ALU.mult, ALU.add))
                    step(nc.vector.tensor_scalar_add(tile_of[:, k, :], tmp[:], ROUND))
                    step(nc.vector.tensor_scalar_add(tmp[:], tile_of[:, k, :], -ROUND))
                    step(nc.vector.tensor_copy(tile_of[:, k, :], tmp[:]))
                    step(nc.vector.scalar_tensor_tensor(out=tmp[:], in0=tile_of[:, k, :], scalar=float(-P),
                                                        in1=local[:, k, :], op0=ALU.mult, op1=ALU.add))
                    step(nc.vector.tensor_copy(local[:, k, :], tmp[:]))
                step(nc.vector.scalar_tensor_tensor(out=key[:], in0=tile_of[:, 0, :], scalar=float(T),
                                                    in1=tile_of[:, 1, :], op0=ALU.mult, op1=ALU.add))
                step(nc.vector.tensor_scalar_mul(keyp[:], key[:], float(P)))
                step(nc.vector.scalar_tensor_tensor(out=rec[:, :, 1], in0=local[:, 0, :], scalar=128.0,
                                                    in1=local[:, 1, :], op0=ALU.mult, op1=ALU.add))
                nc.vector.tensor_copy(g.spare[:P, 0:1], key[:, 0:1]).then_inc(prep, 1)
                dve.wait_ge(consts, 3)

                def one_hot(t, slot):
                    nc.vector.tensor_scalar(hot[:, slot, :, :], iota_nb[:], key[:, bass.ds(t, 1)], None,
                                            ALU.is_equal).then_inc(hot_ready, 1)

                def read_rank(t, u, t_before):
                    dve.wait_ge(counted, t + 1)
                    if t_before is not None:
                        dve.wait_ge(rank_read, t_before)
                    nc.vector.tensor_tensor_reduce(
                        out=junk[:, u % 2], in0=hot[:, u], in1=count[u % 2][:, :, 0:HB], scale=1.0,
                        scalar=0.0, op0=ALU.mult, op1=ALU.add, accum_out=rank[:, u:u + 1]).then_inc(rank_read, 1)

                def positions(i, h, first):
                    dve.wait_ge(rank_read, i * G + 4 * h + 4)
                    nc.vector.tensor_copy(g.ranks[:, bass.ds(i * G + 4 * h, 4)], rank[:, 4 * h:4 * h + 4]).then_inc(
                        ranks_kept, 1)
                    nc.vector.tensor_scalar(over[:], rank[:, 4 * h:4 * h + 4], float(P), PAST, ALU.is_ge,
                                            ALU.mult).then_inc(pos_step, 1)
                    nc.vector.tensor_tensor(pos[:], rank[:, 4 * h:4 * h + 4], keyp[:, bass.ds(i * G + 4 * h, 4)],
                                            ALU.add).then_inc(pos_step, 1)
                    dve.wait_ge(pos_step, (i * Q + h) * 2 + 2)
                    if not first:
                        dve.wait_ge(scattered[h], i * 64)
                    nc.vector.tensor_tensor(idx[:, h, :], pos[:], over[:], ALU.add).then_inc(idx_ready, 1)

                def trip(i, first=False, last=False):
                    for u in range(G):
                        if not (last and u >= G - 2):
                            one_hot(i * G + u + 2, (u + 2) % G)
                        read_rank(i * G + u, u, None if first and u < 2 else i * G + u - 1)
                        if u % 4 == 3:
                            positions(i, u // 4, first)

                one_hot(0, 0)
                one_hot(1, 1)
                trip(0, first=True)
                with dve.Fori(1, TRIPS - 1) as i:
                    trip(i)
                trip(TRIPS - 1, last=True)
                dve.wait_ge(ranks_kept, TRIPS * Q)
                dve.sem_inc(ranked)

            @block.tensor
            def _(pe):
                pe.wait_ge(consts, 3)

                def add(b, what, slot, start=False, inc=None):
                    for c in range(2):
                        mm = nc.tensor.matmul(count[b][:, c, 0:HB], what, hot[:, slot, c, :], start=start,
                                              stop=True, skip_group_check=True)
                    if inc is not None:
                        mm.then_inc(inc, 1)

                def tally(t, u, old=True, older=True):
                    if older:
                        pe.wait_ge(rank_read, t - 1)
                        add(u % 2, rest[:], (u - 2) % G)
                    if old:
                        add(u % 2, ones_nb[:], (u - 1) % G, start=not older)
                    pe.wait_ge(hot_ready, t + 1)
                    add(u % 2, before[:], u, start=not old, inc=counted)

                for u in range(G):
                    tally(u, u, old=u >= 1, older=u >= 2)
                with pe.Fori(1, TRIPS) as i:
                    for u in range(G):
                        tally(i * G + u, u)

GROUPS = [4, 3, 3, 3, 3, 3, 3, 3]
BASES = [sum(GROUPS[:j]) for j in range(len(GROUPS))]
NG = len(GROUPS)
EPS = 1e-5


def root(nc, act, value, out, ready, done):
    act.wait_ge(ready, 1)
    nc.scalar.activation(out, value, ACT.Sqrt).then_inc(done, 1)


def inverse_root(nc, dve, step, value, rooted, tmp, done):
    dve.wait_ge(done, 1)
    step(nc.vector.reciprocal(tmp, rooted))
    step(nc.vector.tensor_tensor(tmp, tmp, value, ALU.mult))
    step(nc.vector.tensor_tensor(tmp, tmp, rooted, ALU.add))
    step(nc.vector.tensor_scalar_mul(tmp, tmp, 0.5))
    step(nc.vector.reciprocal(value, tmp))


def layer_norm(nc, dve, step, x, xn, stats, small, rows_done, var_ready, rstd_ready):
    with dve.Fori(0, T) as t:
        nc.vector.bn_stats(stats[:, bass.ds(t, 1), :].rearrange("p a k -> p (a k)"),
                           x[:, bass.ds(t, 1), :].rearrange("p a k -> p (a k)")).then_inc(rows_done, 1)
    dve.wait_ge(rows_done, T)
    mean, var, dif, mean2 = (small[:, k, :] for k in range(4))
    step(nc.vector.tensor_tensor(mean, stats[:, :, 1], stats[:, :, 4], ALU.add))
    step(nc.vector.tensor_tensor(dif, stats[:, :, 1], stats[:, :, 4], ALU.subtract))
    step(nc.vector.tensor_tensor(var, stats[:, :, 2], stats[:, :, 5], ALU.add))
    step(nc.vector.tensor_scalar_mul(mean, mean, 0.5))
    step(nc.vector.tensor_tensor(dif, dif, dif, ALU.mult))
    step(nc.vector.tensor_scalar(dif, dif, 0.25, EPS, ALU.mult, ALU.add))
    nc.vector.scalar_tensor_tensor(out=var, in0=var, scalar=1.0 / D, in1=dif, op0=ALU.mult,
                                   op1=ALU.add).then_inc(var_ready, 1)
    inverse_root(nc, dve, step, var, mean2, dif, rstd_ready)
    with dve.Fori(0, T) as t:
        one = lambda a: a[:, bass.ds(t, 1), :].rearrange("p a k -> p (a k)")
        nc.vector.tensor_scalar(one(xn), one(x), mean[:, bass.ds(t, 1)], var[:, bass.ds(t, 1)], ALU.subtract,
                                ALU.mult).then_inc(rows_done, 1)
    dve.wait_ge(rows_done, 2 * T)


def split3(nc, step, whole, parts, left):
    step(nc.vector.tensor_copy(parts(0), whole))
    step(nc.vector.tensor_tensor(left, whole, parts(0), ALU.subtract))
    step(nc.vector.tensor_copy(parts(1), left))
    step(nc.vector.tensor_tensor(left, left, parts(1), ALU.subtract))
    step(nc.vector.tensor_copy(parts(2), left))


def normalise_input(nc, g):
    with stage(nc) as (ctx, sem):
        sb = lambda n, s, d: ctx.enter_context(nc.sbuf_tensor(unique(n), s, d))
        x, xn = sb("x_in", [P, T, D], F32), sb("xn_in", [P, T, D], F32)
        stats, small = sb("stats0", [P, T, 6], F32), sb("small0", [P, 4, T], F32)
        left = sb("left0", [P, T, C0], F32)
        x_in, xn_ready, xn_out = sem("x_in_done"), sem("xn_ready"), sem("xn_out")
        rows_done, dve_step = sem("rows_done0"), sem("dve_step0")
        var_ready, rstd_ready = sem("var_ready0"), sem("rstd_ready0")
        with nc.Block() as block:
            @block.scalar
            def _(act):
                root(nc, act, small[:, 1, :], small[:, 3, :], var_ready, rstd_ready)

            @block.sync
            def _(sp):
                sp.dma_start(x[:], g.x.rearrange("(t p) d -> p t d", p=P)).then_inc(x_in, 16)
                sp.wait_ge(xn_ready, 1)
                sp.dma_start(g.xn.rearrange("(t p) d -> p t d", p=P), xn[:]).then_inc(xn_out, 16)
                sp.wait_ge(xn_out, 16)

            @block.vector
            def _(dve):
                step = Step(dve, dve_step)
                dve.wait_ge(x_in, 16)
                layer_norm(nc, dve, step, x, xn, stats, small, rows_done, var_ready, rstd_ready)
                split3(nc, step, xn[:, :, 0:C0], lambda k: g.xparts[:, :, k, :], left[:])
                nc.vector.tensor_copy(g.spare[:P, 0:1], left[:, 0, 0:1]).then_inc(xn_ready, 1)


def load_slots(nc, g):
    CH = NB // P
    with stage(nc) as (ctx, sem):
        sb = lambda n, s, d: ctx.enter_context(nc.sbuf_tensor(unique(n), s, d))
        raw = sb("raw_slots", [P, CH, P, 2], F32)
        turned = [ctx.enter_context(nc.psum_tensor(unique(f"turned{k}"), [P, 2, 512], F32)) for k in range(2)]
        code = sb("code", [P, NB], I32)
        field = sb("field", [P, 2, NB], I32)
        left = sb("left1", [P, NB], F32)
        whole = g.h[:].rearrange("p t c -> p (t c)")[:, 0:NB]
        slots_in, turned_done, dve_step = sem("slots_in"), sem("turned_done"), sem("dve_step1")
        with nc.Block() as block:
            @block.sync
            def _(sp):
                sp.dma_start(raw[:].rearrange("q c e k -> q c (e k)"),
                             g.slots.rearrange("(c q e) k -> q c (e k)", c=CH, q=P)).then_inc(slots_in, 16)

            @block.tensor
            def _(pe):
                pe.wait_ge(slots_in, 16)
                for k in range(2):
                    for c in range(CH):
                        out = turned[k][:, c // 4, (c % 4) * P:(c % 4 + 1) * P]
                        nc.tensor.transpose(out, raw[:, c, :, k], g.ident[0:P, 0:P]).then_inc(turned_done, 1)

            @block.vector
            def _(dve):
                step = Step(dve, dve_step)
                dve.wait_ge(turned_done, 2 * CH)
                for c, (lo, hi) in enumerate(((0, 4 * P), (4 * P, NB))):
                    step(nc.vector.tensor_copy(whole[:, lo:hi], turned[0][:, c, 0:hi - lo]))
                    step(nc.vector.tensor_copy(code[:, lo:hi], turned[1][:, c, 0:hi - lo]))
                step(nc.vector.tensor_scalar(field[:, 0, :], code[:], 7, None, ALU.logical_shift_right))
                step(nc.vector.tensor_scalar(field[:, 1, :], code[:], 127, None, ALU.bitwise_and))
                step(nc.vector.tensor_copy(g.slot_ids[:], field[:]))
                step(nc.vector.memset(g.slot_deg[:, :, 0:1], 1.0))
                split3(nc, step, whole, lambda k: g.slot_deg[:, :, 1 + k], left[:])
                step(nc.vector.tensor_copy(g.slot_w[:], g.slot_deg[:, :, 3]))


def build_blocks(nc, g):
    H = 3
    R = 2
    with stage(nc) as (ctx, sem):
        sb = lambda n, s, d: ctx.enter_context(nc.sbuf_tensor(unique(n), s, d))
        ps = lambda n, s: ctx.enter_context(nc.psum_tensor(unique(n), s, F32))
        src_hot = sb("src_hot", [P, H, 4, P], BF16)
        dst_hot = sb("dst_hot", [P, H, 4, 4, P], BF16)
        degs = sb("degs_now", [P, H, 4, 4], BF16)
        turned = sb("countT", [P, R, 4, P], BF16)
        zero = sb("zero_deg", [P, T * 4], BF16)
        strip = g.h[:].rearrange("p t c -> p (t c)")[:, 0:R * 4 * P].rearrange("p (r u e) -> p r u e", r=R, u=4)
        p_cw = [ps(f"p_cw{r}", [P, 4, 256]) for r in range(R)]
        p_t = [ps(f"p_t{r}", [P, 512]) for r in range(R)]
        p_deg, p_dyn = ps("p_deg", [P, 512]), ps("p_dyn", [P, 512])

        zeroed = sem("zeroed")
        hot_ready, two_ready, three_ready = sem("hot_ready_b"), sem("two_ready"), sem("three_ready")
        pool_go = sem("pool_go")
        blocks = sem("blocks")
        ev_c, ev_w, ev_t = sem("ev_c"), sem("ev_w"), sem("ev_t")
        spread = sem("spread")
        dyn_read = sem("dyn_read")
        strip_out = [sem(f"strip_out{r}") for r in range(R)]

        back = lambda j: H if j >= H else j + NG - max(i for i in range(NG) if i % H == j)

        with nc.Block() as block:
            @block.vector
            def _(dve):
                nc.vector.memset(zero[:], 0.0).then_inc(zeroed, 1)

                def make(s, j, n, first):
                    r, k = j % H, GROUPS[j]
                    if not (first and j < H):
                        dve.wait_ge(blocks, n - back(j) + 1)
                    nc.vector.tensor_copy(degs[:, r, 0:k, :], g.slot_deg[:, bass.ds(s * T + BASES[j], k), :])
                    for u in range(k):
                        b = s * T + BASES[j] + u
                        node = lambda i: g.slot_ids[:, i, bass.ds(b, 1)]
                        nc.vector.tensor_scalar(dst_hot[:, r, u, 0, :], g.iota[:P, 0:P], node(1), None, ALU.is_equal)
                        ins = nc.vector.tensor_scalar(src_hot[:, r, u, :], g.iota[:P, 0:P], node(0), None, ALU.is_equal)
                    ins.then_inc(hot_ready, 1)

                def evacuate(s, j, n, first):
                    w = GROUPS[j] * P
                    dve.wait_ge(blocks, n + 1)
                    if not (first and j < R):
                        dve.wait_ge(spread, n - R + 1)
                    nc.vector.tensor_copy(turned[:, j % R, 0:GROUPS[j], :].rearrange("p u e -> p (u e)"),
                                          p_t[j % R][:P, 0:w]).then_inc(ev_t, 1)

                def read_dyn(s, count):
                    dve.wait_ge(spread, count * NG)
                    nc.vector.tensor_reduce(g.dyn[:, bass.ds(s, 1), :].rearrange("p a k -> p (a k)"),
                                            p_dyn[:P, 0:3 * C0].rearrange("p (k c) -> p c k", k=3), AX.X,
                                            ALU.add).then_inc(dyn_read, 1)

                def whole(s, first=False, last=False):
                    for j in range(NG):
                        n = s * NG + j
                        if j + 1 < NG:
                            make(s, j + 1, n + 1, first)
                        elif not last:
                            make(s + 1, 0, n + 1, False)
                        if j == 0 and not first:
                            evacuate(s - 1, NG - 1, n - 1, False)
                        elif j > 0:
                            evacuate(s, j - 1, n - 1, first)
                        if j == 2 and not first:
                            read_dyn(s - 1, s)

                make(0, 0, 0, True)
                whole(0, first=True)
                with dve.Fori(1, T - 1) as s:
                    whole(s)
                whole(T - 1, last=True)
                evacuate(T - 1, NG - 1, T * NG - 1, False)
                read_dyn(T - 1, T)
                dve.wait_ge(blocks, T * NG)
                nc.vector.tensor_copy(g.deg[:].rearrange("p t k -> p (t k)"), p_deg[:P, 0:T * 4])

            @block.gpsimd
            def _(pool):
                with pool.Fori(0, T) as s:
                    for j in range(NG):
                        r, k = j % H, GROUPS[j]
                        pool.wait_ge(hot_ready, s * NG + j + 1)
                        pool.sem_inc(pool_go)
                        for i in range(1, 3):
                            ins = nc.gpsimd.tensor_tensor(
                                dst_hot[:, r, 0:k, i, :], dst_hot[:, r, 0:k, 0, :],
                                g.slot_deg[:, bass.ds(s * T + BASES[j], k), i:i + 1].to_broadcast([P, k, P]), ALU.mult)
                        ins.then_inc(two_ready, 1)

            @block.scalar
            def _(act):
                def weigh(s, j, n):
                    act.wait_ge(hot_ready, n + 1)
                    for u in range(GROUPS[j]):
                        ins = nc.scalar.activation(dst_hot[:, j % H, u, 3, :], dst_hot[:, j % H, u, 0, :], ACT.Copy,
                                                   scale=g.slot_w[:, bass.ds(s * T + BASES[j] + u, 1)])
                    ins.then_inc(three_ready, 1)

                def evacuate(s, j, n, first):
                    r, k, lo = j % R, GROUPS[j], BASES[j] * P
                    act.wait_ge(blocks, n + 1)
                    nc.scalar.copy(g.counts[:, bass.ds(s, 1), lo:lo + k * P].rearrange("p a (u e) -> p (a u) e", e=P),
                                   p_cw[r][:, 0:k, 0:P]).then_inc(ev_c, 1)
                    if not (first and j < R):
                        act.wait_ge(strip_out[r], (s * (NG // R) + j // R) * 16)
                    nc.scalar.copy(strip[:, r, 0:k, :], p_cw[r][:, 0:k, P:2 * P]).then_inc(ev_w, 1)

                def whole(s, first=False, last=False):
                    for j in range(NG):
                        if j + 1 < NG:
                            weigh(s, j + 1, s * NG + j + 1)
                        elif not last:
                            weigh(s + 1, 0, s * NG + NG)
                        if j > 0:
                            evacuate(s, j - 1, s * NG + j - 1, first)
                        elif not first:
                            evacuate(s - 1, NG - 1, s * NG - 1, False)

                weigh(0, 0, 0)
                whole(0, first=True)
                with act.Fori(1, T - 1) as s:
                    whole(s)
                whole(T - 1, last=True)
                evacuate(T - 1, NG - 1, T * NG - 1, False)

            @block.sync
            def _(sp):
                with sp.Fori(0, T) as s:
                    for j in range(NG):
                        r, k, lo = j % R, GROUPS[j], BASES[j] * P
                        sp.wait_ge(ev_w, s * NG + j + 1)
                        sp.dma_start(g.weights[bass.ds(s * P, P), lo:lo + k * P],
                                     strip[:, r, 0:k, :].rearrange("p u e -> p (u e)")).then_inc(strip_out[r], 16)
                for r in range(R):
                    sp.wait_ge(strip_out[r], T * NG // R * 16)

            @block.tensor
            def _(pe):
                pe.wait_ge(zeroed, 1)
                nc.tensor.matmul(p_deg[:P, 0:T * 4], g.iota[:P, 0:P], zero[:], start=True, stop=True,
                                 skip_group_check=True)

                def products(s, j, n, first):
                    r, h = j % R, j % H
                    pe.wait_ge(hot_ready, n + 1)
                    if not (first and j < R):
                        pe.wait_ge(ev_t, n - R + 1)
                    for u in range(GROUPS[j]):
                        d = BASES[j] + u
                        nc.tensor.matmul(p_deg[:P, d * 4:d * 4 + 4], dst_hot[:, h, u, 0, :], degs[:, h, u, :],
                                         start=False, stop=True, skip_group_check=True)
                        nc.tensor.matmul(p_t[r][:P, u * P:(u + 1) * P], dst_hot[:, h, u, 0, :], src_hot[:, h, u, :],
                                         start=True, stop=True)
                    if not (first and j < R):
                        pe.wait_ge(ev_c, n - R + 1)
                        pe.wait_ge(ev_w, n - R + 1)
                    pe.wait_ge(two_ready, n + 1)
                    pe.wait_ge(three_ready, n + 1)
                    for u in range(GROUPS[j]):
                        nc.tensor.matmul(p_cw[r][:, u, 0:2 * P], src_hot[:, h, u, :],
                                         dst_hot[:, h, u, 0:2, :].rearrange("p k e -> p (k e)"), start=True, stop=False,
                                         skip_group_check=True)
                        for k in range(2, 4):
                            mm = nc.tensor.matmul(p_cw[r][:, u, P:2 * P], src_hot[:, h, u, :], dst_hot[:, h, u, k, :],
                                                  start=False, stop=k == 3, skip_group_check=True)
                    mm.then_inc(blocks, 1)

                def spread_group(j, n, wait_dyn):
                    pe.wait_ge(ev_t, n + 1)
                    if wait_dyn is not None:
                        pe.wait_ge(dyn_read, wait_dyn)
                    for u in range(GROUPS[j]):
                        d = BASES[j] + u
                        mm = nc.tensor.matmul(p_dyn[:P, 0:3 * C0], turned[:, j % R, u, :],
                                              g.xparts[:, d, :, :].rearrange("p k c -> p (k c)"), start=(d == 0),
                                              stop=(d == T - 1))
                    mm.then_inc(spread, 1)

                def whole(s, first=False):
                    for j in range(NG):
                        n = s * NG + j
                        products(s, j, n, first)
                        if j == 0 and not first:
                            spread_group(NG - 1, n - 1, None)
                        elif j > 0:
                            spread_group(j - 1, n - 1, s if j == 1 and not first else None)

                whole(0, first=True)
                with pe.Fori(1, T) as s:
                    whole(s)
                spread_group(NG - 1, T * NG - 1, None)

F = D // 128
QUADS = [(t, min(4, T - t)) for t in range(0, T, 4)]


def turn_tiles(nc, pe, rows, width, psum, ident, wait_free, turned):
    n = 0
    for t0, k in QUADS:
        for lo in range(0, width, 128):
            m = min(128, width - lo)
            if n >= len(psum):
                pe.wait_ge(wait_free, n - len(psum) + 1)
            for u in range(k):
                mm = nc.tensor.transpose(psum[n % len(psum)][0:m, u * P:(u + 1) * P], rows[:, t0 + u, lo:lo + m],
                                         ident[0:P, 0:P])
            mm.then_inc(turned, 1)
            n += 1


def static_degrees(nc, g):
    with stage(nc) as (ctx, sem):
        sb = lambda n, s, d: ctx.enter_context(nc.sbuf_tensor(unique(n), s, d))
        rooted, tmp = sb("rooted_s", [P, T], F32), sb("tmp_s", [P, T], F32)
        loaded, deg_ready, root_done, dve_step = sem("loaded_s"), sem("deg_ready"), sem("root_done_s"), sem("dve_step_s")
        with nc.Block() as block:
            @block.sync
            def _(sp):
                sp.dma_start(g.h[:], g.xn.rearrange("(t p) d -> p t d", p=P)[:, :, 0:C0]).then_inc(loaded, 16)
                sp.dma_start(g.w_static[:], g.L0_gnn_W_static.rearrange("k i o -> i k o")).then_inc(loaded, 16)
                sp.dma_start(g.b_static[:], g.L0_gnn_b_static[None, :, :].to_broadcast([P, 3, C0])).then_inc(loaded, 16)
                sp.wait_ge(loaded, 48)

            @block.scalar
            def _(act):
                root(nc, act, g.dinv_s[:], rooted[:], deg_ready, root_done)

            @block.vector
            def _(dve):
                step = Step(dve, dve_step)
                nc.vector.tensor_scalar(g.dinv_s[:], g.deg[:, :, 0], 1.0, 1e-12, ALU.add, ALU.max).then_inc(deg_ready, 1)
                inverse_root(nc, dve, step, g.dinv_s[:], rooted[:], tmp[:], root_done)


def static_messages(nc, g, i):
    with stage(nc) as (ctx, sem):
        sb = lambda n, s, d: ctx.enter_context(nc.sbuf_tensor(unique(n), s, d))
        ps = lambda n: ctx.enter_context(nc.psum_tensor(unique(n), [128, 512], F32))
        hT = sb("hT", [C0, 2, 4 * P], F32)
        scaled = sb("scaled", [P, T, C0], F32)
        p_turn, p_mul = [ps(f"p_turn{b}") for b in range(2)], [ps(f"p_mul{b}") for b in range(2)]
        turned, turn_read, multiplied, mul_read = sem("turned_s"), sem("turn_read"), sem("multiplied"), sem("mul_read")
        dve_step = sem("dve_step_s")
        NQ = len(QUADS)

        with nc.Block() as block:
            @block.scalar
            def _(act):
                for q, (t0, k) in enumerate(QUADS):
                    act.wait_ge(turned, q + 1)
                    if q >= 2:
                        act.wait_ge(multiplied, q - 1)
                    nc.scalar.copy(hT[:, q % 2, 0:k * P], p_turn[q % 2][0:C0, 0:k * P]).then_inc(turn_read, 1)

            @block.tensor
            def _(pe):
                def turn(q):
                    t0, k = QUADS[q]
                    if q >= 2:
                        pe.wait_ge(turn_read, q - 1)
                    for u in range(k):
                        mm = nc.tensor.transpose(p_turn[q % 2][0:C0, u * P:(u + 1) * P], g.h[:, t0 + u, :],
                                                 g.ident[0:P, 0:P])
                    mm.then_inc(turned, 1)

                def multiply(q):
                    t0, k = QUADS[q]
                    pe.wait_ge(turn_read, q + 1)
                    if q >= 2:
                        pe.wait_ge(mul_read, q - 1)
                    for u in range(k):
                        mm = nc.tensor.matmul(p_mul[q % 2][0:P, u * C0:(u + 1) * C0], hT[:, q % 2, u * P:(u + 1) * P],
                                              g.w_static[:, i, :], start=True, stop=True)
                    mm.then_inc(multiplied, 1)

                turn(0)
                for q in range(NQ):
                    if q + 1 < NQ:
                        turn(q + 1)
                    multiply(q)

            @block.vector
            def _(dve):
                step = Step(dve, dve_step)
                for q, (t0, k) in enumerate(QUADS):
                    dve.wait_ge(multiplied, q + 1)
                    nc.vector.tensor_tensor(
                        scaled[:, t0:t0 + k, :], p_mul[q % 2][0:P, 0:k * C0].rearrange("p (u c) -> p u c", u=k),
                        g.dinv_s[:, t0:t0 + k, None].to_broadcast([P, k, C0]), ALU.mult).then_inc(mul_read, 1)
                dve.wait_ge(mul_read, NQ)
                split3(nc, step, scaled[:], lambda k: g.parts[:, :, k, :], g.own[:])
                step(nc.vector.tensor_tensor(g.own[:], scaled[:], g.dinv_s[:, :, None].to_broadcast([P, T, C0]),
                                             ALU.mult))
                step(nc.vector.tensor_tensor(g.own[:], g.own[:], g.b_static[:, i:i + 1, :].to_broadcast([P, T, C0]),
                                             ALU.add))


def static_sums(nc, g):
    with stage(nc) as (ctx, sem):
        summed = ctx.enter_context(nc.sbuf_tensor(unique("summed"), [P, 2, 2, C0], F32))
        p_agg = [ctx.enter_context(nc.psum_tensor(unique(f"p_agg{b}"), [128, 512], F32)) for b in range(2)]
        aggregated, agg_read, before_relu, h_ready = sem("aggregated"), sem("agg_read"), sem("before_relu"), sem("h_ready")

        with nc.Block() as block:
            @block.tensor
            def _(pe):
                def aggregate(d, b):
                    for s in range(T):
                        mm = nc.tensor.matmul(p_agg[b][0:P, 0:3 * C0], g.counts[:, s, bass.ds(d * P, P)],
                                              g.parts[:, s, :, :].rearrange("p k c -> p (k c)"),
                                              start=(s == 0), stop=(s == T - 1))
                    mm.then_inc(aggregated, 1)

                aggregate(0, 0)
                aggregate(1, 1)
                with pe.Fori(1, T // 2) as m:
                    for b in range(2):
                        pe.wait_ge(agg_read, m * 2 + b - 1)
                        aggregate(m * 2 + b, b)
                pe.wait_ge(agg_read, T - 2)
                aggregate(T - 1, 0)

            @block.vector
            def _(dve):
                def update(d, b):
                    row = lambda a: a[:, bass.ds(d, 1), :].rearrange("p a c -> p (a c)")
                    dve.wait_ge(aggregated, d + 1)
                    nc.vector.tensor_reduce(summed[:, b, 0, :],
                                            p_agg[b][0:P, 0:3 * C0].rearrange("p (k c) -> p c k", k=3), AX.X,
                                            ALU.add).then_inc(agg_read, 1)
                    dve.wait_ge(agg_read, d + 1)
                    nc.vector.scalar_tensor_tensor(out=summed[:, b, 1, :], in0=summed[:, b, 0, :],
                                                   scalar=g.dinv_s[:, bass.ds(d, 1)], in1=row(g.own), op0=ALU.mult,
                                                   op1=ALU.add).then_inc(before_relu, 1)
                    dve.wait_ge(before_relu, d + 1)
                    nc.vector.tensor_scalar_max(row(g.h), summed[:, b, 1, :], 0.0).then_inc(h_ready, 1)

                with dve.Fori(0, T // 2) as m:
                    for b in range(2):
                        update(m * 2 + b, b)
                update(T - 1, 0)
                dve.wait_ge(h_ready, T)


def first_gnn_out(nc, g):
    with stage(nc) as (ctx, sem):
        sb = lambda n, s, d: ctx.enter_context(nc.sbuf_tensor(unique(n), s, d))
        ps = lambda n: ctx.enter_context(nc.psum_tensor(unique(n), [128, 512], F32))
        xn, xT = sb("xn_g", [P, T, D], F32), sb("xT_g", [128, F, N], F32)
        HID = 128
        hid = sb("hid_g", [HID, N], F32)
        x = g.xr
        w1, w2, wa = sb("w1_g", [128, F, HID], F32), sb("w2_g", [HID, C0], F32), sb("wa_g", [128, F, D], F32)
        b1, b2, ba = sb("b1_g", [HID, 1], F32), sb("b2_g", [P, C0], F32), sb("ba_g", [P, D], F32)
        factor = sb("factor_g", [P, T, C0], F32)
        psum = [ps(f"p_g{b}") for b in range(8)]
        loaded, x_in, w_in = sem("xn_in_g"), sem("x_in_g"), sem("w_in_g")
        turned, turn_read = sem("turned_g"), sem("turn_read_g")
        hid_done, hid_ready = sem("hid_done"), sem("hid_ready")
        ew_done, ew_read, dve_step = sem("ew_done"), sem("ew_read"), sem("dve_step_g")
        summed_ready, turned2, turn2_read = sem("summed_ready"), sem("turned2_g"), sem("turn2_read_g")
        out_done, out_read = sem("out_done_g"), sem("out_read_g")
        NQ = len(QUADS)
        PAIRS = [(t, min(2, T - t)) for t in range(0, T, 2)]

        with nc.Block() as block:
            @block.sync
            def _(sp):
                sp.dma_start(xn[:], g.xn.rearrange("(t p) d -> p t d", p=P)).then_inc(loaded, 16)
                sp.dma_start(w1[:], g.L0_gnn_W1.rearrange("(f i) o -> i f o", i=128)).then_inc(w_in, 16)
                sp.dma_start(b1[:], g.L0_gnn_b1[:, None]).then_inc(w_in, 16)
                sp.dma_start(w2[:], g.L0_gnn_W2).then_inc(w_in, 16)
                sp.dma_start(b2[:], g.L0_gnn_b2[None, :].to_broadcast([P, C0])).then_inc(w_in, 16)
                sp.dma_start(wa[:], g.L0_gnn_W_aggr.rearrange("(f i) o -> i f o", i=128)).then_inc(w_in, 16)
                sp.dma_start(ba[:], g.L0_gnn_b_aggr[None, :].to_broadcast([P, D])).then_inc(w_in, 16)
                sp.dma_start(x[:], g.x.rearrange("(t p) d -> p t d", p=P)).then_inc(x_in, 16)

            @block.tensor
            def _(pe):
                pe.wait_ge(loaded, 16)
                turn_tiles(nc, pe, xn, D, psum[0:4], g.ident, turn_read, turned)
                pe.wait_ge(w_in, 96)
                for q, (t0, k) in enumerate(QUADS):
                    cols = slice(t0 * P, (t0 + k) * P)
                    pe.wait_ge(turn_read, 2 * q + 2)
                    if q >= 2:
                        pe.wait_ge(hid_ready, q - 1)
                    for f in range(F):
                        mm = nc.tensor.matmul(psum[4 + q % 2][0:HID, 0:k * P], w1[:, f, :], xT[:, f, cols],
                                              start=(f == 0), stop=(f == F - 1))
                    mm.then_inc(hid_done, 1)
                for q, (t0, k) in enumerate(QUADS):
                    pe.wait_ge(hid_ready, q + 1)
                    if q >= 2:
                        pe.wait_ge(ew_read, q - 1)
                    for u in range(k):
                        mm = nc.tensor.matmul(psum[6 + q % 2][0:P, u * C0:(u + 1) * C0],
                                              hid[:, (t0 + u) * P:(t0 + u + 1) * P], w2[:], start=True, stop=True)
                    mm.then_inc(ew_done, 1)
                pe.wait_ge(summed_ready, 1)
                turn_tiles(nc, pe, g.h, C0, psum[0:2], g.ident, turn2_read, turned2)
                pe.wait_ge(turn2_read, NQ)
                for n, (t0, k) in enumerate(PAIRS):
                    if n >= 4:
                        pe.wait_ge(out_read, n - 3)
                    for u in range(k):
                        for f in range(F):
                            mm = nc.tensor.matmul(psum[2 + n % 4][0:P, u * D:(u + 1) * D],
                                                  xT[:, f, (t0 + u) * P:(t0 + u + 1) * P], wa[:, f, :],
                                                  start=(f == 0), stop=(f == F - 1))
                    mm.then_inc(out_done, 1)

            @block.scalar
            def _(act):
                n = 0
                for t0, k in QUADS:
                    for f in range(F):
                        act.wait_ge(turned, n + 1)
                        nc.scalar.copy(xT[:, f, t0 * P:(t0 + k) * P], psum[n % 4][:, 0:k * P]).then_inc(turn_read, 1)
                        n += 1
                act.wait_ge(w_in, 96)
                for q, (t0, k) in enumerate(QUADS):
                    act.wait_ge(hid_done, q + 1)
                    nc.scalar.activation(hid[:, t0 * P:(t0 + k) * P], psum[4 + q % 2][0:HID, 0:k * P], ACT.Gelu,
                                         bias=b1[:, 0:1]).then_inc(hid_ready, 1)
                for q, (t0, k) in enumerate(QUADS):
                    act.wait_ge(turned2, q + 1)
                    nc.scalar.copy(xT[0:C0, 0, t0 * P:(t0 + k) * P], psum[q % 2][0:C0, 0:k * P]).then_inc(turn2_read, 1)

            @block.vector
            def _(dve):
                step = Step(dve, dve_step)
                dve.wait_ge(w_in, 96)
                for q, (t0, k) in enumerate(QUADS):
                    dve.wait_ge(ew_done, q + 1)
                    nc.vector.tensor_tensor(factor[:, t0:t0 + k, :],
                                            psum[6 + q % 2][0:P, 0:k * C0].rearrange("p (u c) -> p u c", u=k),
                                            b2[:, None, :].to_broadcast([P, k, C0]), ALU.add).then_inc(ew_read, 1)
                dve.wait_ge(ew_read, NQ)
                step(nc.vector.tensor_tensor(factor[:], factor[:], g.dyn[:], ALU.mult))
                nc.vector.tensor_tensor(g.h[:], g.h[:], factor[:], ALU.add).then_inc(summed_ready, 1)
                dve.wait_ge(x_in, 16)
                step(nc.vector.tensor_tensor(x[:], x[:], ba[:, None, :].to_broadcast([P, T, D]), ALU.add))
                for n, (t0, k) in enumerate(PAIRS):
                    dve.wait_ge(out_done, n + 1)
                    nc.vector.tensor_tensor(x[:, t0:t0 + k, :],
                                            psum[2 + n % 4][0:P, 0:k * D].rearrange("p (u c) -> p u c", u=k),
                                            x[:, t0:t0 + k, :], ALU.add).then_inc(out_read, 1)


def count_rounds(nc, g):
    with stage(nc) as (ctx, sem):
        sb = lambda n, s, d: ctx.enter_context(nc.sbuf_tensor(unique(n), s, d))
        most, row, one = sb("most", [P, 1], F32), sb("row_x", [1, P], F32), sb("one_x", [1, 2], F32)
        p_row = ctx.enter_context(nc.psum_tensor(unique("p_row_x"), [128, 512], F32))
        step_x, most_ready, row_done = sem("step_x"), sem("most_ready"), sem("row_done")
        with nc.Block() as block:
            @block.vector
            def _(dve):
                step = Step(dve, step_x)
                V = nc.vector
                V.tensor_reduce(most[:], g.ranks[:], AX.X, ALU.max).then_inc(most_ready, 1)
                dve.wait_ge(row_done, 1)
                step(V.tensor_reduce(one[:, 0:1], p_row[0:1, 0:P], AX.X, ALU.max))
                step(V.tensor_scalar(one[:, 1:2], one[:, 0:1], 1.0 / P, -(P // 2) / P, ALU.mult, ALU.add))
                step(V.tensor_scalar_add(one[:, 0:1], one[:, 1:2], ROUND))
                step(V.tensor_scalar_add(one[:, 1:2], one[:, 0:1], -ROUND))
                step(V.tensor_scalar_add(g.rounds[:], one[:, 1:2], 1.0))
                step(V.memset(g.offset[:], 0.0))

            @block.tensor
            def _(pe):
                pe.wait_ge(most_ready, 1)
                nc.tensor.transpose(p_row[0:1, 0:P], most[:], g.ident[0:P, 0:P]).then_inc(row_done, 1)


def clear_high(nc, g):
    with stage(nc) as (ctx, sem):
        zero = ctx.enter_context(nc.sbuf_tensor(unique("zero_h"), [P, N], BF16))
        zeroed, stored = sem("zeroed_h"), sem("stored_h")
        with nc.Block() as block:
            @block.vector
            def _(dve):
                nc.vector.memset(zero[:], 0.0).then_inc(zeroed, 1)

            @block.sync
            def _(sp):
                sp.wait_ge(zeroed, 1)
                for t in range(T):
                    sp.dma_start(g.high[t * P:(t + 1) * P, :], zero[:]).then_inc(stored, 16)
                sp.wait_ge(stored, 16 * T)


def scatter_again(nc, g):
    with stage(nc) as (ctx, sem):
        sb = lambda n, s, d: ctx.enter_context(nc.sbuf_tensor(unique(n), s, d))
        rec, keyp, rank = sb("rec_x", [P, EC, 2], F32), sb("keyp_x", [P, EC], F32), sb("rank_x", [P, EC], F32)
        low, at = sb("low_x", [P, EC], F32), sb("at_x", [P, EC], U32)
        blank = sb("blank_x", [P, NB, 2], F32)
        idx, staged = sb("idx_x", [P, 4], U32), sb("staged_x", [P, 4, 2], F32)
        edges_in, blanked, blank_out, step_x = sem("edges_in_x"), sem("blanked_x"), sem("blank_out_x"), sem("step_y")
        at_ready, four_ready, four_out, go = sem("at_ready"), sem("four_ready"), sem("four_out"), sem("go_x")
        with nc.Block() as block:
            @block.sync
            def _(sp):
                sp.dma_start(rec[:].rearrange("p t k -> p (t k)"), g.edge_rec).then_inc(edges_in, 16)
                sp.dma_start(keyp[:], g.edge_key).then_inc(edges_in, 16)
                sp.dma_start(rank[:], g.edge_rank).then_inc(edges_in, 16)
                sp.wait_ge(blanked, 2)
                sp.dma_start(g.slots.rearrange("(p n) k -> p (n k)", p=P),
                             blank[:].rearrange("p n k -> p (n k)")).then_inc(blank_out, 16)

            @block.vector
            def _(dve):
                step = Step(dve, step_x)
                V = nc.vector
                V.memset(blank[:, :, 0], 0.0).then_inc(blanked, 1)
                V.memset(blank[:, :, 1], EMPTY).then_inc(blanked, 1)
                step(V.tensor_scalar_add(g.offset[:], g.offset[:], float(P)))
                dve.wait_ge(edges_in, 48)
                step(V.tensor_scalar(rank[:], rank[:], g.offset[:, 0:1], None, ALU.subtract))
                step(V.tensor_tensor(keyp[:], keyp[:], rank[:], ALU.add))
                step(V.tensor_scalar(low[:], rank[:], 0.0, PAST, ALU.is_lt, ALU.mult))
                step(V.tensor_tensor(keyp[:], keyp[:], low[:], ALU.add))
                step(V.tensor_scalar(low[:], rank[:], float(P), PAST, ALU.is_ge, ALU.mult))
                V.tensor_tensor(at[:], keyp[:], low[:], ALU.add).then_inc(at_ready, 1)
                dve.wait_ge(at_ready, 1)

                def four(i):
                    V.tensor_copy(idx[:], at[:, bass.ds(i * 4, 4)])
                    V.tensor_copy(staged[:], rec[:, bass.ds(i * 4, 4), :]).then_inc(four_ready, 1)

                four(0)
                with dve.Fori(1, EC // 4) as i:
                    dve.wait_ge(four_out, i * 64)
                    four(i)

            @block.gpsimd
            def _(pool):
                bound = pool.to_reg(NB * P - 1)
                pool.wait_ge(blank_out, 16)
                with pool.Fori(0, EC // 4) as i:
                    pool.wait_ge(four_ready, i + 1)
                    pool.sem_inc(go)
                    for u in range(4):
                        pool.indirect_dma_start(
                            out=g.slots, out_offset=bass.IndirectOffsetOnAxis(ap=idx[:, u:u + 1], axis=0),
                            in_=staged[:, u, :], in_offset=None, bounds_check=bound,
                            oob_is_err=False).then_inc(four_out, 16)
                pool.wait_ge(four_out, EC * 16)


def add_blocks(nc, g):
    with stage(nc) as (ctx, sem):
        sb = lambda n, s, d: ctx.enter_context(nc.sbuf_tensor(unique(n), s, d))
        ps = lambda n: ctx.enter_context(nc.psum_tensor(unique(n), [P, 512], F32))
        src16, dst16, turned = sb("src16_x", [P, P], BF16), sb("dst16_x", [P, P], BF16), sb("turned_x", [P, P], BF16)
        src32, dst32 = sb("src32_x", [P, P], F32), sb("dst32_x", [P, P], F32)
        weight, high = sb("weight_x", [P, P], F32), sb("high_x", [P, P], BF16)
        lane, xrow = sb("lane_x", [P, 3], F32), sb("xrow_x", [P, 3 * C0], BF16)
        degs = sb("degs_x", [P, 4], BF16)
        v, carry = sb("v_x", [P, P], F32), sb("carry_x", [P, P], F32)
        p_w, p_c, p_t, p_deg, p_dyn = ps("p_w_x"), ps("p_c_x"), ps("p_t_x"), ps("p_deg_x"), ps("p_dyn_x")
        read, held, hot, product = sem("read_x"), sem("held_x"), sem("hot_x"), sem("product_x")
        turned_ready, dyn_done, updated, stored, chain = (
            sem(k) for k in ("turned_ready_x", "dyn_done_x", "updated_x", "stored_x", "chain_x"))
        CHAIN = 9

        def buckets(engine, body):
            with engine.Fori(0, T) as s:
                with engine.Fori(0, T) as d:
                    body(s, d, s * T + d)

        with nc.Block() as block:
            @block.sync
            def _(sp):
                def body(s, d, n):
                    at = bass.ds(s * P, P), bass.ds(d * P, P)
                    sp.dma_start(weight[:], g.weights[at[0], at[1]]).then_inc(read, 16)
                    sp.dma_start(high[:], g.high[at[0], at[1]]).then_inc(read, 16)
                    sp.wait_ge(updated, n + 1)
                    sp.sem_inc(held)
                    sp.dma_start(g.weights[at[0], at[1]], weight[:]).then_inc(stored, 16)
                    sp.dma_start(g.high[at[0], at[1]], high[:]).then_inc(stored, 16)
                    sp.wait_ge(stored, (n + 1) * 32)
                    sp.sem_inc(held)
                buckets(sp, body)

            @block.vector
            def _(dve):
                V = nc.vector
                flat = lambda a: a.rearrange("p a c -> p (a c)")

                def body(s, d, n):
                    c = [0]

                    def step(ins):
                        c[0] += 1
                        ins.then_inc(chain, 1)
                        dve.wait_ge(chain, n * CHAIN + c[0])

                    b = s * T + d
                    V.tensor_copy(lane[:, 0:2], g.slot_ids[:, :, bass.ds(b, 1)].rearrange("p a c -> p (a c)"))
                    V.tensor_copy(xrow[:], g.xparts[:, bass.ds(d, 1), :, :].rearrange("p a k c -> p (a k c)"))
                    V.tensor_copy(degs[:], flat(g.slot_deg[:, bass.ds(b, 1), :]))
                    step(V.tensor_reduce(lane[:, 2:3], g.slot_deg[:, bass.ds(b, 1), 1:4].rearrange("p a k -> p (a k)"),
                                         AX.X, ALU.add))
                    V.tensor_scalar(src16[:], g.iota[:P, 0:P], lane[:, 0:1], None, ALU.is_equal)
                    V.tensor_scalar(dst16[:], g.iota[:P, 0:P], lane[:, 1:2], None, ALU.is_equal)
                    V.tensor_scalar(src32[:], g.iota[:P, 0:P], lane[:, 0:1], None, ALU.is_equal)
                    V.tensor_scalar(dst32[:], g.iota[:P, 0:P], lane[:, 1:2], lane[:, 2:3], ALU.is_equal,
                                    ALU.mult).then_inc(hot, 1)
                    dve.wait_ge(product, n + 1)
                    V.tensor_copy(turned[:], p_t[:, 0:P]).then_inc(turned_ready, 1)
                    dve.wait_ge(read, (n + 1) * 32)
                    step(V.tensor_tensor(weight[:], weight[:], p_w[:, 0:P], ALU.add))
                    count = flat(g.counts[:, bass.ds(s, 1), bass.ds(d * P, P)])
                    step(V.tensor_tensor(v[:], count, p_c[:, 0:P], ALU.add))
                    step(V.tensor_scalar(carry[:], v[:], 256.0, None, ALU.is_ge))
                    step(V.scalar_tensor_tensor(out=count, in0=carry[:], scalar=-256.0, in1=v[:], op0=ALU.mult,
                                                op1=ALU.add))
                    step(V.tensor_tensor(high[:], high[:], carry[:], ALU.add))
                    degree = flat(g.deg[:, bass.ds(d, 1), :])
                    step(V.tensor_tensor(degree, degree, p_deg[:, 0:4], ALU.add))
                    dve.wait_ge(dyn_done, n + 1)
                    step(V.tensor_reduce(v[:, 0:C0], p_dyn[:, 0:3 * C0].rearrange("p (k c) -> p c k", k=3), AX.X, ALU.add))
                    row = flat(g.dyn[:, bass.ds(s, 1), :])
                    step(V.tensor_tensor(row, row, v[:, 0:C0], ALU.add))
                    assert c[0] == CHAIN
                    dve.sem_inc(updated)
                buckets(dve, body)

            @block.tensor
            def _(pe):
                def body(s, d, n):
                    pe.wait_ge(hot, n + 1)
                    nc.tensor.matmul(p_w[:, 0:P], src32[:], dst32[:], start=True, stop=True)
                    nc.tensor.matmul(p_c[:, 0:P], src16[:], dst16[:], start=True, stop=True)
                    nc.tensor.matmul(p_t[:, 0:P], dst16[:], src16[:], start=True, stop=True)
                    nc.tensor.matmul(p_deg[:, 0:4], dst16[:], degs[:], start=True, stop=True).then_inc(product, 1)
                    pe.wait_ge(turned_ready, n + 1)
                    nc.tensor.matmul(p_dyn[:, 0:3 * C0], turned[:], xrow[:], start=True, stop=True).then_inc(dyn_done, 1)
                buckets(pe, body)


def further_rounds(nc, g):
    rounds = nc.values_load(g.rounds[0:1, 0:1], min_val=1, max_val=E // P)
    with nc.If(rounds > 1):
        nc.all_engine_barrier()
        clear_high(nc, g)
        with nc.Fori(1, rounds):
            nc.all_engine_barrier()
            scatter_again(nc, g)
            load_slots(nc, g)
            add_blocks(nc, g)


def add_high_counts(nc, g):
    rounds = nc.values_load(g.rounds[0:1, 0:1], min_val=1, max_val=E // P)
    with nc.If(rounds > 1):
        nc.all_engine_barrier()
        with stage(nc) as (ctx, sem):
            high = ctx.enter_context(nc.sbuf_tensor(unique("high_y"), [P, P], BF16))
            part = ctx.enter_context(nc.sbuf_tensor(unique("part_y"), [P, 3 * C0], BF16))
            v = ctx.enter_context(nc.sbuf_tensor(unique("v_y"), [P, C0], F32))
            total = ctx.enter_context(nc.psum_tensor(unique("total_y"), [P, 512], F32))
            read, taken, summed, used, chain, held = sem("read_y"), sem("taken_y"), sem("summed_y"), sem("used_y"), sem("chain_y"), sem("held_y")

            def blocks(engine, body):
                with engine.Fori(0, T) as d:
                    with engine.Fori(0, T) as s:
                        body(s, d, d * T + s)

            with nc.Block() as block:
                @block.sync
                def _(sp):
                    def body(s, d, n):
                        sp.dma_start(high[:], g.high[bass.ds(s * P, P), bass.ds(d * P, P)]).then_inc(read, 16)
                        sp.wait_ge(used, n + 1)
                        sp.sem_inc(held)
                    blocks(sp, body)

                @block.tensor
                def _(pe):
                    def body(s, d, n):
                        pe.wait_ge(read, (n + 1) * 16)
                        pe.wait_ge(taken, n + 1)
                        nc.tensor.matmul(total[:, 0:3 * C0], high[:], part[:], start=True, stop=True).then_inc(summed, 1)
                    blocks(pe, body)

                @block.vector
                def _(dve):
                    V = nc.vector

                    def body(s, d, n):
                        V.tensor_copy(part[:], g.parts[:, bass.ds(s, 1), :, :].rearrange("p a k c -> p (a k c)")
                                      ).then_inc(taken, 1)
                        dve.wait_ge(summed, n + 1)
                        V.tensor_reduce(v[:], total[:, 0:3 * C0].rearrange("p (k c) -> p c k", k=3), AX.X,
                                        ALU.add).then_inc(chain, 1)
                        dve.wait_ge(chain, n * 3 + 1)
                        V.tensor_scalar(v[:], v[:], g.dinv_s[:, bass.ds(d, 1)], 256.0, ALU.mult, ALU.mult).then_inc(chain, 1)
                        dve.wait_ge(chain, n * 3 + 2)
                        row = g.own[:, bass.ds(d, 1), :].rearrange("p a c -> p (a c)")
                        V.tensor_tensor(row, row, v[:], ALU.add).then_inc(chain, 1)
                        dve.wait_ge(chain, n * 3 + 3)
                        dve.sem_inc(used)
                    blocks(dve, body)

NE = 8
CAP = -(-5 * N // (4 * NE))
CT = -(-CAP // P)
CP = CT * P
F1 = 1024
LARGEST = 1e4


def route_first(nc, g):
    with stage(nc) as (ctx, sem):
        sb = lambda n, s, d: ctx.enter_context(nc.sbuf_tensor(unique(n), s, d))
        ps = lambda n: ctx.enter_context(nc.psum_tensor(unique(n), [128, 512], F32))
        xn, xT = sb("xn_r", [P, T, D], F32), sb("xT_r", [128, F, N], F32)
        stats, small = sb("stats_r", [P, T, 6], F32), sb("small_r", [P, 4, T], F32)
        zero = sb("zero_r", [P, 1, D], F32)
        gate, gate_b = sb("gate_r", [128, F, NE], F32), sb("gate_b_r", [P, NE], F32)
        tri = sb("tri_r", [P, P], F32)
        number, rev = sb("number_r", [P, NE], F32), sb("rev_r", [P, NE], F32)
        logits, a, b = sb("logits_r", [P, T, NE], F32), sb("a_r", [P, T, NE], F32), sb("b_r", [P, T, NE], F32)
        hot, totals = sb("hot_r", [P, T, NE], F32), sb("totals_r", [P, 2, T, NE], F32)
        top, total, place, kept = (sb(f"{k}_r", [P, T], F32) for k in ("top", "total", "place", "kept"))
        where = sb("where_r", [P, T], F32)
        scatter_at = sb("scatter_at_r", [P, T], U32)
        psum = [ps(f"p_r{k}") for k in range(4)]
        p_gate, p_count, p_total = ps("p_gate"), ps("p_count"), ps("p_total")
        cleared, clear_out, w_in = sem("cleared_r"), sem("clear_out_r"), sem("w_in_r")
        rows_done, var_ready, root_done = sem("rows_done_r"), sem("var_ready_r"), sem("root_done_r")
        xn_ready, dve_step = sem("xn_ready_r"), sem("dve_step_r")
        turned, turn_read, gated = sem("turned_r"), sem("turn_read_r"), sem("gated_r")
        exp_asked, exp_done, hot_ready, counted = sem("exp_asked"), sem("exp_done"), sem("hot_ready_r"), sem("counted_r")
        places_ready, consts, scattered = sem("places_ready"), sem("consts_r"), sem("scattered_r")

        with nc.Block() as block:
            @block.sync
            def _(sp):
                sp.dma_start(gate[:], g.L0_ffn_gate_w.rearrange("(f i) e -> i f e", i=128)).then_inc(w_in, 16)
                sp.dma_start(gate_b[:], g.L0_ffn_gate_b[None, :].to_broadcast([P, NE])).then_inc(w_in, 16)
                sp.wait_ge(cleared, 1)
                sp.dma_start(g.placed.rearrange("(p n) d -> p n d", p=P),
                             zero[:].to_broadcast([P, NE * CP // P, D])).then_inc(clear_out, 16)

            @block.gpsimd
            def _(pool):
                pool.memset(zero[:], 0.0).then_inc(cleared, 1)
                pool.iota(number[:], pattern=[[1, NE]], base=0, channel_multiplier=0,
                          allow_small_or_imprecise_dtypes=True).then_inc(consts, 1)
                pool.iota(rev[:], pattern=[[-1, NE]], base=NE, channel_multiplier=0,
                          allow_small_or_imprecise_dtypes=True).then_inc(consts, 1)
                pool.affine_select(out=tri[:], in_=g.ones[0:P, 0:P], compare_op=ALU.is_gt, fill=0.0, base=0,
                                   pattern=[[1, P]], channel_multiplier=-1).then_inc(consts, 1)
                bound = pool.to_reg(NE * CP - 1)
                pool.wait_ge(clear_out, 16)
                pool.wait_ge(places_ready, 1)
                for t in range(T):
                    pool.indirect_dma_start(
                        out=g.placed, out_offset=bass.IndirectOffsetOnAxis(ap=scatter_at[:, t:t + 1], axis=0),
                        in_=xn[:, t, :], in_offset=None, bounds_check=bound, oob_is_err=False).then_inc(scattered, 16)
                pool.wait_ge(scattered, 16 * T)

            @block.scalar
            def _(act):
                root(nc, act, small[:, 1, :], small[:, 3, :], var_ready, root_done)
                n = 0
                for t0, k in QUADS:
                    for f in range(F):
                        act.wait_ge(turned, n + 1)
                        nc.scalar.copy(xT[:, f, t0 * P:(t0 + k) * P], psum[n % 4][:, 0:k * P]).then_inc(turn_read, 1)
                        n += 1
                act.wait_ge(exp_asked, 1)
                nc.scalar.activation(b[:], a[:], ACT.Exp).then_inc(exp_done, 1)

            @block.tensor
            def _(pe):
                pe.wait_ge(xn_ready, 1)
                turn_tiles(nc, pe, xn, D, psum, g.ident, turn_read, turned)
                pe.wait_ge(w_in, 32)
                pe.wait_ge(turn_read, F * len(QUADS))
                for t in range(T):
                    for f in range(F):
                        mm = nc.tensor.matmul(p_gate[0:P, t * NE:(t + 1) * NE], xT[:, f, t * P:(t + 1) * P],
                                              gate[:, f, :], start=(f == 0), stop=(f == F - 1))
                mm.then_inc(gated, 1)
                pe.wait_ge(hot_ready, 1)
                pe.wait_ge(consts, 3)
                flat = hot[:].rearrange("p t e -> p (t e)")
                nc.tensor.matmul(p_total[0:P, 0:T * NE], g.ones[0:P, 0:P], flat, start=True, stop=True).then_inc(counted, 1)
                nc.tensor.matmul(p_count[0:P, 0:T * NE], tri[:], flat, start=True, stop=True).then_inc(counted, 1)

            @block.vector
            def _(dve):
                step = Step(dve, dve_step)
                bc = lambda v: v[:, :, None].to_broadcast([P, T, NE])
                layer_norm(nc, dve, step, g.xr, xn, stats, small, rows_done, var_ready, root_done)
                dve.sem_inc(xn_ready)
                dve.wait_ge(gated, 1)
                dve.wait_ge(w_in, 32)
                dve.wait_ge(consts, 3)
                V = nc.vector
                step(V.tensor_tensor(logits[:], p_gate[0:P, 0:T * NE].rearrange("p (t e) -> p t e", e=NE),
                                     gate_b[:, None, :].to_broadcast([P, T, NE]), ALU.add))
                step(V.tensor_reduce(top[:], logits[:], AX.X, ALU.max))
                V.tensor_tensor(a[:], logits[:], bc(top), ALU.subtract).then_inc(exp_asked, 1)
                step(V.tensor_tensor(hot[:], logits[:], bc(top), ALU.is_equal))
                step(V.tensor_tensor(hot[:], hot[:], rev[:, None, :].to_broadcast([P, T, NE]), ALU.mult))
                step(V.tensor_reduce(top[:], hot[:], AX.X, ALU.max))
                step(V.tensor_tensor(hot[:], hot[:], bc(top), ALU.is_equal))
                dve.sem_inc(hot_ready)
                dve.wait_ge(exp_done, 1)
                step(V.tensor_reduce(total[:], b[:], AX.X, ALU.add))
                step(V.reciprocal(g.chance[:], total[:]))
                step(V.tensor_scalar(top[:], top[:], -float(CP), float(NE * CP), ALU.mult, ALU.add))
                dve.wait_ge(counted, 2)
                step(V.tensor_copy(totals[:, 0], p_total[0:P, 0:T * NE].rearrange("p (t e) -> p t e", e=NE)))
                now, hop = 0, 1
                while hop < T:
                    step(V.tensor_copy(totals[:, 1 - now, 0:hop, :], totals[:, now, 0:hop, :]))
                    step(V.tensor_tensor(totals[:, 1 - now, hop:T, :], totals[:, now, hop:T, :],
                                         totals[:, now, 0:T - hop, :], ALU.add))
                    now, hop = 1 - now, hop * 2
                step(V.tensor_tensor(a[:], totals[:, now], p_total[0:P, 0:T * NE].rearrange("p (t e) -> p t e", e=NE),
                                     ALU.subtract))
                step(V.tensor_tensor(a[:], a[:], p_count[0:P, 0:T * NE].rearrange("p (t e) -> p t e", e=NE), ALU.add))
                step(V.tensor_tensor(a[:], a[:], hot[:], ALU.mult))
                step(V.tensor_reduce(place[:], a[:], AX.X, ALU.add))
                step(V.tensor_scalar(kept[:], place[:], float(CAP), None, ALU.is_lt))
                step(V.tensor_tensor(g.chance[:], g.chance[:], kept[:], ALU.mult))
                step(V.tensor_scalar(kept[:], kept[:], -PAST, PAST, ALU.mult, ALU.add))
                step(V.tensor_tensor(where[:], top[:], place[:], ALU.add))
                step(V.tensor_tensor(scatter_at[:], where[:], kept[:], ALU.add))
                step(V.tensor_scalar_min(place[:], place[:], float(CAP - 1)))
                step(V.tensor_tensor(g.gather_at[:], top[:], place[:], ALU.add))
                dve.sem_inc(places_ready)


def first_experts(nc, g):
    M1 = F1 // 128
    with stage(nc) as (ctx, sem):
        sb = lambda n, s, d: ctx.enter_context(nc.sbuf_tensor(unique(n), s, d))
        ps = lambda n: ctx.enter_context(nc.psum_tensor(unique(n), [128, 512], F32))
        rows = sb("rows_f", [P, 2, CT, D], F32)
        xT = sb("xT_f", [128, 2, F, CP], F32)
        w1, w2 = sb("w1_f", [128, 2, F, F1], F32), sb("w2_f", [128, 2, M1, D], F32)
        b1, b2 = sb("b1_f", [128, NE, M1], F32), sb("b2_f", [P, NE, D], F32)
        b1_rows = sb("b1_rows_f", [NE * M1, 128], F32)
        hid = sb("hid_f", [128, 2, M1, CP], F32)
        y = sb("y_f", [P, 2, CT, D], F32)
        p_turn = [ps(f"p_turn_f{k}") for k in range(2)]
        p_hid = [ps(f"p_hid_f{k}") for k in range(3)]
        p_out = [ps(f"p_out_f{k}") for k in range(2)]
        biases, rows_in = sem("biases_f"), [sem(f"rows_in_f{k}") for k in range(2)]
        w_in, y_out = [sem(f"w_in_f{k}") for k in range(2)], [sem(f"y_out_f{k}") for k in range(2)]
        turned, turn_read = sem("turned_f"), sem("turn_read_f")
        b1_turned, b1_ready = sem("b1_turned_f"), sem("b1_ready_f")
        hid_done, hid_ready = sem("hid_done_f"), sem("hid_ready_f")
        out_done, out_read = sem("out_done_f"), sem("out_read_f")

        with nc.Block() as block:
            @block.sync
            def _(sp):
                sp.dma_start(b1_rows[:], g.L0_ffn_b1.rearrange("e (m i) -> (e m) i", i=128)).then_inc(biases, 16)
                sp.dma_start(b2[:], g.L0_ffn_b2[None, :, :].to_broadcast([P, NE, D])).then_inc(biases, 16)
                for e in range(NE):
                    k = e % 2
                    if e >= 2:
                        sp.wait_ge(hid_done, (e - 1) * M1)
                    sp.dma_start(rows[:, k], g.placed[e * CP:(e + 1) * CP, :].rearrange("(u p) d -> p u d", p=P)
                                 ).then_inc(rows_in[k], 16)
                    sp.dma_start(w1[:, k], g.L0_ffn_w1[e].rearrange("(f i) o -> i f o", i=128)).then_inc(w_in[k], 16)
                    if e >= 2:
                        sp.wait_ge(out_done, (e - 1) * CT)
                    sp.dma_start(w2[:, k], g.L0_ffn_w2[e].rearrange("(m i) o -> i m o", i=128)).then_inc(w_in[k], 16)

            @block.gpsimd
            def _(pool):
                for e in range(NE):
                    pool.wait_ge(out_read, (e + 1) * CT)
                    pool.dma_start(g.results[e * CP:(e + 1) * CP, :].rearrange("(u p) d -> p u d", p=P),
                                   y[:, e % 2]).then_inc(y_out[e % 2], 16)
                for k in range(2):
                    pool.wait_ge(y_out[k], 16 * NE // 2)

            @block.tensor
            def _(pe):
                def turn(e):
                    k = e % 2
                    pe.wait_ge(rows_in[k], 16 * (e // 2 + 1))
                    for f in range(F):
                        n = e * F + f
                        if n >= 2:
                            pe.wait_ge(turn_read, n - 1)
                        for u in range(CT):
                            mm = nc.tensor.transpose(p_turn[f][:, u * P:(u + 1) * P],
                                                     rows[:, k, u, f * 128:(f + 1) * 128], g.ident[0:P, 0:P])
                        mm.then_inc(turned, 1)

                pe.wait_ge(biases, 32)
                nc.tensor.transpose(p_hid[0][:, 0:NE * M1], b1_rows[:], g.ident[0:NE * M1, 0:NE * M1]).then_inc(b1_turned, 1)
                turn(0)
                pe.wait_ge(b1_ready, 1)
                for e in range(NE):
                    k = e % 2
                    pe.wait_ge(turn_read, (e + 1) * F)
                    pe.wait_ge(w_in[k], 32 * (e // 2 + 1))
                    for m in range(M1):
                        n = e * M1 + m
                        if n >= 3:
                            pe.wait_ge(hid_ready, n - 2)
                        for f in range(F):
                            mm = nc.tensor.matmul(p_hid[n % 3][:, 0:CP], w1[:, k, f, m * 128:(m + 1) * 128],
                                                  xT[:, k, f, :], start=(f == 0), stop=(f == F - 1))
                        mm.then_inc(hid_done, 1)
                    if e + 1 < NE:
                        turn(e + 1)
                    pe.wait_ge(hid_ready, (e + 1) * M1)
                    for u in range(CT):
                        n = e * CT + u
                        if n >= 2:
                            pe.wait_ge(out_read, n - 1)
                        for m in range(M1):
                            mm = nc.tensor.matmul(p_out[n % 2][0:P, 0:D], hid[:, k, m, u * P:(u + 1) * P],
                                                  w2[:, k, m, :], start=(m == 0), stop=(m == M1 - 1))
                        mm.then_inc(out_done, 1)

            @block.scalar
            def _(act):
                act.wait_ge(b1_turned, 1)
                nc.scalar.copy(b1[:].rearrange("p e m -> p (e m)"), p_hid[0][:, 0:NE * M1]).then_inc(b1_ready, 1)
                act.wait_ge(b1_ready, 1)
                for e in range(NE):
                    k = e % 2
                    if e >= 2:
                        act.wait_ge(out_done, (e - 1) * CT)
                    for m in range(M1):
                        n = e * M1 + m
                        act.wait_ge(hid_done, n + 1)
                        nc.scalar.activation(hid[:, k, m, :], p_hid[n % 3][:, 0:CP], ACT.Relu,
                                             bias=b1[:, e, m:m + 1]).then_inc(hid_ready, 1)

            @block.vector
            def _(dve):
                dve.wait_ge(biases, 32)

                def take_turned(e):
                    k = e % 2
                    if e >= 2:
                        dve.wait_ge(hid_done, (e - 1) * M1)
                    for f in range(F):
                        dve.wait_ge(turned, e * F + f + 1)
                        nc.vector.tensor_copy(xT[:, k, f, :], p_turn[f][:, 0:CP]).then_inc(turn_read, 1)

                take_turned(0)
                for e in range(NE):
                    k = e % 2
                    if e + 1 < NE:
                        take_turned(e + 1)
                    if e >= 2:
                        dve.wait_ge(y_out[k], 16 * (e // 2))
                    for u in range(CT):
                        dve.wait_ge(out_done, e * CT + u + 1)
                        nc.vector.tensor_tensor(y[:, k, u, :], p_out[(e * CT + u) % 2][0:P, 0:D], b2[:, e, :],
                                                ALU.add).then_inc(out_read, 1)


def combine_first(nc, g):
    with stage(nc) as (ctx, sem):
        sb = lambda n, s, d: ctx.enter_context(nc.sbuf_tensor(unique(n), s, d))
        y = sb("y_c", [P, T, D], F32)
        z = sb("z_c", [P, T, D], F32)
        high, low = sb("high_c", [P, D], F32), sb("low_c", [P, D], F32)
        mask = sb("mask_c", [P, 2, 3, D], U32)
        gathered = [sem(f"gathered{k}") for k in range(5)]
        consts, scaled, masked, kept, added = sem("consts_c"), sem("scaled_c"), sem("masked_c"), sem("kept_c"), sem("added_c")

        with nc.Block() as block:
            @block.gpsimd
            def _(pool):
                pool.memset(high[:], LARGEST)
                pool.memset(low[:], -LARGEST)
                pool.memset(z[:], 0.0).then_inc(consts, 1)
                for t in range(T):
                    if t >= 5:
                        pool.wait_ge(gathered[t % 5], 16 * (t // 5))
                    pool.indirect_dma_start(
                        out=y[:, t, :], out_offset=None, in_=g.results,
                        in_offset=bass.IndirectOffsetOnAxis(ap=g.gather_at[:, t:t + 1], axis=0)
                    ).then_inc(gathered[t % 5], 16)

            @block.scalar
            def _(act):
                for t in range(T):
                    act.wait_ge(gathered[t % 5], 16 * (t // 5 + 1))
                    nc.scalar.activation(y[:, t, :], y[:, t, :], ACT.Copy, scale=g.chance[:, t:t + 1]).then_inc(scaled, 1)

            @block.vector
            def _(dve):
                V = nc.vector
                INF = float("inf")
                dve.wait_ge(consts, 1)
                for t in range(T):
                    k = t % 2
                    dve.wait_ge(scaled, t + 1)
                    if t >= 2:
                        dve.wait_ge(kept, 3 * (t - 1))
                    V.tensor_tensor(mask[:, k, 0, :], y[:, t, :], y[:, t, :], ALU.is_equal)
                    V.tensor_scalar(mask[:, k, 1, :], y[:, t, :], LIMIT, None, ALU.is_gt)
                    V.tensor_scalar(mask[:, k, 2, :], y[:, t, :], -LIMIT, None, ALU.is_lt).then_inc(masked, 1)
                    dve.wait_ge(masked, t + 1)
                    V.copy_predicated(z[:, t, :], mask[:, k, 0, :], y[:, t, :]).then_inc(kept, 1)
                    dve.wait_ge(kept, 3 * t + 1)
                    V.copy_predicated(z[:, t, :], mask[:, k, 1, :], high[:]).then_inc(kept, 1)
                    dve.wait_ge(kept, 3 * t + 2)
                    V.copy_predicated(z[:, t, :], mask[:, k, 2, :], low[:]).then_inc(kept, 1)
                    dve.wait_ge(kept, 3 * t + 3)
                    V.tensor_tensor(g.xr[:, t, :], g.xr[:, t, :], z[:, t, :], ALU.add).then_inc(added, 1)
                dve.wait_ge(added, T)


LIMIT = 3.4028234663852886e38

WINDOWS = [(0, [(0, 4), (4, 4), (8, 4), (12, 4)]), (16, [(16, 4), (20, 4), (24, 1)])]
PAIRS = [(t, min(2, T - t)) for t in range(0, T, 2)]


def second_gnn(nc, g):
    RING = 5
    with stage(nc) as (ctx, sem):
        sb = lambda n, s, d: ctx.enter_context(nc.sbuf_tensor(unique(n), s, d))
        msg = sb("msg_w", [P, T, D], F32)
        xT, outT = sb("xT_w", [128, F, N], F32), sb("outT_w", [128, F, N], F32)
        strips = sb("strips_w", [P, RING, 16 * P], F32)
        msg_now = sb("msg_now", [P, RING, D], F32)
        dinv_row = sb("dinv_row", [128, N], F32)
        stats, small = sb("stats_w", [P, T, 6], F32), sb("small_w", [P, 4, T], F32)
        dinv, rooted, tmp, mask = (sb(f"{k}_w", [P, T], F32) for k in ("dinv", "rooted", "tmp", "mask"))
        dinv_t = sb("dinv_t", [T, P], F32)
        w = [sb(f"w{i}_w", [128, F, D], F32) for i in range(2)]
        cols = sb("cols_w", [128, 4, F], F32)
        bn = sb("bn_w", [128, F, 7, 6], F32)
        agg = sb("agg_w", [128, F, 2], F32)
        norm = sb("norm_w", [128, 4, F], F32)
        bank = [ctx.enter_context(nc.psum_tensor(unique(f"bank_w{k}"), [128, 512], F32)) for k in range(8)]

        w_in, rows_done, var_ready, root_done = sem("w_in_w"), sem("rows_done_w"), sem("var_ready_w"), sem("root_done_w")
        dve_step, xn_ready, turned, turn_read = sem("dve_step_w"), sem("xn_ready_w"), sem("turned_w"), sem("turn_read_w")
        deg_ready, deg_rooted = sem("deg_ready_w"), sem("deg_rooted_w")
        dinv_ready, dinv_turned, dinv_read, dinv_out, row_in = (
            sem(k) for k in ("dinv_ready", "dinv_turned", "dinv_read", "dinv_out", "row_in"))
        multiplied, msg_ready = sem("multiplied_w"), sem("msg_ready")
        strip_in = [sem(f"strip_in{k}") for k in range(RING)]
        now_ready = sem("now_ready")
        strip_used, scaled, out_ready = sem("strip_used"), sem("scaled_w"), sem("out_ready_w")
        bn_ready, bn_rooted, norm_ready = sem("bn_ready"), sem("bn_rooted"), sem("norm_ready")
        mixed, final_ready, back, added = sem("mixed"), sem("final_ready"), sem("back"), sem("added_w")
        NQ, NP, NCH = len(QUADS), len(PAIRS), 7
        BIG = 2 * NCH

        with nc.Block() as block:
            @block.sync
            def _(sp):
                for i, name in enumerate((g.L1_gnn_W1, g.L1_gnn_W2)):
                    sp.dma_start(w[i][:], name.rearrange("(f i) o -> i f o", i=128)).then_inc(w_in, 16)
                for i, name in enumerate((g.L1_gnn_b1, g.L1_gnn_b2, g.L1_gnn_gamma, g.L1_gnn_beta)):
                    for f in range(F):
                        sp.dma_start(cols[:, i, f:f + 1], name[f * 128:(f + 1) * 128, None]).then_inc(w_in, 16)
                sp.wait_ge(dinv_read, 1)
                sp.dma_start(g.dinv.rearrange("(t p) -> t p", p=P), dinv_t[:]).then_inc(dinv_out, 16)
                sp.wait_ge(dinv_out, 16)
                sp.dma_start(dinv_row[:], g.dinv[None, :].to_broadcast([128, N])).then_inc(row_in, 16)
                for i in range(2):
                    for v, (first, chunks) in enumerate(WINDOWS):
                        lo, width = first * P, sum(k for _, k in chunks) * P
                        trip = (i * 2 + v) * (T // RING)

                        def load(m, fresh):
                            for r in range(RING):
                                s = m * RING + r
                                if not fresh:
                                    sp.wait_ge(strip_used, (m + trip - 1) * RING + r + 1)
                                sp.dma_start(strips[:, r, 0:width], g.weights[bass.ds(s * P, P), lo:lo + width]
                                             ).then_inc(strip_in[r], 16)

                        load(0, i == 0 and v == 0)
                        with sp.Fori(1, T // RING) as m:
                            load(m, False)

            @block.scalar
            def _(act):
                root(nc, act, dinv[:], rooted[:], deg_ready, deg_rooted)
                root(nc, act, small[:, 1, :], small[:, 3, :], var_ready, root_done)
                n = 0
                for t0, k in QUADS:
                    for f in range(F):
                        act.wait_ge(turned, n + 1)
                        nc.scalar.copy(xT[:, f, t0 * P:(t0 + k) * P], bank[n % 4][:, 0:k * P]).then_inc(turn_read, 1)
                        n += 1
                act.wait_ge(w_in, 160)
                for i, func in enumerate((ACT.Relu, ACT.Identity)):
                    n = 0
                    act.wait_ge(msg_ready, (i + 1) * NP)
                    for v, (_, chunks) in enumerate(WINDOWS):
                        trip = (i * 2 + v) * (T // RING)

                        def take(m, fresh):
                            for r in range(RING):
                                if not fresh:
                                    act.wait_ge(strip_used, (m + trip - 1) * RING + r + 1)
                                nc.scalar.copy(msg_now[:, r, :], msg[:, bass.ds(m * RING + r, 1), :].rearrange(
                                    "p a c -> p (a c)")).then_inc(now_ready, 1)

                        take(0, i == 0 and v == 0)
                        with act.Fori(1, T // RING) as m:
                            take(m, False)
                        for t0, k in chunks:
                            for f in range(F):
                                act.wait_ge(scaled, i * BIG + n + 1)
                                o = outT[:, f, t0 * P:(t0 + k) * P]
                                nc.scalar.activation(o, o, func, bias=cols[:, i, f:f + 1]).then_inc(out_ready, 1)
                                n += 1
                root(nc, act, norm[:, 0, :], norm[:, 1, :], bn_ready, bn_rooted)
                act.wait_ge(norm_ready, 1)
                n = 0
                for t0, k in QUADS:
                    for f in range(F):
                        act.wait_ge(mixed, n + 1)
                        o = outT[:, f, t0 * P:(t0 + k) * P]
                        nc.scalar.activation(o, o, ACT.Relu, bias=norm[:, 3, f:f + 1]).then_inc(final_ready, 1)
                        n += 1

            @block.tensor
            def _(pe):
                pe.wait_ge(dinv_ready, 1)
                nc.tensor.transpose(bank[7][0:T, 0:P], dinv[:], g.ident[0:P, 0:P]).then_inc(dinv_turned, 1)
                pe.wait_ge(xn_ready, 1)
                turn_tiles(nc, pe, msg, D, bank[0:4], g.ident, turn_read, turned)
                pe.wait_ge(w_in, 160)
                pe.wait_ge(turn_read, F * NQ)
                pe.wait_ge(dinv_read, 1)
                for i in range(2):
                    rows = xT if i == 0 else outT
                    for n, (t0, k) in enumerate(PAIRS):
                        if i and n == 0:
                            pe.wait_ge(out_ready, BIG)
                        if n >= 8:
                            pe.wait_ge(msg_ready, i * NP + n - 7)
                        for u in range(k):
                            for f in range(F):
                                mm = nc.tensor.matmul(bank[n % 8][0:P, u * D:(u + 1) * D],
                                                      rows[:, f, (t0 + u) * P:(t0 + u + 1) * P], w[i][:, f, :],
                                                      start=(f == 0), stop=(f == F - 1))
                        mm.then_inc(multiplied, 1)
                    pe.wait_ge(msg_ready, (i + 1) * NP)
                    before = 0
                    for v, (first, chunks) in enumerate(WINDOWS):
                        if v:
                            pe.wait_ge(scaled, i * BIG + before)
                        for c, (t0, k) in enumerate(chunks):
                            for f in range(F):
                                for u in range(k):
                                    nc.tensor.matmul(bank[2 * c + f][:, u * P:(u + 1) * P],
                                                     msg[:, t0 + u, f * 128:(f + 1) * 128], g.ident[0:P, 0:P],
                                                     start=(u == 0), stop=False, skip_group_check=True)

                        trip = (i * 2 + v) * (T // RING)
                        with pe.Fori(0, T // RING) as m:
                            for r in range(RING):
                                pe.wait_ge(strip_in[r], (m + trip + 1) * 16)
                                pe.wait_ge(now_ready, (m + trip) * RING + r + 1)
                                for f in range(F):
                                    for c, (t0, k) in enumerate(chunks):
                                        mm = nc.tensor.matmul(
                                            bank[2 * c + f][:, 0:k * P],
                                            msg_now[:, r, f * 128:(f + 1) * 128],
                                            strips[:, r, (t0 - first) * P:(t0 - first + k) * P], start=False,
                                            stop=True, skip_group_check=True)
                                mm.then_inc(strip_used, 1)
                        before += 2 * len(chunks)
                for n, (t0, k) in enumerate(PAIRS):
                    if n == 0:
                        pe.wait_ge(scaled, 2 * BIG)
                    pe.wait_ge(final_ready, F * ((t0 + k - 1) // 4 + 1))
                    if n >= 8:
                        pe.wait_ge(added, n - 7)
                    for u in range(k):
                        for f in range(F):
                            mm = nc.tensor.transpose(bank[n % 8][0:P, u * D + f * 128:u * D + (f + 1) * 128],
                                                     outT[:, f, (t0 + u) * P:(t0 + u + 1) * P], g.ident[:, :])
                    mm.then_inc(back, 1)

            @block.vector
            def _(dve):
                step = Step(dve, dve_step)
                V = nc.vector
                step(V.tensor_reduce(dinv[:], g.deg[:, :, 1:4], AX.X, ALU.add))
                step(V.tensor_scalar_add(dinv[:], dinv[:], 1.0))
                step(V.tensor_scalar(mask[:], dinv[:], 0.0, None, ALU.is_gt))
                V.tensor_scalar_max(dinv[:], dinv[:], 1e-30).then_inc(deg_ready, 1)
                inverse_root(nc, dve, step, dinv[:], rooted[:], tmp[:], deg_rooted)
                V.tensor_tensor(dinv[:], dinv[:], mask[:], ALU.mult).then_inc(dinv_ready, 1)
                dve.wait_ge(dinv_turned, 1)
                V.tensor_copy(dinv_t[:], bank[7][0:T, 0:P]).then_inc(dinv_read, 1)
                layer_norm(nc, dve, step, g.xr, msg, stats, small, rows_done, var_ready, root_done)
                dve.sem_inc(xn_ready)
                dve.wait_ge(w_in, 160)
                dve.wait_ge(turned, F * NQ)
                for i in range(2):
                    if i:
                        dve.wait_ge(strip_used, 2 * T)
                    for n, (t0, k) in enumerate(PAIRS):
                        dve.wait_ge(multiplied, i * NP + n + 1)
                        V.tensor_tensor(msg[:, t0:t0 + k, :],
                                        bank[n % 8][0:P, 0:k * D].rearrange("p (u c) -> p u c", u=k),
                                        dinv[:, t0:t0 + k, None].to_broadcast([P, k, D]), ALU.mult).then_inc(msg_ready, 1)
                    if i == 0:
                        dve.wait_ge(row_in, 16)
                    for v, (first, chunks) in enumerate(WINDOWS):
                        dve.wait_ge(strip_used, (i * 2 + v + 1) * T)
                        for c, (t0, k) in enumerate(chunks):
                            for f in range(F):
                                at = slice(t0 * P, (t0 + k) * P)
                                V.tensor_tensor(outT[:, f, at], bank[2 * c + f][:, 0:k * P], dinv_row[:, at],
                                                ALU.mult).then_inc(scaled, 1)
                dve.wait_ge(out_ready, 2 * BIG)
                for f in range(F):
                    for q, (t0, k) in enumerate(QUADS):
                        ins = V.bn_stats(bn[:, f, q, :], outT[:, f, t0 * P:(t0 + k) * P])
                step(ins)
                for f in range(F):
                    step(V.bn_aggr(agg[:, f, :], bn[:, f, :, :].rearrange("p q k -> p (q k)")))
                V.tensor_scalar_add(norm[:, 0, :], agg[:, :, 1], EPS).then_inc(bn_ready, 1)
                inverse_root(nc, dve, step, norm[:, 0, :], norm[:, 1, :], norm[:, 2, :], bn_rooted)
                step(V.tensor_tensor(norm[:, 0, :], norm[:, 0, :], cols[:, 2, :], ALU.mult))
                step(V.tensor_tensor(norm[:, 2, :], norm[:, 0, :], agg[:, :, 0], ALU.mult))
                step(V.tensor_tensor(norm[:, 3, :], cols[:, 3, :], norm[:, 2, :], ALU.subtract))
                dve.sem_inc(norm_ready)
                for t0, k in QUADS:
                    for f in range(F):
                        at = slice(t0 * P, (t0 + k) * P)
                        V.scalar_tensor_tensor(out=outT[:, f, at], in0=outT[:, f, at], scalar=norm[:, 0, f:f + 1],
                                               in1=xT[:, f, at], op0=ALU.mult, op1=ALU.add).then_inc(mixed, 1)
                for n, (t0, k) in enumerate(PAIRS):
                    dve.wait_ge(back, n + 1)
                    V.tensor_tensor(g.xr[:, t0:t0 + k, :], g.xr[:, t0:t0 + k, :],
                                    bank[n % 8][0:P, 0:k * D].rearrange("p (u c) -> p u c", u=k),
                                    ALU.add).then_inc(added, 1)
                dve.wait_ge(added, NP)

F2 = 512
FAR = -1e30
NT = 2 * N // P + NE


def route_second(nc, g):
    with stage(nc) as (ctx, sem):
        sb = lambda n, s, d: ctx.enter_context(nc.sbuf_tensor(unique(n), s, d))
        ps = lambda n: ctx.enter_context(nc.psum_tensor(unique(n), [128, 512], F32))
        xn, xT = sb("xn_z", [P, T, D], F32), sb("xT_z", [128, F, N], F32)
        stats, small = sb("stats_z", [P, T, 6], F32), sb("small_z", [P, 4, T], F32)
        zero = sb("zero_z", [P, 1, D], F32)
        gb = sb("gb_z", [P, 2, D], F32)
        wr, br = sb("wr_z", [128, F, NE], F32), sb("br_z", [P, NE], F32)
        rev, tri = sb("rev_z", [P, NE], F32), sb("tri_z", [P, P], F32)
        number = sb("number_z", [P, NT], F32)
        logits, a, share = sb("logits_z", [P, T, NE], F32), sb("a_z", [P, T, NE], F32), sb("share_z", [P, T, NE], F32)
        hot = sb("hot_z", [P, 2, T, NE], F32)
        both, totals = sb("both_z", [P, T, NE], F32), sb("totals_z", [P, 2, T, NE], F32)
        top, pick = sb("top_z", [P, 2, T], F32), sb("pick_z", [P, T], F32)
        ratio, place = sb("ratio_z", [P, T], F32), sb("place_z", [P, T], F32)
        tiles, ends, starts = (sb(f"{k}_z", [P, NE], F32) for k in ("tiles", "ends", "starts"))
        past, owner = sb("past_z", [P, NT, NE - 1], F32), sb("owner_z", [P, NT], F32)
        shareT = sb("shareT_z", [NE, N], F32)
        b2 = sb("b2_z", [NE, D], F32)
        bank = [ps(f"bank_z{k}") for k in range(8)]
        small_in = sem("small_in_z")
        rows_done, var_ready, root_done = sem("rows_done_z"), sem("var_ready_z"), sem("root_done_z")
        dve_step, xn_ready, turned, turn_read = sem("dve_step_z"), sem("xn_ready_z"), sem("turned_z"), sem("turn_read_z")
        consts, gated, asked, answered = sem("consts_z"), sem("gated_z"), sem("asked_z"), sem("answered_z")
        picked, counted, places_ready = sem("picked_z"), sem("counted_z"), sem("places_ready_z")
        share_ready, share_turned, share_read = sem("share_ready"), sem("share_turned"), sem("share_read")
        biased, bias_read = sem("biased"), sem("bias_read")
        cleared, clear_out, scattered = sem("cleared_z"), sem("clear_out_z"), sem("scattered_z")
        NQ, NP = len(QUADS), len(PAIRS)

        with nc.Block() as block:
            @block.sync
            def _(sp):
                for k, v in enumerate((g.L1_ffn_gamma, g.L1_ffn_beta)):
                    sp.dma_start(gb[:, k, :], v[None, :].to_broadcast([P, D])).then_inc(small_in, 16)
                sp.dma_start(wr[:], g.L1_ffn_Wr.rearrange("(f i) e -> i f e", i=128)).then_inc(small_in, 16)
                sp.dma_start(br[:], g.L1_ffn_br[None, :].to_broadcast([P, NE])).then_inc(small_in, 16)
                sp.dma_start(b2[:], g.L1_ffn_b2).then_inc(small_in, 16)
                sp.wait_ge(cleared, 1)
                sp.dma_start(g.placed2.rearrange("(p n) d -> p n d", p=P), zero[:].to_broadcast([P, NT, D])).then_inc(
                    clear_out, 16)

            @block.gpsimd
            def _(pool):
                pool.memset(zero[:], 0.0).then_inc(cleared, 1)
                pool.iota(rev[:], pattern=[[-1, NE]], base=NE, channel_multiplier=0,
                          allow_small_or_imprecise_dtypes=True).then_inc(consts, 1)
                pool.iota(number[:], pattern=[[1, NT]], base=0, channel_multiplier=0,
                          allow_small_or_imprecise_dtypes=True).then_inc(consts, 1)
                pool.affine_select(out=tri[:], in_=g.ones[0:P, 0:P], compare_op=ALU.is_gt, fill=0.0, base=0,
                                   pattern=[[1, P]], channel_multiplier=-1).then_inc(consts, 1)
                bound = pool.to_reg(NT * P - 1)
                pool.wait_ge(clear_out, 16)
                for k in range(2):
                    pool.wait_ge(places_ready, k + 1)
                    for t in range(T):
                        pool.indirect_dma_start(
                            out=g.placed2, out_offset=bass.IndirectOffsetOnAxis(ap=g.place_at[:, k, t:t + 1], axis=0),
                            in_=xn[:, t, :], in_offset=None, bounds_check=bound, oob_is_err=False).then_inc(scattered, 16)
                pool.wait_ge(scattered, 2 * 16 * T)

            @block.scalar
            def _(act):
                root(nc, act, small[:, 1, :], small[:, 3, :], var_ready, root_done)
                n = 0
                for t0, k in QUADS:
                    for f in range(F):
                        act.wait_ge(turned, n + 1)
                        nc.scalar.copy(xT[:, f, t0 * P:(t0 + k) * P], bank[n % 4][:, 0:k * P]).then_inc(turn_read, 1)
                        n += 1
                act.wait_ge(asked, 1)
                nc.scalar.activation(ratio[:], ratio[:], ACT.Exp).then_inc(answered, 1)

            @block.tensor
            def _(pe):
                pe.wait_ge(xn_ready, 1)
                turn_tiles(nc, pe, xn, D, bank[0:4], g.ident, turn_read, turned)
                pe.wait_ge(small_in, 80)
                pe.wait_ge(turn_read, F * NQ)
                for t in range(T):
                    for f in range(F):
                        mm = nc.tensor.matmul(bank[5][0:P, t * NE:(t + 1) * NE], xT[:, f, t * P:(t + 1) * P],
                                              wr[:, f, :], start=(f == 0), stop=(f == F - 1))
                mm.then_inc(gated, 1)
                pe.wait_ge(picked, 1)
                pe.wait_ge(consts, 3)
                flat = both[:].rearrange("p t e -> p (t e)")
                nc.tensor.matmul(bank[2][0:P, 0:T * NE], g.ones[0:P, 0:P], flat, start=True, stop=True).then_inc(counted, 1)
                nc.tensor.matmul(bank[3][0:P, 0:T * NE], tri[:], flat, start=True, stop=True).then_inc(counted, 1)
                pe.wait_ge(share_ready, 1)
                for q, (t0, k) in enumerate(QUADS):
                    if q >= 2:
                        pe.wait_ge(share_read, q - 1)
                    for u in range(k):
                        mm = nc.tensor.transpose(bank[6 + q % 2][0:NE, u * P:(u + 1) * P], share[:, t0 + u, :],
                                                 g.ident[0:P, 0:P])
                    mm.then_inc(share_turned, 1)
                pe.wait_ge(share_read, NQ)
                for n, (t0, k) in enumerate(PAIRS):
                    if n >= 4:
                        pe.wait_ge(bias_read, n - 3)
                    for u in range(k):
                        mm = nc.tensor.matmul(bank[4 + n % 4][0:P, u * D:(u + 1) * D],
                                              shareT[:, (t0 + u) * P:(t0 + u + 1) * P], b2[:], start=True, stop=True)
                    mm.then_inc(biased, 1)

            @block.vector
            def _(dve):
                step = Step(dve, dve_step)
                V = nc.vector
                bc = lambda v: v[:, :, None].to_broadcast([P, T, NE])
                per_expert = lambda b: b[0:P, 0:T * NE].rearrange("p (t e) -> p t e", e=NE)
                layer_norm(nc, dve, step, g.xr, xn, stats, small, rows_done, var_ready, root_done)
                dve.wait_ge(small_in, 80)
                step(V.tensor_tensor(xn[:], xn[:], gb[:, 0:1, :].to_broadcast([P, T, D]), ALU.mult))
                V.tensor_tensor(xn[:], xn[:], gb[:, 1:2, :].to_broadcast([P, T, D]), ALU.add).then_inc(xn_ready, 1)
                dve.wait_ge(gated, 1)
                dve.wait_ge(consts, 3)
                step(V.tensor_tensor(logits[:], per_expert(bank[5]), br[:, None, :].to_broadcast([P, T, NE]), ALU.add))
                for k in range(2):
                    step(V.tensor_reduce(top[:, k, :], logits[:], AX.X, ALU.max))
                    step(V.tensor_tensor(a[:], logits[:], bc(top[:, k, :]), ALU.is_equal))
                    step(V.tensor_tensor(a[:], a[:], rev[:, None, :].to_broadcast([P, T, NE]), ALU.mult))
                    step(V.tensor_reduce(pick[:], a[:], AX.X, ALU.max))
                    step(V.tensor_tensor(hot[:, k], a[:], bc(pick[:]), ALU.is_equal))
                    if k == 0:
                        step(V.scalar_tensor_tensor(out=logits[:], in0=hot[:, 0], scalar=FAR, in1=logits[:],
                                                    op0=ALU.mult, op1=ALU.add))
                V.tensor_tensor(both[:], hot[:, 0], hot[:, 1], ALU.add).then_inc(picked, 1)
                dve.wait_ge(counted, 2)
                step(V.tensor_copy(totals[:, 0], per_expert(bank[2])))
                now, hop = 0, 1
                while hop < T:
                    step(V.tensor_copy(totals[:, 1 - now, 0:hop, :], totals[:, now, 0:hop, :]))
                    step(V.tensor_tensor(totals[:, 1 - now, hop:T, :], totals[:, now, hop:T, :],
                                         totals[:, now, 0:T - hop, :], ALU.add))
                    now, hop = 1 - now, hop * 2
                step(V.tensor_scalar(tiles[:], totals[:, now, T - 1, :], 1.0 / P, (P // 2) / P, ALU.mult, ALU.add))
                step(V.tensor_scalar_add(ends[:], tiles[:], ROUND))
                step(V.tensor_scalar_add(tiles[:], ends[:], -ROUND))
                step(V.tensor_copy(ends[:], tiles[:]))
                for e in range(1, NE):
                    step(V.tensor_tensor(ends[:, e:e + 1], ends[:, e:e + 1], ends[:, e - 1:e], ALU.add))
                step(V.tensor_tensor(starts[:], ends[:], tiles[:], ALU.subtract))
                step(V.tensor_tensor(a[:], totals[:, now], per_expert(bank[2]), ALU.subtract))
                step(V.tensor_tensor(a[:], a[:], per_expert(bank[3]), ALU.add))
                step(V.tensor_scalar_mul(starts[:], starts[:], float(P)))
                step(V.tensor_tensor(a[:], a[:], starts[:, None, :].to_broadcast([P, T, NE]), ALU.add))
                for k in range(2):
                    step(V.tensor_tensor(totals[:, 0], hot[:, k], a[:], ALU.mult))
                    step(V.tensor_reduce(place[:], totals[:, 0], AX.X, ALU.add))
                    step(V.tensor_copy(g.place_at[:, k, :], place[:]))
                    dve.sem_inc(places_ready)
                step(V.tensor_tensor(past[:], number[:, :, None].to_broadcast([P, NT, NE - 1]),
                                     ends[:, None, 0:NE - 1].to_broadcast([P, NT, NE - 1]), ALU.is_ge))
                step(V.tensor_reduce(owner[:], past[:], AX.X, ALU.add))
                step(V.tensor_copy(g.expert_of[:], owner[0:1, :]))
                V.tensor_tensor(ratio[:], top[:, 1, :], top[:, 0, :], ALU.subtract).then_inc(asked, 1)
                dve.wait_ge(answered, 1)
                step(V.tensor_scalar_add(g.shares[:, 0, :], ratio[:], 1.0))
                step(V.reciprocal(g.shares[:, 0, :], g.shares[:, 0, :]))
                step(V.tensor_tensor(g.shares[:, 1, :], ratio[:], g.shares[:, 0, :], ALU.mult))
                step(V.tensor_tensor(share[:], hot[:, 0], bc(g.shares[:, 0, :]), ALU.mult))
                step(V.tensor_tensor(a[:], hot[:, 1], bc(g.shares[:, 1, :]), ALU.mult))
                V.tensor_tensor(share[:], share[:], a[:], ALU.add).then_inc(share_ready, 1)
                for q, (t0, k) in enumerate(QUADS):
                    dve.wait_ge(share_turned, q + 1)
                    V.tensor_copy(shareT[:, t0 * P:(t0 + k) * P], bank[6 + q % 2][0:NE, 0:k * P]).then_inc(share_read, 1)
                for n, (t0, k) in enumerate(PAIRS):
                    dve.wait_ge(biased, n + 1)
                    V.tensor_tensor(g.xr[:, t0:t0 + k, :], g.xr[:, t0:t0 + k, :],
                                    bank[4 + n % 4][0:P, 0:k * D].rearrange("p (u c) -> p u c", u=k),
                                    ALU.add).then_inc(bias_read, 1)
                dve.wait_ge(bias_read, NP)


def second_experts(nc, g):
    M2 = F2 // 128
    with stage(nc) as (ctx, sem):
        sb = lambda n, s, d: ctx.enter_context(nc.sbuf_tensor(unique(n), s, d))
        ps = lambda n: [ctx.enter_context(nc.psum_tensor(unique(f"{n}{k}"), [128, 512], F32)) for k in range(2)]
        rows, xT = sb("rows_v", [P, 2, D], F32), sb("xT_v", [128, 2, F, P], F32)
        before, hidT = sb("before_v", [P, 2, F2], F32), sb("hidT_v", [128, 2, M2, P], F32)
        y = sb("y_v", [P, 2, D], F32)
        b1_rows, b1 = sb("b1_rows_v", [NE * M2, 128], F32), sb("b1_v", [128, NE, M2], F32)
        p_x, p_up, p_h, p_y = ps("p_x_v"), ps("p_up_v"), ps("p_h_v"), ps("p_y_v")
        b1_in, b1_turned, b1_ready, tile_held = sem("b1_in_v"), sem("b1_turned_v"), sem("b1_ready_v"), sem("tile_held")
        rows_in, y_out = [sem(f"rows_in_v{k}") for k in range(2)], [sem(f"y_out_v{k}") for k in range(2)]
        x_turned, x_ready, up_done, up_read = sem("x_turned_v"), sem("x_ready_v"), sem("up_done_v"), sem("up_read_v")
        h_turned, h_ready, down_done, y_ready = sem("h_turned_v"), sem("h_ready_v"), sem("down_done_v"), sem("y_ready_v")

        def in_pairs(engine, first, last, body):
            with engine.Fori(first // 2, last // 2) as m:
                body(m * 2 + 1, 1, m)
                body(m * 2 + 2, 0, m + 1)

        with nc.Block() as block:
            @block.sync
            def _(sp):
                def load(i, b):
                    sp.dma_start(rows[:, b], g.placed2[bass.ds(i * P, P), :]).then_inc(rows_in[b], 16)

                sp.dma_start(b1_rows[:], g.L1_ffn_b1.rearrange("e (m i) -> (e m) i", i=128)).then_inc(b1_in, 16)
                load(0, 0)
                load(1, 1)
                with sp.Fori(1, NT // 2) as m:
                    for b in range(2):
                        sp.wait_ge(x_turned, m * 2 + b - 1)
                        load(m * 2 + b, b)

            @block.gpsimd
            def _(pool):
                with pool.Fori(0, NT // 2) as m:
                    for b in range(2):
                        pool.wait_ge(y_ready, m * 2 + b + 1)
                        pool.sem_inc(tile_held)
                        pool.dma_start(g.results2[bass.ds((m * 2 + b) * P, P), :], y[:, b]).then_inc(y_out[b], 16)
                for b in range(2):
                    pool.wait_ge(y_out[b], 16 * (NT // 2))

            @block.tensor
            def _(pe):
                def turn_rows(i, b, m, first):
                    pe.wait_ge(rows_in[b], m * 16 + 16)
                    if not first:
                        pe.wait_ge(x_ready, i - 1)
                    for f in range(F):
                        mm = nc.tensor.transpose(p_x[b][:, f * P:(f + 1) * P], rows[:, b, f * 128:(f + 1) * 128],
                                                 g.ident[0:P, 0:P])
                    mm.then_inc(x_turned, 1)

                def up(i, b, first):
                    e = pe.value_load(g.expert_of[0:1, bass.ds(i, 1)], min_val=0, max_val=NE - 1)
                    pe.wait_ge(x_ready, i + 1)
                    if not first:
                        pe.wait_ge(up_read, i - 1)
                    for f in range(F):
                        mm = nc.tensor.matmul(p_up[b][0:P, :], xT[:, b, f, :],
                                              g.w1_all[:, bass.ds(e, 1), f, :].rearrange("p a o -> p (a o)"),
                                              start=(f == 0), stop=(f == F - 1))
                    mm.then_inc(up_done, 1)

                def turn_hidden(i, b, first):
                    pe.wait_ge(up_read, i + 1)
                    if not first:
                        pe.wait_ge(h_ready, i - 1)
                    for m in range(M2):
                        mm = nc.tensor.transpose(p_h[b][:, m * P:(m + 1) * P], before[:, b, m * 128:(m + 1) * 128],
                                                 g.ident[0:P, 0:P])
                    mm.then_inc(h_turned, 1)

                def down(i, b, first):
                    e = pe.value_load(g.expert_of[0:1, bass.ds(i, 1)], min_val=0, max_val=NE - 1)
                    pe.wait_ge(h_ready, i + 1)
                    if not first:
                        pe.wait_ge(y_ready, i - 1)
                    for m in range(M2):
                        mm = nc.tensor.matmul(p_y[b][0:P, 0:D], hidT[:, b, m, :],
                                              g.w2_all[:, bass.ds(e, 1), m, :].rearrange("p a o -> p (a o)"),
                                              start=(m == 0), stop=(m == M2 - 1))
                    mm.then_inc(down_done, 1)

                pe.wait_ge(b1_in, 16)
                nc.tensor.transpose(p_h[1][:, 0:NE * M2], b1_rows[:], g.ident[0:NE * M2, 0:NE * M2]).then_inc(b1_turned, 1)
                turn_rows(0, 0, 0, True)
                up(0, 0, True)
                turn_rows(1, 1, 0, True)
                turn_hidden(0, 0, True)
                pe.wait_ge(b1_ready, 1)
                up(1, 1, True)
                turn_rows(2, 0, 1, False)
                down(0, 0, True)
                turn_hidden(1, 1, True)
                up(2, 0, False)
                turn_rows(3, 1, 1, False)
                down(1, 1, True)
                turn_hidden(2, 0, False)

                def both(i, b, m):
                    up(i, b, False)
                    turn_rows(i + 1, 1 - b, m + b, False)
                    down(i - 1, 1 - b, False)
                    turn_hidden(i, b, False)

                in_pairs(pe, 3, NT - 1, both)
                up(NT - 1, 1, False)
                down(NT - 2, 0, False)
                turn_hidden(NT - 1, 1, False)
                down(NT - 1, 1, False)

            @block.scalar
            def _(act):
                act.wait_ge(b1_turned, 1)
                nc.scalar.copy(b1[:].rearrange("p e m -> p (e m)"), p_h[1][:, 0:NE * M2]).then_inc(b1_ready, 1)
                act.wait_ge(b1_ready, 1)

                def gelu(i, b, first):
                    e = act.value_load(g.expert_of[0:1, bass.ds(i, 1)], min_val=0, max_val=NE - 1)
                    act.wait_ge(h_turned, i + 1)
                    if not first:
                        act.wait_ge(down_done, i - 1)
                    for m in range(M2):
                        ins = nc.scalar.activation(hidT[:, b, m, :], p_h[b][:, m * P:(m + 1) * P], ACT.Gelu,
                                                   bias=b1[:, bass.ds(e, 1), m])
                    ins.then_inc(h_ready, 1)

                gelu(0, 0, True)
                gelu(1, 1, True)
                with act.Fori(1, NT // 2) as m:
                    for b in range(2):
                        gelu(m * 2 + b, b, False)

            @block.vector
            def _(dve):
                V = nc.vector

                def take_rows(i, b, first):
                    dve.wait_ge(x_turned, i + 1)
                    if not first:
                        dve.wait_ge(up_done, i - 1)
                    V.tensor_copy(xT[:, b].rearrange("p f e -> p (f e)"), p_x[b][:, 0:F * P]).then_inc(x_ready, 1)

                def take_up(i, b, first):
                    dve.wait_ge(up_done, i + 1)
                    if not first:
                        dve.wait_ge(h_turned, i - 1)
                    V.tensor_copy(before[:, b], p_up[b][0:P, :]).then_inc(up_read, 1)

                def take_y(i, b, m, first):
                    dve.wait_ge(down_done, i + 1)
                    if not first:
                        dve.wait_ge(y_out[b], m * 16)
                    V.tensor_copy(y[:, b], p_y[b][0:P, 0:D]).then_inc(y_ready, 1)

                take_rows(0, 0, True)
                take_up(0, 0, True)
                take_rows(1, 1, True)
                take_up(1, 1, True)
                take_rows(2, 0, False)
                take_y(0, 0, 0, True)
                take_up(2, 0, False)
                take_rows(3, 1, False)
                take_y(1, 1, 0, True)

                def both(i, b, m):
                    take_up(i, b, False)
                    take_rows(i + 1, 1 - b, False)
                    take_y(i - 1, 1 - b, m if b else m - 1, False)

                in_pairs(dve, 3, NT - 1, both)
                take_up(NT - 1, 1, False)
                take_y(NT - 2, 0, NT // 2 - 1, False)
                take_y(NT - 1, 1, NT // 2 - 1, False)


def combine_second(nc, g):
    with stage(nc) as (ctx, sem):
        y = ctx.enter_context(nc.sbuf_tensor(unique("y_u"), [P, T, 2, D], F32))
        gathered = [sem(f"gathered_u{k}") for k in range(5)]
        first_added, summed, x_out = sem("first_added"), sem("summed_u"), sem("x_out_u")
        with nc.Block() as block:
            @block.gpsimd
            def _(pool):
                for n in range(2 * T):
                    if n >= 5:
                        pool.wait_ge(gathered[n % 5], 16 * (n // 5))
                    pool.indirect_dma_start(
                        out=y[:, n // 2, n % 2, :], out_offset=None, in_=g.results2,
                        in_offset=bass.IndirectOffsetOnAxis(ap=g.place_at[:, n % 2, n // 2:n // 2 + 1], axis=0)
                    ).then_inc(gathered[n % 5], 16)

            @block.vector
            def _(dve):
                for t in range(T):
                    for k in range(2):
                        n = 2 * t + k
                        dve.wait_ge(gathered[n % 5], 16 * (n // 5 + 1))
                        if k:
                            dve.wait_ge(first_added, t + 1)
                        nc.vector.scalar_tensor_tensor(
                            out=g.xr[:, t, :], in0=y[:, t, k, :], scalar=g.shares[:, k, t:t + 1], in1=g.xr[:, t, :],
                            op0=ALU.mult, op1=ALU.add).then_inc(summed if k else first_added, 1)

            @block.sync
            def _(sp):
                for t0 in range(0, T, 5):
                    sp.wait_ge(summed, t0 + 5)
                    sp.dma_start(g.out.rearrange("(t p) d -> p t d", p=P)[:, t0:t0 + 5, :], g.xr[:, t0:t0 + 5, :]
                                 ).then_inc(x_out, 16)
                sp.wait_ge(x_out, T // 5 * 16)


def second_ffn(nc, g):
    with ExitStack() as ctx:
        sb = lambda n, s, d: ctx.enter_context(nc.sbuf_tensor(unique(n), s, d))
        g.place_at, g.shares = sb("place_at", [P, 2, T], U32), sb("shares", [P, 2, T], F32)
        g.expert_of = sb("expert_of", [1, NT], I32)
        g.w1_all, g.w2_all = sb("w1_all", [128, NE, F, F2], F32), sb("w2_all", [128, NE, F2 // 128, D], F32)
        w_all_in = nc.alloc_semaphore(name=unique("w_all_in"))
        with nc.Block() as block:
            @block.scalar
            def _(act):
                for e in range(NE):
                    act.dma_start(g.w1_all[:, e], g.L1_ffn_W1[e].rearrange("(f i) o -> i f o", i=128)).then_inc(w_all_in, 16)
                    act.dma_start(g.w2_all[:, e], g.L1_ffn_W2[e].rearrange("(m i) o -> i m o", i=128)).then_inc(w_all_in, 16)
        route_second(nc, g)
        with nc.Block() as block:
            @block.tensor
            def _(pe):
                pe.wait_ge(w_all_in, NE * 32)
        second_experts(nc, g)
        nc.clear_and_free_semaphores([w_all_in])
        nc.all_engine_barrier()
        combine_second(nc, g)


def prepare(nc, g):
    with stage(nc) as (_, sem):
        ones_ready, ready = sem("ones_ready"), sem("consts_ready")
        with nc.Block() as block:
            @block.gpsimd
            def _(pool):
                pool.iota(g.iota[:], pattern=[[1, 128]], base=0, channel_multiplier=0,
                          allow_small_or_imprecise_dtypes=True).then_inc(ready, 1)
                pool.memset(g.ones[:], 1.0).then_inc(ones_ready, 1)
                pool.wait_ge(ones_ready, 1)
                pool.affine_select(out=g.ident[:], in_=g.ones[:], compare_op=ALU.is_equal, fill=0.0, base=0,
                                   pattern=[[-1, 128]], channel_multiplier=1).then_inc(ready, 1)
                pool.wait_ge(ready, 2)


def program(nc, g):
    dram = lambda n, s: nc.dram_tensor(n, s, F32).ap()
    g.slots = dram("slots", (NB * P, 2))
    g.xn, g.weights, g.dinv = dram("xn_dram", (N, D)), dram("weights_dram", (N, N)), dram("dinv_dram", (N,))
    g.edge_rec, g.edge_key, g.edge_rank = dram("edge_rec", (P, 2 * EC)), dram("edge_key", (P, EC)), dram("edge_rank", (P, EC))
    g.high = nc.dram_tensor("high_counts", (N, N), BF16).ap()
    g.placed, g.results = dram("placed_dram", (NE * CP, D)), dram("results_dram", (NE * CP, D))
    g.placed2, g.results2 = dram("placed2_dram", (NT * P, D)), dram("results2_dram", (NT * P, D))
    with ExitStack() as whole:
        keep = lambda ctx, n, s, d: ctx.enter_context(nc.sbuf_tensor(unique(n), s, d))
        g.spare = keep(whole, "spare", [128, 4], F32)
        g.ident, g.ones = keep(whole, "ident", [128, 128], F32), keep(whole, "ones", [128, 128], F32)
        g.iota = keep(whole, "iota", [128, 128], BF16)
        g.rounds, g.offset = keep(whole, "rounds", [1, 1], I32), keep(whole, "offset", [P, 1], F32)
        g.deg = keep(whole, "deg", [P, T, 4], F32)
        prepare(nc, g)
        g.dyn, g.h = keep(whole, "dyn", [P, T, C0], F32), keep(whole, "h", [P, T, C0], F32)
        with ExitStack() as ctx:
            g.ranks = keep(ctx, "ranks", [P, EC], F32)
            sort_edges(nc, g)
            count_rounds(nc, g)
        with ExitStack() as graph:
            g.xparts = keep(graph, "xparts", [P, T, 3, C0], BF16)
            normalise_input(nc, g)
            g.counts = keep(graph, "counts", [P, T, N], BF16)
            with ExitStack() as build:
                g.slot_w, g.slot_ids = keep(build, "slot_w", [P, NB], F32), keep(build, "slot_ids", [P, 2, NB], F32)
                g.slot_deg = keep(build, "slot_deg", [P, NB, 4], BF16)
                load_slots(nc, g)
                build_blocks(nc, g)
                further_rounds(nc, g)
            g.parts, g.own = g.xparts, keep(graph, "own", [P, T, C0], F32)
            g.w_static, g.b_static = keep(graph, "w_static", [C0, 3, C0], F32), keep(graph, "b_static", [P, 3, C0], F32)
            g.dinv_s = keep(graph, "dinv_s", [P, T], F32)
            static_degrees(nc, g)
            for i in range(3):
                static_messages(nc, g, i)
                add_high_counts(nc, g)
                static_sums(nc, g)
        g.xr = keep(whole, "xr", [P, T, D], F32)
        first_gnn_out(nc, g)
        g.chance, g.gather_at = keep(whole, "chance", [P, T], F32), keep(whole, "gather_at", [P, T], U32)
        route_first(nc, g)
        first_experts(nc, g)
        combine_first(nc, g)
        second_gnn(nc, g)
        second_ffn(nc, g)


_INS = ["x", "src", "dst", "edge_weight", "L0_gnn_W_static", "L0_gnn_b_static", "L0_gnn_W1", "L0_gnn_b1", "L0_gnn_W2",
        "L0_gnn_b2", "L0_gnn_W_aggr", "L0_gnn_b_aggr", "L0_ffn_gate_w", "L0_ffn_gate_b", "L0_ffn_w1", "L0_ffn_b1",
        "L0_ffn_w2", "L0_ffn_b2", "L1_gnn_W1", "L1_gnn_b1", "L1_gnn_W2", "L1_gnn_b2", "L1_gnn_gamma", "L1_gnn_beta",
        "L1_ffn_gamma", "L1_ffn_beta", "L1_ffn_Wr", "L1_ffn_br", "L1_ffn_W1", "L1_ffn_b1", "L1_ffn_W2", "L1_ffn_b2"]


class Tensors:
    pass


def kernel(**inputs):
    import numpy as _np
    import concourse.bacc as _bacc
    from concourse import mybir as _mybir
    from concourse.bass_utils import run_bass_kernel_spmd as _run

    nc = _bacc.Bacc("TRN2", target_bir_lowering=False, num_devices=1)
    arrays, g = {}, Tensors()
    for name in _INS:
        a = _np.ascontiguousarray(inputs[name])
        arrays[f"in_{name}_dram"] = a
        g.__dict__[name] = nc.dram_tensor(f"in_{name}_dram", a.shape, _mybir.dt.from_np(a.dtype),
                                          kind="ExternalInput").ap()
    g.out = nc.dram_tensor("out_0_dram", (N, D), _mybir.dt.float32, kind="ExternalOutput").ap()
    program(nc, g)
    r = _run(nc, [arrays], core_ids=[0])
    return r.results[0]["out_0_dram"]
```

```python
from contextlib import ExitStack, contextmanager

import concourse.bass as bass
from concourse import mybir

F32 = mybir.dt.float32
BF16 = mybir.dt.bfloat16
F16 = mybir.dt.float16
I32 = mybir.dt.int32
U32 = mybir.dt.uint32
ALU = mybir.AluOpType
ACT = mybir.ActivationFunctionType
AX = mybir.AxisListType

N, D, E = 3125, 256, 50000
P = 125
T = N // P
NB = T * T
EC = E // P
C0 = 64
NO_LANE = 127
EMPTY = float(NO_LANE * 128 + NO_LANE)
PAST = float(1 << 20)
ROUND = float(3 << 22)


class Step:

    def __init__(self, engine, semaphore):
        self.engine, self.semaphore, self.count = engine, semaphore, 0

    def __call__(self, instruction):
        self.count += 1
        instruction.then_inc(self.semaphore, 1)
        self.engine.wait_ge(self.semaphore, self.count)


_uses = {}


def unique(name):
    _uses[name] = _uses.get(name, 0) + 1
    return f"{name}_{_uses[name]}"


@contextmanager
def stage(nc):
    sems = []

    def sem(name):
        sems.append(nc.alloc_semaphore(name=unique(name)))
        return sems[-1]

    with ExitStack() as ctx:
        yield ctx, sem
    nc.all_engine_barrier()
    nc.clear_and_free_semaphores(sems)
    nc.all_engine_barrier()


def sort_edges(nc, g):
    G = 16
    TRIPS = EC // G
    Q = 2
    W = G // Q
    HB = (NB + 1) // 2
    with stage(nc) as (ctx, sem):
        sb = lambda n, s, d: ctx.enter_context(nc.sbuf_tensor(unique(n), s, d))
        src_i, dst_i = sb("src_i", [P, EC], I32), sb("dst_i", [P, EC], I32)
        local = sb("local", [P, 2, EC], F32)
        tile_of = sb("tile_of", [P, 2, EC], F32)
        tmp = sb("tmp_edge", [P, EC], F32)
        key = sb("key", [P, EC], F32)
        keyp = sb("keyp", [P, EC], F32)
        rec = sb("rec", [P, EC, 2], F32)
        blank = sb("blank", [P, NB, 2], F32)
        iota_nb = sb("iota_nb", [P, 2, HB], F16)
        ones_nb = sb("ones_nb", [P, P], BF16)
        before = sb("before", [P, P], BF16)
        rest = sb("rest", [P, P], BF16)
        hot = sb("hot", [P, G, 2, HB], BF16)
        junk = sb("junk", [P, 2, 2, HB], BF16)
        rank = sb("rank_ring", [P, G], F32)
        over = sb("over", [P, W], F32)
        pos = sb("pos", [P, W], F32)
        idx = sb("idx", [P, Q, W], U32)
        staged = sb("staged", [P, Q, W, 2], F32)
        count = [ctx.enter_context(nc.psum_tensor(unique(f"count{b}"), [P, 2, 512], F32)) for b in range(2)]

        edges_in, blank_out = sem("edges_in"), sem("blank_out")
        consts, prep, w_placed = sem("consts"), sem("prep"), sem("w_placed")
        dve_step, pos_step = sem("dve_step_a"), sem("pos_step")
        hot_ready, counted, rank_read = sem("hot_ready"), sem("counted"), sem("rank_read")
        idx_ready, stage_ready = sem("idx_ready"), sem("stage_ready")
        ranks_kept, ranked, edges_out = sem("ranks_kept"), sem("ranked"), sem("edges_out")
        pool_read, scatter_go = sem("pool_read"), sem("scatter_go")
        scattered = [sem(f"scattered{h}") for h in range(Q)]

        with nc.Block() as block:
            @block.sync
            def _(sp):
                sp.dma_start(src_i[:], g.src.rearrange("(p t) -> p t", p=P)).then_inc(edges_in, 16)
                sp.dma_start(dst_i[:], g.dst.rearrange("(p t) -> p t", p=P)).then_inc(edges_in, 16)
                sp.dma_start(tmp[:], g.edge_weight.rearrange("(p t) -> p t", p=P)).then_inc(edges_in, 16)
                sp.wait_ge(consts, 1)
                sp.dma_start(g.slots.rearrange("(p n) k -> p (n k)", p=P),
                             blank[:].rearrange("p n k -> p (n k)")).then_inc(blank_out, 16)
                sp.wait_ge(blank_out, 16)
                sp.dma_start(g.x_in[:], g.x.rearrange("(t p) d -> p t d", p=P)).then_inc(edges_out, 16)
                sp.wait_ge(ranked, 1)
                sp.dma_start(g.edge_rec, rec[:].rearrange("p t k -> p (t k)")).then_inc(edges_out, 16)
                sp.dma_start(g.edge_key, keyp[:]).then_inc(edges_out, 16)
                sp.dma_start(g.edge_rank, g.ranks[:]).then_inc(edges_out, 16)
                sp.wait_ge(edges_out, 64)

            @block.gpsimd
            def _(pool):
                pool.memset(blank[:, :, 0], 0.0)
                pool.memset(blank[:, :, 1], EMPTY).then_inc(consts, 1)
                pool.iota(iota_nb[:], pattern=[[HB, 2], [1, HB]], base=0, channel_multiplier=0,
                          allow_small_or_imprecise_dtypes=True).then_inc(consts, 1)
                pool.memset(ones_nb[:], 1.0).then_inc(pool_read, 1)
                pool.wait_ge(pool_read, 1)
                pool.affine_select(out=before[:], in_=ones_nb[:], compare_op=ALU.is_gt, fill=0.0, base=0,
                                   pattern=[[1, P]], channel_multiplier=-1)
                pool.affine_select(out=rest[:], in_=ones_nb[:], compare_op=ALU.is_ge, fill=0.0, base=0,
                                   pattern=[[-1, P]], channel_multiplier=1).then_inc(consts, 1)
                pool.wait_ge(blank_out, 16)

                bound = pool.to_reg(NB * P - 1)

                def scatter(i, h):
                    pool.wait_ge(idx_ready, i * Q + h + 1)
                    pool.wait_ge(stage_ready, i * Q + h + 1)
                    pool.sem_inc(scatter_go)
                    for u in range(W):
                        pool.indirect_dma_start(
                            out=g.slots, out_offset=bass.IndirectOffsetOnAxis(ap=idx[:, h, u:u + 1], axis=0),
                            in_=staged[:, h, u, :], in_offset=None, bounds_check=bound,
                            oob_is_err=False).then_inc(scattered[h], 16)

                with pool.Fori(0, TRIPS) as i:
                    for h in range(Q):
                        scatter(i, h)
                for h in range(Q):
                    pool.wait_ge(scattered[h], TRIPS * W * 16)

            @block.scalar
            def _(act):
                act.wait_ge(edges_in, 48)
                nc.scalar.copy(rec[:, :, 0], tmp[:]).then_inc(w_placed, 1)
                act.wait_ge(prep, 1)
                act.wait_ge(w_placed, 1)

                def fill_stage(i, h, first):
                    if not first:
                        act.wait_ge(scattered[h], i * (W * 16))
                    nc.scalar.copy(staged[:, h, :, :], rec[:, bass.ds(i * G + W * h, W), :]).then_inc(stage_ready, 1)

                for h in range(Q):
                    fill_stage(0, h, True)
                with act.Fori(1, TRIPS) as i:
                    for h in range(Q):
                        fill_stage(i, h, False)

            @block.vector
            def _(dve):
                step = Step(dve, dve_step)
                dve.wait_ge(edges_in, 48)
                dve.wait_ge(w_placed, 1)
                for k, ids in enumerate((src_i, dst_i)):
                    step(nc.vector.tensor_copy(local[:, k, :], ids[:]))
                    step(nc.vector.tensor_scalar(tmp[:], local[:, k, :], 1.0 / P, -(P // 2) / P, ALU.mult, ALU.add))
                    step(nc.vector.tensor_scalar_add(tile_of[:, k, :], tmp[:], ROUND))
                    step(nc.vector.tensor_scalar_add(tmp[:], tile_of[:, k, :], -ROUND))
                    step(nc.vector.tensor_copy(tile_of[:, k, :], tmp[:]))
                    step(nc.vector.scalar_tensor_tensor(out=tmp[:], in0=tile_of[:, k, :], scalar=float(-P),
                                                        in1=local[:, k, :], op0=ALU.mult, op1=ALU.add))
                    step(nc.vector.tensor_copy(local[:, k, :], tmp[:]))
                step(nc.vector.scalar_tensor_tensor(out=key[:], in0=tile_of[:, 0, :], scalar=float(T),
                                                    in1=tile_of[:, 1, :], op0=ALU.mult, op1=ALU.add))
                step(nc.vector.tensor_scalar_mul(keyp[:], key[:], float(P)))
                step(nc.vector.scalar_tensor_tensor(out=rec[:, :, 1], in0=local[:, 0, :], scalar=128.0,
                                                    in1=local[:, 1, :], op0=ALU.mult, op1=ALU.add))
                nc.vector.tensor_copy(g.spare[:P, 0:1], key[:, 0:1]).then_inc(prep, 1)
                dve.wait_ge(consts, 3)

                def one_hot(t, slot):
                    nc.vector.tensor_scalar(hot[:, slot, :, :], iota_nb[:], key[:, bass.ds(t, 1)], None,
                                            ALU.is_equal).then_inc(hot_ready, 1)

                def read_rank(t, u, t_before):
                    dve.wait_ge(counted, t + 1)
                    if t_before is not None:
                        dve.wait_ge(rank_read, t_before)
                    nc.vector.tensor_tensor_reduce(
                        out=junk[:, u % 2], in0=hot[:, u], in1=count[u % 2][:, :, 0:HB], scale=1.0,
                        scalar=0.0, op0=ALU.mult, op1=ALU.add, accum_out=rank[:, u:u + 1]).then_inc(rank_read, 1)

                def positions(i, h, first):
                    now = slice(W * h, W * h + W)
                    dve.wait_ge(rank_read, i * G + W * h + W)
                    nc.vector.tensor_copy(g.ranks[:, bass.ds(i * G + W * h, W)], rank[:, now]).then_inc(ranks_kept, 1)
                    nc.vector.tensor_scalar(over[:], rank[:, now], float(P), PAST, ALU.is_ge, ALU.mult).then_inc(pos_step, 1)
                    nc.vector.tensor_tensor(pos[:], rank[:, now], keyp[:, bass.ds(i * G + W * h, W)],
                                            ALU.add).then_inc(pos_step, 1)
                    dve.wait_ge(pos_step, (i * Q + h) * 2 + 2)
                    if not first:
                        dve.wait_ge(scattered[h], i * (W * 16))
                    nc.vector.tensor_tensor(idx[:, h, :], pos[:], over[:], ALU.add).then_inc(idx_ready, 1)

                def trip(i, first=False, last=False):
                    for u in range(G):
                        if not (last and u >= G - 2):
                            one_hot(i * G + u + 2, (u + 2) % G)
                        read_rank(i * G + u, u, None if first and u < 2 else i * G + u - 1)
                        if u % W == W - 1:
                            positions(i, u // W, first)

                one_hot(0, 0)
                one_hot(1, 1)
                trip(0, first=True)
                with dve.Fori(1, TRIPS - 1) as i:
                    trip(i)
                trip(TRIPS - 1, last=True)
                dve.wait_ge(ranks_kept, TRIPS * Q)
                dve.sem_inc(ranked)

            @block.tensor
            def _(pe):
                pe.wait_ge(consts, 3)

                def add(b, what, slot, start=False, inc=None):
                    for c in range(2):
                        mm = nc.tensor.matmul(count[b][:, c, 0:HB], what, hot[:, slot, c, :], start=start,
                                              stop=True, skip_group_check=True)
                    if inc is not None:
                        mm.then_inc(inc, 1)

                def tally(t, u, old=True, older=True):
                    if older:
                        pe.wait_ge(rank_read, t - 1)
                        add(u % 2, rest[:], (u - 2) % G)
                    if old:
                        add(u % 2, ones_nb[:], (u - 1) % G, start=not older)
                    pe.wait_ge(hot_ready, t + 1)
                    add(u % 2, before[:], u, start=not old, inc=counted)

                for u in range(G):
                    tally(u, u, old=u >= 1, older=u >= 2)
                with pe.Fori(1, TRIPS) as i:
                    for u in range(G):
                        tally(i * G + u, u)

GROUPS = [3, 3, 3, 3, 3, 3, 3, 4]
BASES = [sum(GROUPS[:j]) for j in range(len(GROUPS))]
NG = len(GROUPS)
EPS = 1e-5


def root(nc, act, value, out, ready, done):
    act.wait_ge(ready, 1)
    nc.scalar.activation(out, value, ACT.Sqrt).then_inc(done, 1)


def inverse_root(nc, dve, step, value, rooted, tmp, done):
    dve.wait_ge(done, 1)
    step(nc.vector.reciprocal(tmp, rooted))
    step(nc.vector.tensor_tensor(tmp, tmp, value, ALU.mult))
    step(nc.vector.tensor_tensor(tmp, tmp, rooted, ALU.add))
    step(nc.vector.tensor_scalar_mul(tmp, tmp, 0.5))
    step(nc.vector.reciprocal(value, tmp))


def layer_norm(nc, dve, step, x, xn, stats, small, rows_done, var_ready, rstd_ready, scale=None, shift=None,
               halfway=None):
    V = nc.vector
    one = lambda a, t: a[:, bass.ds(t, 1), :].rearrange("p a k -> p (a k)")
    FEW = 5
    with dve.Fori(0, T // FEW) as m:
        for u in range(FEW):
            V.bn_stats(one(stats, m * FEW + u), one(x, m * FEW + u)).then_inc(rows_done, 1)
    dve.wait_ge(rows_done, T)
    mean, var, dif, mean2 = (small[:, k, :] for k in range(4))
    step(V.tensor_tensor(mean, stats[:, :, 1], stats[:, :, 4], ALU.add))
    step(V.tensor_tensor(dif, stats[:, :, 1], stats[:, :, 4], ALU.subtract))
    step(V.tensor_tensor(var, stats[:, :, 2], stats[:, :, 5], ALU.add))
    step(V.tensor_scalar_mul(mean, mean, 0.5))
    step(V.tensor_tensor(dif, dif, dif, ALU.mult))
    step(V.tensor_scalar(dif, dif, 0.25, EPS, ALU.mult, ALU.add))
    V.scalar_tensor_tensor(out=var, in0=var, scalar=1.0 / D, in1=dif, op0=ALU.mult, op1=ALU.add).then_inc(var_ready, 1)
    inverse_root(nc, dve, step, var, mean2, dif, rstd_ready)
    with dve.Fori(0, T // FEW) as m:
        for u in range(FEW):
            t = m * FEW + u
            if scale is None:
                V.tensor_scalar(one(xn, t), one(x, t), mean[:, bass.ds(t, 1)], var[:, bass.ds(t, 1)], ALU.subtract,
                                ALU.mult).then_inc(rows_done, 1)
            else:
                V.scalar_tensor_tensor(out=one(xn, t), in0=one(x, t), scalar=mean[:, bass.ds(t, 1)], in1=scale,
                                       op0=ALU.subtract, op1=ALU.mult).then_inc(halfway, 1)
        if scale is not None:
            for u in range(FEW):
                t = m * FEW + u
                dve.wait_ge(halfway, t + 1)
                V.scalar_tensor_tensor(out=one(xn, t), in0=one(xn, t), scalar=var[:, bass.ds(t, 1)], in1=shift,
                                       op0=ALU.mult, op1=ALU.add).then_inc(rows_done, 1)
    dve.wait_ge(rows_done, 2 * T)


def split3(nc, step, whole, parts, left):
    step(nc.vector.tensor_copy(parts(0), whole))
    step(nc.vector.tensor_tensor(left, whole, parts(0), ALU.subtract))
    step(nc.vector.tensor_copy(parts(1), left))
    step(nc.vector.tensor_tensor(left, left, parts(1), ALU.subtract))
    step(nc.vector.tensor_copy(parts(2), left))


def normalise_input(nc, g):
    with stage(nc) as (ctx, sem):
        sb = lambda n, s, d: ctx.enter_context(nc.sbuf_tensor(unique(n), s, d))
        x, xn = g.x_in, sb("xn_in", [P, T, D], F32)
        stats, small = sb("stats0", [P, T, 6], F32), sb("small0", [P, 4, T], F32)
        left = sb("left0", [P, T, C0], F32)
        xn_out = sem("xn_out")
        rows_done, dve_step = sem("rows_done0"), sem("dve_step0")
        var_ready, rstd_ready = sem("var_ready0"), sem("rstd_ready0")
        with nc.Block() as block:
            @block.scalar
            def _(act):
                root(nc, act, small[:, 1, :], small[:, 3, :], var_ready, rstd_ready)

            @block.sync
            def _(sp):
                sp.wait_ge(rows_done, 2 * T)
                sp.dma_start(g.xn.rearrange("(t p) d -> p t d", p=P), xn[:]).then_inc(xn_out, 16)
                sp.wait_ge(xn_out, 16)

            @block.vector
            def _(dve):
                step = Step(dve, dve_step)
                layer_norm(nc, dve, step, x, xn, stats, small, rows_done, var_ready, rstd_ready)
                split3(nc, step, xn[:, :, 0:C0], lambda k: g.xparts[:, :, k, :], left[:])


def load_slots(nc, g):
    CH = NB // P
    with stage(nc) as (ctx, sem):
        sb = lambda n, s, d: ctx.enter_context(nc.sbuf_tensor(unique(n), s, d))
        raw = sb("raw_slots", [P, CH, P, 2], F32)
        turned = [ctx.enter_context(nc.psum_tensor(unique(f"turned{k}"), [P, 2, 512], F32)) for k in range(2)]
        code = sb("code", [P, NB], I32)
        field = sb("field", [P, 2, NB], I32)
        left = sb("left1", [P, NB], F32)
        whole = g.h[:].rearrange("p t c -> p (t c)")[:, 0:NB]
        slots_in, turned_done, dve_step = sem("slots_in"), sem("turned_done"), sem("dve_step1")
        with nc.Block() as block:
            @block.sync
            def _(sp):
                sp.dma_start(raw[:].rearrange("q c e k -> q c (e k)"),
                             g.slots.rearrange("(c q e) k -> q c (e k)", c=CH, q=P)).then_inc(slots_in, 16)

            @block.tensor
            def _(pe):
                pe.wait_ge(slots_in, 16)
                for k in range(2):
                    for c in range(CH):
                        out = turned[k][:, c // 4, (c % 4) * P:(c % 4 + 1) * P]
                        nc.tensor.transpose(out, raw[:, c, :, k], g.ident[0:P, 0:P]).then_inc(turned_done, 1)

            @block.vector
            def _(dve):
                step = Step(dve, dve_step)
                dve.wait_ge(turned_done, 2 * CH)
                for c, (lo, hi) in enumerate(((0, 4 * P), (4 * P, NB))):
                    step(nc.vector.tensor_copy(whole[:, lo:hi], turned[0][:, c, 0:hi - lo]))
                    step(nc.vector.tensor_copy(code[:, lo:hi], turned[1][:, c, 0:hi - lo]))
                step(nc.vector.tensor_scalar(field[:, 0, :], code[:], 7, None, ALU.logical_shift_right))
                step(nc.vector.tensor_scalar(field[:, 1, :], code[:], 127, None, ALU.bitwise_and))
                step(nc.vector.tensor_copy(g.slot_ids[:], field[:]))
                step(nc.vector.memset(g.slot_deg[:, :, 0:1], 1.0))
                split3(nc, step, whole, lambda k: g.slot_deg[:, :, 1 + k], left[:])
                step(nc.vector.tensor_copy(g.slot_w[:], g.slot_deg[:, :, 3]))


def build_blocks(nc, g):
    H = 3
    R = 2
    with stage(nc) as (ctx, sem):
        sb = lambda n, s, d: ctx.enter_context(nc.sbuf_tensor(unique(n), s, d))
        ps = lambda n, s: ctx.enter_context(nc.psum_tensor(unique(n), s, F32))
        src_hot = sb("src_hot", [P, H, 4, P], BF16)
        dst_hot = sb("dst_hot", [P, H, 4, 4, P], BF16)
        degs = sb("degs_now", [P, H, 4, 4], BF16)
        turned = sb("countT", [P, R, 4, P], BF16)
        zero = sb("zero_deg", [P, T * 4], BF16)
        strip = g.h[:].rearrange("p t c -> p (t c)")[:, 0:R * 4 * P].rearrange("p (r u e) -> p r u e", r=R, u=4)
        p_cw = [ps(f"p_cw{r}", [P, 4, 256]) for r in range(R)]
        p_t = [ps(f"p_t{r}", [P, 512]) for r in range(R)]
        p_deg, p_dyn = ps("p_deg", [P, 512]), ps("p_dyn", [P, 512])

        zeroed = sem("zeroed")
        hot_ready, two_ready, three_ready = sem("hot_ready_b"), sem("two_ready"), sem("three_ready")
        pool_go = sem("pool_go")
        blocks = sem("blocks")
        ev_c, ev_w, ev_t = sem("ev_c"), sem("ev_w"), sem("ev_t")
        spread = sem("spread")
        dyn_read = sem("dyn_read")
        strip_out = [sem(f"strip_out{r}") for r in range(R)]

        back = lambda j: H if j >= H else j + NG - max(i for i in range(NG) if i % H == j)

        with nc.Block() as block:
            @block.vector
            def _(dve):
                nc.vector.memset(zero[:], 0.0).then_inc(zeroed, 1)

                def make(s, j, n, first):
                    r, k = j % H, GROUPS[j]
                    if not (first and j < H):
                        dve.wait_ge(blocks, n - back(j) + 1)
                    nc.vector.tensor_copy(degs[:, r, 0:k, :], g.slot_deg[:, bass.ds(s * T + BASES[j], k), :])
                    for u in range(k):
                        b = s * T + BASES[j] + u
                        node = lambda i: g.slot_ids[:, i, bass.ds(b, 1)]
                        nc.vector.tensor_scalar(dst_hot[:, r, u, 0, :], g.iota[:P, 0:P], node(1), None, ALU.is_equal)
                        ins = nc.vector.tensor_scalar(src_hot[:, r, u, :], g.iota[:P, 0:P], node(0), None, ALU.is_equal)
                    ins.then_inc(hot_ready, 1)

                def evacuate(s, j, n, first):
                    w = GROUPS[j] * P
                    dve.wait_ge(blocks, n + 1)
                    if not (first and j < R):
                        dve.wait_ge(spread, n - R + 1)
                    nc.vector.tensor_copy(turned[:, j % R, 0:GROUPS[j], :].rearrange("p u e -> p (u e)"),
                                          p_t[j % R][:P, 0:w]).then_inc(ev_t, 1)

                def read_dyn(s, count):
                    dve.wait_ge(spread, count * NG)
                    nc.vector.tensor_reduce(g.dyn[:, bass.ds(s, 1), :].rearrange("p a k -> p (a k)"),
                                            p_dyn[:P, 0:3 * C0].rearrange("p (k c) -> p c k", k=3), AX.X,
                                            ALU.add).then_inc(dyn_read, 1)

                def whole(s, first=False, last=False):
                    for j in range(NG):
                        n = s * NG + j
                        if j + 1 < NG:
                            make(s, j + 1, n + 1, first)
                        elif not last:
                            make(s + 1, 0, n + 1, False)
                        if j == 0 and not first:
                            evacuate(s - 1, NG - 1, n - 1, False)
                        elif j > 0:
                            evacuate(s, j - 1, n - 1, first)
                        if j == 1 and not first:
                            read_dyn(s - 1, s)

                make(0, 0, 0, True)
                whole(0, first=True)
                with dve.Fori(1, T - 1) as s:
                    whole(s)
                whole(T - 1, last=True)
                evacuate(T - 1, NG - 1, T * NG - 1, False)
                read_dyn(T - 1, T)
                dve.wait_ge(blocks, T * NG)
                nc.vector.tensor_copy(g.deg[:].rearrange("p t k -> p (t k)"), p_deg[:P, 0:T * 4])

            @block.gpsimd
            def _(pool):
                with pool.Fori(0, T) as s:
                    for j in range(NG):
                        r, k = j % H, GROUPS[j]
                        pool.wait_ge(hot_ready, s * NG + j + 1)
                        pool.sem_inc(pool_go)
                        for i in range(1, 3):
                            ins = nc.gpsimd.tensor_tensor(
                                dst_hot[:, r, 0:k, i, :], dst_hot[:, r, 0:k, 0, :],
                                g.slot_deg[:, bass.ds(s * T + BASES[j], k), i:i + 1].to_broadcast([P, k, P]), ALU.mult)
                        ins.then_inc(two_ready, 1)

            @block.scalar
            def _(act):
                def weigh(s, j, n):
                    act.wait_ge(hot_ready, n + 1)
                    for u in range(GROUPS[j]):
                        ins = nc.scalar.activation(dst_hot[:, j % H, u, 3, :], dst_hot[:, j % H, u, 0, :], ACT.Copy,
                                                   scale=g.slot_w[:, bass.ds(s * T + BASES[j] + u, 1)])
                    ins.then_inc(three_ready, 1)

                def evacuate(s, j, n, first):
                    r, k, lo = j % R, GROUPS[j], BASES[j] * P
                    act.wait_ge(blocks, n + 1)
                    nc.scalar.copy(g.counts[:, bass.ds(s, 1), lo:lo + k * P].rearrange("p a (u e) -> p (a u) e", e=P),
                                   p_cw[r][:, 0:k, 0:P]).then_inc(ev_c, 1)
                    if not (first and j < R):
                        act.wait_ge(strip_out[r], (s * (NG // R) + j // R) * 16)
                    nc.scalar.copy(strip[:, r, 0:k, :], p_cw[r][:, 0:k, P:2 * P]).then_inc(ev_w, 1)

                def whole(s, first=False, last=False):
                    for j in range(NG):
                        if j + 1 < NG:
                            weigh(s, j + 1, s * NG + j + 1)
                        elif not last:
                            weigh(s + 1, 0, s * NG + NG)
                        if j > 0:
                            evacuate(s, j - 1, s * NG + j - 1, first)
                        elif not first:
                            evacuate(s - 1, NG - 1, s * NG - 1, False)

                weigh(0, 0, 0)
                whole(0, first=True)
                with act.Fori(1, T - 1) as s:
                    whole(s)
                whole(T - 1, last=True)
                evacuate(T - 1, NG - 1, T * NG - 1, False)

            @block.sync
            def _(sp):
                with sp.Fori(0, T) as s:
                    for j in range(NG):
                        r, k, lo = j % R, GROUPS[j], BASES[j] * P
                        sp.wait_ge(ev_w, s * NG + j + 1)
                        sp.dma_start(g.weights[bass.ds(s * P, P), lo:lo + k * P],
                                     strip[:, r, 0:k, :].rearrange("p u e -> p (u e)")).then_inc(strip_out[r], 16)
                for r in range(R):
                    sp.wait_ge(strip_out[r], T * NG // R * 16)

            @block.tensor
            def _(pe):
                pe.wait_ge(zeroed, 1)
                nc.tensor.matmul(p_deg[:P, 0:T * 4], g.iota[:P, 0:P], zero[:], start=True, stop=True,
                                 skip_group_check=True)

                def products(s, j, n, first):
                    r, h = j % R, j % H
                    pe.wait_ge(hot_ready, n + 1)
                    if not (first and j < R):
                        pe.wait_ge(ev_t, n - R + 1)
                    for u in range(GROUPS[j]):
                        d = BASES[j] + u
                        nc.tensor.matmul(p_deg[:P, d * 4:d * 4 + 4], dst_hot[:, h, u, 0, :], degs[:, h, u, :],
                                         start=False, stop=True, skip_group_check=True)
                        nc.tensor.matmul(p_t[r][:P, u * P:(u + 1) * P], dst_hot[:, h, u, 0, :], src_hot[:, h, u, :],
                                         start=True, stop=True)
                    if not (first and j < R):
                        pe.wait_ge(ev_c, n - R + 1)
                        pe.wait_ge(ev_w, n - R + 1)
                    pe.wait_ge(two_ready, n + 1)
                    pe.wait_ge(three_ready, n + 1)
                    for u in range(GROUPS[j]):
                        nc.tensor.matmul(p_cw[r][:, u, 0:2 * P], src_hot[:, h, u, :],
                                         dst_hot[:, h, u, 0:2, :].rearrange("p k e -> p (k e)"), start=True, stop=False,
                                         skip_group_check=True)
                        for k in range(2, 4):
                            mm = nc.tensor.matmul(p_cw[r][:, u, P:2 * P], src_hot[:, h, u, :], dst_hot[:, h, u, k, :],
                                                  start=False, stop=k == 3, skip_group_check=True)
                    mm.then_inc(blocks, 1)

                def spread_group(j, n, wait_dyn):
                    pe.wait_ge(ev_t, n + 1)
                    if wait_dyn is not None:
                        pe.wait_ge(dyn_read, wait_dyn)
                    for u in range(GROUPS[j]):
                        d = BASES[j] + u
                        mm = nc.tensor.matmul(p_dyn[:P, 0:3 * C0], turned[:, j % R, u, :],
                                              g.xparts[:, d, :, :].rearrange("p k c -> p (k c)"), start=(d == 0),
                                              stop=(d == T - 1))
                    mm.then_inc(spread, 1)

                def whole(s, first=False):
                    for j in range(NG):
                        n = s * NG + j
                        products(s, j, n, first)
                        if j == 0 and not first:
                            spread_group(NG - 1, n - 1, None)
                        elif j > 0:
                            spread_group(j - 1, n - 1, s if j == 1 and not first else None)

                whole(0, first=True)
                with pe.Fori(1, T) as s:
                    whole(s)
                spread_group(NG - 1, T * NG - 1, None)

F = D // 128
QUADS = [(t, min(4, T - t)) for t in range(0, T, 4)]


def turn_tiles(nc, pe, rows, width, psum, ident, wait_free, turned, rows_done=None, before=0,
               then=None):
    n = 0
    for t0, k in QUADS:
        if rows_done is not None:
            pe.wait_ge(rows_done, before + t0 + k)
        for lo in range(0, width, 128):
            m = min(128, width - lo)
            if n >= len(psum):
                pe.wait_ge(wait_free, n - len(psum) + 1)
            for u in range(k):
                mm = nc.tensor.transpose(psum[n % len(psum)][0:m, u * P:(u + 1) * P], rows[:, t0 + u, lo:lo + m],
                                         ident[0:P, 0:P])
            mm.then_inc(turned, 1)
            n += 1
        if then is not None and t0 > 0:
            then(t0 // 4 - 1)
    if then is not None:
        then(len(QUADS) - 1)


def static_degrees(nc, g):
    with stage(nc) as (ctx, sem):
        sb = lambda n, s, d: ctx.enter_context(nc.sbuf_tensor(unique(n), s, d))
        rooted, tmp = sb("rooted_s", [P, T], F32), sb("tmp_s", [P, T], F32)
        loaded, deg_ready, root_done, dve_step = sem("loaded_s"), sem("deg_ready"), sem("root_done_s"), sem("dve_step_s")
        with nc.Block() as block:
            @block.sync
            def _(sp):
                sp.dma_start(g.h[:], g.xn.rearrange("(t p) d -> p t d", p=P)[:, :, 0:C0]).then_inc(loaded, 16)
                sp.dma_start(g.w_static[:], g.L0_gnn_W_static.rearrange("k i o -> i k o")).then_inc(loaded, 16)
                sp.dma_start(g.b_static[:], g.L0_gnn_b_static[None, :, :].to_broadcast([P, 3, C0])).then_inc(loaded, 16)
                sp.wait_ge(loaded, 48)

            @block.scalar
            def _(act):
                root(nc, act, g.dinv_s[:], rooted[:], deg_ready, root_done)

            @block.vector
            def _(dve):
                step = Step(dve, dve_step)
                nc.vector.tensor_scalar(g.dinv_s[:], g.deg[:, :, 0], 1.0, 1e-12, ALU.add, ALU.max).then_inc(deg_ready, 1)
                inverse_root(nc, dve, step, g.dinv_s[:], rooted[:], tmp[:], root_done)


def static_messages(nc, g):
    i = 0
    with stage(nc) as (ctx, sem):
        sb = lambda n, s, d: ctx.enter_context(nc.sbuf_tensor(unique(n), s, d))
        ps = lambda n: ctx.enter_context(nc.psum_tensor(unique(n), [128, 512], F32))
        hT = sb("hT", [C0, 2, 4 * P], F32)
        scaled = sb("scaled", [P, T, C0], F32)
        p_turn, p_mul = [ps(f"p_turn{b}") for b in range(2)], [ps(f"p_mul{b}") for b in range(2)]
        turned, turn_read, multiplied, mul_read = sem("turned_s"), sem("turn_read"), sem("multiplied"), sem("mul_read")
        dve_step = sem("dve_step_s")
        NQ = len(QUADS)

        with nc.Block() as block:
            @block.scalar
            def _(act):
                for q, (t0, k) in enumerate(QUADS):
                    act.wait_ge(turned, q + 1)
                    if q >= 2:
                        act.wait_ge(multiplied, q - 1)
                    nc.scalar.copy(hT[:, q % 2, 0:k * P], p_turn[q % 2][0:C0, 0:k * P]).then_inc(turn_read, 1)

            @block.tensor
            def _(pe):
                def turn(q):
                    t0, k = QUADS[q]
                    if q >= 2:
                        pe.wait_ge(turn_read, q - 1)
                    for u in range(k):
                        mm = nc.tensor.transpose(p_turn[q % 2][0:C0, u * P:(u + 1) * P], g.h[:, t0 + u, :],
                                                 g.ident[0:P, 0:P])
                    mm.then_inc(turned, 1)

                def multiply(q):
                    t0, k = QUADS[q]
                    pe.wait_ge(turn_read, q + 1)
                    if q >= 2:
                        pe.wait_ge(mul_read, q - 1)
                    for u in range(k):
                        mm = nc.tensor.matmul(p_mul[q % 2][0:P, u * C0:(u + 1) * C0], hT[:, q % 2, u * P:(u + 1) * P],
                                              g.w_static[:, i, :], start=True, stop=True)
                    mm.then_inc(multiplied, 1)

                turn(0)
                for q in range(NQ):
                    if q + 1 < NQ:
                        turn(q + 1)
                    multiply(q)

            @block.vector
            def _(dve):
                step = Step(dve, dve_step)
                for q, (t0, k) in enumerate(QUADS):
                    dve.wait_ge(multiplied, q + 1)
                    nc.vector.tensor_tensor(
                        scaled[:, t0:t0 + k, :], p_mul[q % 2][0:P, 0:k * C0].rearrange("p (u c) -> p u c", u=k),
                        g.dinv_s[:, t0:t0 + k, None].to_broadcast([P, k, C0]), ALU.mult).then_inc(mul_read, 1)
                    dve.wait_ge(mul_read, q + 1)
                    now = slice(t0, t0 + k)
                    own, whole = g.own[:, now, :], scaled[:, now, :]
                    split3(nc, step, whole, lambda j: g.parts[0][:, now, j, :], own)
                    step(nc.vector.tensor_tensor(own, whole, g.dinv_s[:, now, None].to_broadcast([P, k, C0]), ALU.mult))
                    step(nc.vector.tensor_tensor(own, own, g.b_static[:, i:i + 1, :].to_broadcast([P, k, C0]), ALU.add))


def static_sums(nc, g, i):
    go_on = i < 2
    now, after = g.parts[i % 2], g.parts[(i + 1) % 2]
    with stage(nc) as (ctx, sem):
        sb = lambda n, s, d: ctx.enter_context(nc.sbuf_tensor(unique(n), s, d))
        ps = lambda n: [ctx.enter_context(nc.psum_tensor(unique(f"{n}{b}"), [128, 512], F32)) for b in range(2)]
        summed, h_now = sb("summed", [P, 2, 2, C0], F32), sb("h_now", [P, 2, C0], F32)
        hT, scaled, left = sb("hT_s", [C0, 2, P], F32), sb("scaled_s", [P, 2, C0], F32), sb("left_s", [P, C0], F32)
        p_agg, p_turn, p_mul = ps("p_agg"), ps("p_turn_s"), ps("p_mul_s")
        aggregated, agg_read, before_relu, h_ready = sem("aggregated"), sem("agg_read"), sem("before_relu"), sem("h_ready")
        h_turned, turn_read, multiplied = sem("h_turned_s"), sem("turn_read_s"), sem("multiplied_s")
        scaled_ready, split_step = sem("scaled_ready"), sem("split_step")
        SPLIT = 6
        row = lambda a, t: a[:, bass.ds(t, 1), :].rearrange("p a c -> p (a c)")

        def over_tiles(body):
            for d in range(T + 3 if go_on else T):
                body(d, d % 2)

        within = lambda n: 0 <= n < T
        again = lambda n: n >= 2

        with nc.Block() as block:
            @block.tensor
            def _(pe):
                def aggregate(d, b):
                    if again(d):
                        pe.wait_ge(agg_read, d - 1)
                    for s in range(T):
                        mm = nc.tensor.matmul(p_agg[b][0:P, 0:3 * C0], g.counts[:, s, d * P:(d + 1) * P],
                                              now[:, s, :, :].rearrange("p k c -> p (k c)"),
                                              start=(s == 0), stop=(s == T - 1))
                    mm.then_inc(aggregated, 1)

                def multiply(n, b):
                    pe.wait_ge(turn_read, n + 1)
                    if again(n):
                        pe.wait_ge(scaled_ready, n - 1)
                    nc.tensor.matmul(p_mul[b][0:P, 0:C0], hT[:, b, :], g.w_static[:, i + 1, :], start=True,
                                     stop=True).then_inc(multiplied, 1)

                def turn(n, b):
                    pe.wait_ge(h_ready, n + 1)
                    if again(n):
                        pe.wait_ge(turn_read, n - 1)
                    nc.tensor.transpose(p_turn[b][0:C0, 0:P], h_now[:, b, :], g.ident[0:P, 0:P]).then_inc(h_turned, 1)

                def body(d, b):
                    if within(d):
                        aggregate(d, b)
                    if go_on and within(d - 2):
                        multiply(d - 2, b)
                    if go_on and within(d - 1):
                        turn(d - 1, 1 - b)

                over_tiles(body)

            @block.scalar
            def _(act):
                def scale(n, b):
                    act.wait_ge(multiplied, n + 1)
                    if again(n):
                        act.wait_ge(split_step, (n - 1) * SPLIT)
                    nc.scalar.activation(scaled[:, b, :], p_mul[b][0:P, 0:C0], ACT.Copy,
                                         scale=g.dinv_s[:, bass.ds(n, 1)]).then_inc(scaled_ready, 1)

                def take_turned(n, b):
                    act.wait_ge(h_turned, n + 1)
                    if again(n):
                        act.wait_ge(multiplied, n - 1)
                    nc.scalar.copy(hT[:, b, :], p_turn[b][0:C0, 0:P]).then_inc(turn_read, 1)

                def body(d, b):
                    if within(d - 2):
                        scale(d - 2, b)
                    if within(d - 1):
                        take_turned(d - 1, 1 - b)

                if go_on:
                    over_tiles(body)

            @block.vector
            def _(dve):
                V = nc.vector

                def update(d, b):
                    dve.wait_ge(aggregated, d + 1)
                    V.tensor_reduce(summed[:, b, 0, :], p_agg[b][0:P, 0:3 * C0].rearrange("p (k c) -> p c k", k=3), AX.X,
                                    ALU.add).then_inc(agg_read, 1)
                    dve.wait_ge(agg_read, d + 1)
                    V.scalar_tensor_tensor(out=summed[:, b, 1, :], in0=summed[:, b, 0, :],
                                           scalar=g.dinv_s[:, bass.ds(d, 1)], in1=row(g.own, d), op0=ALU.mult,
                                           op1=ALU.add).then_inc(before_relu, 1)
                    dve.wait_ge(before_relu, d + 1)
                    if go_on and again(d):
                        dve.wait_ge(h_turned, d - 1)
                    V.tensor_scalar_max(h_now[:, b, :] if go_on else row(g.h, d), summed[:, b, 1, :],
                                        0.0).then_inc(h_ready, 1)

                def split(n, b):
                    whole, c = scaled[:, b, :], [0]

                    def step(ins):
                        c[0] += 1
                        ins.then_inc(split_step, 1)
                        dve.wait_ge(split_step, n * SPLIT + c[0])

                    dve.wait_ge(scaled_ready, n + 1)
                    split3(nc, step, whole, lambda k: after[:, n, k, :], left[:])
                    V.scalar_tensor_tensor(out=g.own[:, n, :], in0=whole, scalar=g.dinv_s[:, n:n + 1],
                                           in1=g.b_static[:, i + 1, :], op0=ALU.mult, op1=ALU.add).then_inc(split_step, 1)

                def body(d, b):
                    if within(d):
                        update(d, b)
                    if go_on and within(d - 3):
                        split(d - 3, 1 - b)

                over_tiles(body)
                dve.wait_ge(h_ready, T)


def first_gnn_out(nc, g):
    with stage(nc) as (ctx, sem):
        sb = lambda n, s, d: ctx.enter_context(nc.sbuf_tensor(unique(n), s, d))
        ps = lambda n: ctx.enter_context(nc.psum_tensor(unique(n), [128, 512], F32))
        xn, xT = sb("xn_g", [P, T, D], F32), sb("xT_g", [128, F, N], F32)
        HID = 128
        hid = sb("hid_g", [HID, N], F32)
        x = g.xr
        w1, w2, wa = sb("w1_g", [128, F, HID], F32), sb("w2_g", [HID, C0], F32), sb("wa_g", [128, F, D], F32)
        b1, b2, ba = sb("b1_g", [HID, 1], F32), sb("b2_g", [P, C0], F32), sb("ba_g", [P, D], F32)
        factor = sb("factor_g", [P, T, C0], F32)
        psum = [ps(f"p_g{b}") for b in range(8)]
        loaded, x_in, w_in = sem("xn_in_g"), sem("x_in_g"), sem("w_in_g")
        turned, turn_read = sem("turned_g"), sem("turn_read_g")
        hid_done, hid_ready = sem("hid_done"), sem("hid_ready")
        ew_done, ew_read, dve_step = sem("ew_done"), sem("ew_read"), sem("dve_step_g")
        summed_ready, turned2, turn2_read = sem("summed_ready"), sem("turned2_g"), sem("turn2_read_g")
        out_done, out_read = sem("out_done_g"), sem("out_read_g")
        NQ = len(QUADS)
        PAIRS = [(t, min(2, T - t)) for t in range(0, T, 2)]

        with nc.Block() as block:
            @block.sync
            def _(sp):
                sp.dma_start(xn[:], g.xn.rearrange("(t p) d -> p t d", p=P)).then_inc(loaded, 16)
                sp.dma_start(w1[:], g.L0_gnn_W1.rearrange("(f i) o -> i f o", i=128)).then_inc(w_in, 16)
                sp.dma_start(b1[:], g.L0_gnn_b1[:, None]).then_inc(w_in, 16)
                sp.dma_start(w2[:], g.L0_gnn_W2).then_inc(w_in, 16)
                sp.dma_start(b2[:], g.L0_gnn_b2[None, :].to_broadcast([P, C0])).then_inc(w_in, 16)
                sp.dma_start(wa[:], g.L0_gnn_W_aggr.rearrange("(f i) o -> i f o", i=128)).then_inc(w_in, 16)
                sp.dma_start(ba[:], g.L0_gnn_b_aggr[None, :].to_broadcast([P, D])).then_inc(w_in, 16)
                sp.dma_start(x[:], g.x.rearrange("(t p) d -> p t d", p=P)).then_inc(x_in, 16)

            @block.tensor
            def _(pe):
                pe.wait_ge(loaded, 16)
                turn_tiles(nc, pe, xn, D, psum[0:4], g.ident, turn_read, turned)
                pe.wait_ge(w_in, 96)
                for q, (t0, k) in enumerate(QUADS):
                    cols = slice(t0 * P, (t0 + k) * P)
                    pe.wait_ge(turn_read, 2 * q + 2)
                    if q >= 2:
                        pe.wait_ge(hid_ready, q - 1)
                    for f in range(F):
                        mm = nc.tensor.matmul(psum[4 + q % 2][0:HID, 0:k * P], w1[:, f, :], xT[:, f, cols],
                                              start=(f == 0), stop=(f == F - 1))
                    mm.then_inc(hid_done, 1)
                for q, (t0, k) in enumerate(QUADS):
                    pe.wait_ge(hid_ready, q + 1)
                    if q >= 2:
                        pe.wait_ge(ew_read, q - 1)
                    for u in range(k):
                        mm = nc.tensor.matmul(psum[6 + q % 2][0:P, u * C0:(u + 1) * C0],
                                              hid[:, (t0 + u) * P:(t0 + u + 1) * P], w2[:], start=True, stop=True)
                    mm.then_inc(ew_done, 1)
                pe.wait_ge(summed_ready, 1)
                turn_tiles(nc, pe, g.h, C0, psum[0:2], g.ident, turn2_read, turned2)
                pe.wait_ge(turn2_read, NQ)
                for n, (t0, k) in enumerate(PAIRS):
                    if n >= 4:
                        pe.wait_ge(out_read, n - 3)
                    for u in range(k):
                        for f in range(F):
                            mm = nc.tensor.matmul(psum[2 + n % 4][0:P, u * D:(u + 1) * D],
                                                  xT[:, f, (t0 + u) * P:(t0 + u + 1) * P], wa[:, f, :],
                                                  start=(f == 0), stop=(f == F - 1))
                    mm.then_inc(out_done, 1)

            @block.scalar
            def _(act):
                n = 0
                for t0, k in QUADS:
                    for f in range(F):
                        act.wait_ge(turned, n + 1)
                        nc.scalar.copy(xT[:, f, t0 * P:(t0 + k) * P], psum[n % 4][:, 0:k * P]).then_inc(turn_read, 1)
                        n += 1
                act.wait_ge(w_in, 96)
                for q, (t0, k) in enumerate(QUADS):
                    act.wait_ge(hid_done, q + 1)
                    nc.scalar.activation(hid[:, t0 * P:(t0 + k) * P], psum[4 + q % 2][0:HID, 0:k * P], ACT.Gelu,
                                         bias=b1[:, 0:1]).then_inc(hid_ready, 1)
                for q, (t0, k) in enumerate(QUADS):
                    act.wait_ge(turned2, q + 1)
                    nc.scalar.copy(xT[0:C0, 0, t0 * P:(t0 + k) * P], psum[q % 2][0:C0, 0:k * P]).then_inc(turn2_read, 1)

            @block.vector
            def _(dve):
                step = Step(dve, dve_step)
                dve.wait_ge(w_in, 96)
                dve.wait_ge(x_in, 16)
                step(nc.vector.tensor_tensor(x[:], x[:], ba[:, None, :].to_broadcast([P, T, D]), ALU.add))
                for q, (t0, k) in enumerate(QUADS):
                    dve.wait_ge(ew_done, q + 1)
                    nc.vector.tensor_tensor(factor[:, t0:t0 + k, :],
                                            psum[6 + q % 2][0:P, 0:k * C0].rearrange("p (u c) -> p u c", u=k),
                                            b2[:, None, :].to_broadcast([P, k, C0]), ALU.add).then_inc(ew_read, 1)
                dve.wait_ge(ew_read, NQ)
                step(nc.vector.tensor_tensor(factor[:], factor[:], g.dyn[:], ALU.mult))
                nc.vector.tensor_tensor(g.h[:], g.h[:], factor[:], ALU.add).then_inc(summed_ready, 1)
                for n, (t0, k) in enumerate(PAIRS):
                    dve.wait_ge(out_done, n + 1)
                    nc.vector.tensor_tensor(x[:, t0:t0 + k, :],
                                            psum[2 + n % 4][0:P, 0:k * D].rearrange("p (u c) -> p u c", u=k),
                                            x[:, t0:t0 + k, :], ALU.add).then_inc(out_read, 1)


def count_rounds(nc, g):
    with stage(nc) as (ctx, sem):
        sb = lambda n, s, d: ctx.enter_context(nc.sbuf_tensor(unique(n), s, d))
        most, row, one = sb("most", [P, 1], F32), sb("row_x", [1, P], F32), sb("one_x", [1, 2], F32)
        p_row = ctx.enter_context(nc.psum_tensor(unique("p_row_x"), [128, 512], F32))
        step_x, most_ready, row_done = sem("step_x"), sem("most_ready"), sem("row_done")
        with nc.Block() as block:
            @block.vector
            def _(dve):
                step = Step(dve, step_x)
                V = nc.vector
                V.tensor_reduce(most[:], g.ranks[:], AX.X, ALU.max).then_inc(most_ready, 1)
                dve.wait_ge(row_done, 1)
                step(V.tensor_reduce(one[:, 0:1], p_row[0:1, 0:P], AX.X, ALU.max))
                step(V.tensor_scalar(one[:, 1:2], one[:, 0:1], 1.0 / P, -(P // 2) / P, ALU.mult, ALU.add))
                step(V.tensor_scalar_add(one[:, 0:1], one[:, 1:2], ROUND))
                step(V.tensor_scalar_add(one[:, 1:2], one[:, 0:1], -ROUND))
                step(V.tensor_scalar_add(g.rounds[:], one[:, 1:2], 1.0))
                step(V.memset(g.offset[:], 0.0))

            @block.tensor
            def _(pe):
                pe.wait_ge(most_ready, 1)
                nc.tensor.transpose(p_row[0:1, 0:P], most[:], g.ident[0:P, 0:P]).then_inc(row_done, 1)


def clear_high(nc, g):
    with stage(nc) as (ctx, sem):
        zero = ctx.enter_context(nc.sbuf_tensor(unique("zero_h"), [P, N], BF16))
        zeroed, stored = sem("zeroed_h"), sem("stored_h")
        with nc.Block() as block:
            @block.vector
            def _(dve):
                nc.vector.memset(zero[:], 0.0).then_inc(zeroed, 1)

            @block.sync
            def _(sp):
                sp.wait_ge(zeroed, 1)
                for t in range(T):
                    sp.dma_start(g.high[t * P:(t + 1) * P, :], zero[:]).then_inc(stored, 16)
                sp.wait_ge(stored, 16 * T)


def scatter_again(nc, g):
    with stage(nc) as (ctx, sem):
        sb = lambda n, s, d: ctx.enter_context(nc.sbuf_tensor(unique(n), s, d))
        rec, keyp, rank = sb("rec_x", [P, EC, 2], F32), sb("keyp_x", [P, EC], F32), sb("rank_x", [P, EC], F32)
        low, at = sb("low_x", [P, EC], F32), sb("at_x", [P, EC], U32)
        blank = sb("blank_x", [P, NB, 2], F32)
        idx, staged = sb("idx_x", [P, 4], U32), sb("staged_x", [P, 4, 2], F32)
        edges_in, blanked, blank_out, step_x = sem("edges_in_x"), sem("blanked_x"), sem("blank_out_x"), sem("step_y")
        at_ready, four_ready, four_out, go = sem("at_ready"), sem("four_ready"), sem("four_out"), sem("go_x")
        with nc.Block() as block:
            @block.sync
            def _(sp):
                sp.dma_start(rec[:].rearrange("p t k -> p (t k)"), g.edge_rec).then_inc(edges_in, 16)
                sp.dma_start(keyp[:], g.edge_key).then_inc(edges_in, 16)
                sp.dma_start(rank[:], g.edge_rank).then_inc(edges_in, 16)
                sp.wait_ge(blanked, 2)
                sp.dma_start(g.slots.rearrange("(p n) k -> p (n k)", p=P),
                             blank[:].rearrange("p n k -> p (n k)")).then_inc(blank_out, 16)

            @block.vector
            def _(dve):
                step = Step(dve, step_x)
                V = nc.vector
                V.memset(blank[:, :, 0], 0.0).then_inc(blanked, 1)
                V.memset(blank[:, :, 1], EMPTY).then_inc(blanked, 1)
                step(V.tensor_scalar_add(g.offset[:], g.offset[:], float(P)))
                dve.wait_ge(edges_in, 48)
                step(V.tensor_scalar(rank[:], rank[:], g.offset[:, 0:1], None, ALU.subtract))
                step(V.tensor_tensor(keyp[:], keyp[:], rank[:], ALU.add))
                step(V.tensor_scalar(low[:], rank[:], 0.0, PAST, ALU.is_lt, ALU.mult))
                step(V.tensor_tensor(keyp[:], keyp[:], low[:], ALU.add))
                step(V.tensor_scalar(low[:], rank[:], float(P), PAST, ALU.is_ge, ALU.mult))
                V.tensor_tensor(at[:], keyp[:], low[:], ALU.add).then_inc(at_ready, 1)
                dve.wait_ge(at_ready, 1)

                def four(i):
                    V.tensor_copy(idx[:], at[:, bass.ds(i * 4, 4)])
                    V.tensor_copy(staged[:], rec[:, bass.ds(i * 4, 4), :]).then_inc(four_ready, 1)

                four(0)
                with dve.Fori(1, EC // 4) as i:
                    dve.wait_ge(four_out, i * 64)
                    four(i)

            @block.gpsimd
            def _(pool):
                bound = pool.to_reg(NB * P - 1)
                pool.wait_ge(blank_out, 16)
                with pool.Fori(0, EC // 4) as i:
                    pool.wait_ge(four_ready, i + 1)
                    pool.sem_inc(go)
                    for u in range(4):
                        pool.indirect_dma_start(
                            out=g.slots, out_offset=bass.IndirectOffsetOnAxis(ap=idx[:, u:u + 1], axis=0),
                            in_=staged[:, u, :], in_offset=None, bounds_check=bound,
                            oob_is_err=False).then_inc(four_out, 16)
                pool.wait_ge(four_out, EC * 16)


def add_blocks(nc, g):
    with stage(nc) as (ctx, sem):
        sb = lambda n, s, d: ctx.enter_context(nc.sbuf_tensor(unique(n), s, d))
        ps = lambda n: ctx.enter_context(nc.psum_tensor(unique(n), [P, 512], F32))
        src16, dst16, turned = sb("src16_x", [P, P], BF16), sb("dst16_x", [P, P], BF16), sb("turned_x", [P, P], BF16)
        src32, dst32 = sb("src32_x", [P, P], F32), sb("dst32_x", [P, P], F32)
        weight, high = sb("weight_x", [P, P], F32), sb("high_x", [P, P], BF16)
        lane, xrow = sb("lane_x", [P, 3], F32), sb("xrow_x", [P, 3 * C0], BF16)
        degs = sb("degs_x", [P, 4], BF16)
        v, carry = sb("v_x", [P, P], F32), sb("carry_x", [P, P], F32)
        p_w, p_c, p_t, p_deg, p_dyn = ps("p_w_x"), ps("p_c_x"), ps("p_t_x"), ps("p_deg_x"), ps("p_dyn_x")
        read, held, hot, product = sem("read_x"), sem("held_x"), sem("hot_x"), sem("product_x")
        turned_ready, dyn_done, updated, stored, chain = (
            sem(k) for k in ("turned_ready_x", "dyn_done_x", "updated_x", "stored_x", "chain_x"))
        CHAIN = 9

        def buckets(engine, body):
            with engine.Fori(0, T) as s:
                with engine.Fori(0, T) as d:
                    body(s, d, s * T + d)

        with nc.Block() as block:
            @block.sync
            def _(sp):
                def body(s, d, n):
                    at = bass.ds(s * P, P), bass.ds(d * P, P)
                    sp.dma_start(weight[:], g.weights[at[0], at[1]]).then_inc(read, 16)
                    sp.dma_start(high[:], g.high[at[0], at[1]]).then_inc(read, 16)
                    sp.wait_ge(updated, n + 1)
                    sp.sem_inc(held)
                    sp.dma_start(g.weights[at[0], at[1]], weight[:]).then_inc(stored, 16)
                    sp.dma_start(g.high[at[0], at[1]], high[:]).then_inc(stored, 16)
                    sp.wait_ge(stored, (n + 1) * 32)
                    sp.sem_inc(held)
                buckets(sp, body)

            @block.vector
            def _(dve):
                V = nc.vector
                flat = lambda a: a.rearrange("p a c -> p (a c)")

                def body(s, d, n):
                    c = [0]

                    def step(ins):
                        c[0] += 1
                        ins.then_inc(chain, 1)
                        dve.wait_ge(chain, n * CHAIN + c[0])

                    b = s * T + d
                    V.tensor_copy(lane[:, 0:2], g.slot_ids[:, :, bass.ds(b, 1)].rearrange("p a c -> p (a c)"))
                    V.tensor_copy(xrow[:], g.xparts[:, bass.ds(d, 1), :, :].rearrange("p a k c -> p (a k c)"))
                    V.tensor_copy(degs[:], flat(g.slot_deg[:, bass.ds(b, 1), :]))
                    step(V.tensor_reduce(lane[:, 2:3], g.slot_deg[:, bass.ds(b, 1), 1:4].rearrange("p a k -> p (a k)"),
                                         AX.X, ALU.add))
                    V.tensor_scalar(src16[:], g.iota[:P, 0:P], lane[:, 0:1], None, ALU.is_equal)
                    V.tensor_scalar(dst16[:], g.iota[:P, 0:P], lane[:, 1:2], None, ALU.is_equal)
                    V.tensor_scalar(src32[:], g.iota[:P, 0:P], lane[:, 0:1], None, ALU.is_equal)
                    V.tensor_scalar(dst32[:], g.iota[:P, 0:P], lane[:, 1:2], lane[:, 2:3], ALU.is_equal,
                                    ALU.mult).then_inc(hot, 1)
                    dve.wait_ge(product, n + 1)
                    V.tensor_copy(turned[:], p_t[:, 0:P]).then_inc(turned_ready, 1)
                    dve.wait_ge(read, (n + 1) * 32)
                    step(V.tensor_tensor(weight[:], weight[:], p_w[:, 0:P], ALU.add))
                    count = flat(g.counts[:, bass.ds(s, 1), bass.ds(d * P, P)])
                    step(V.tensor_tensor(v[:], count, p_c[:, 0:P], ALU.add))
                    step(V.tensor_scalar(carry[:], v[:], 256.0, None, ALU.is_ge))
                    step(V.scalar_tensor_tensor(out=count, in0=carry[:], scalar=-256.0, in1=v[:], op0=ALU.mult,
                                                op1=ALU.add))
                    step(V.tensor_tensor(high[:], high[:], carry[:], ALU.add))
                    degree = flat(g.deg[:, bass.ds(d, 1), :])
                    step(V.tensor_tensor(degree, degree, p_deg[:, 0:4], ALU.add))
                    dve.wait_ge(dyn_done, n + 1)
                    step(V.tensor_reduce(v[:, 0:C0], p_dyn[:, 0:3 * C0].rearrange("p (k c) -> p c k", k=3), AX.X, ALU.add))
                    row = flat(g.dyn[:, bass.ds(s, 1), :])
                    step(V.tensor_tensor(row, row, v[:, 0:C0], ALU.add))
                    assert c[0] == CHAIN
                    dve.sem_inc(updated)
                buckets(dve, body)

            @block.tensor
            def _(pe):
                def body(s, d, n):
                    pe.wait_ge(hot, n + 1)
                    nc.tensor.matmul(p_w[:, 0:P], src32[:], dst32[:], start=True, stop=True)
                    nc.tensor.matmul(p_c[:, 0:P], src16[:], dst16[:], start=True, stop=True)
                    nc.tensor.matmul(p_t[:, 0:P], dst16[:], src16[:], start=True, stop=True)
                    nc.tensor.matmul(p_deg[:, 0:4], dst16[:], degs[:], start=True, stop=True).then_inc(product, 1)
                    pe.wait_ge(turned_ready, n + 1)
                    nc.tensor.matmul(p_dyn[:, 0:3 * C0], turned[:], xrow[:], start=True, stop=True).then_inc(dyn_done, 1)
                buckets(pe, body)


def further_rounds(nc, g):
    rounds = nc.values_load(g.rounds[0:1, 0:1], min_val=1, max_val=E // P)
    with nc.If(rounds > 1):
        nc.all_engine_barrier()
        clear_high(nc, g)
        with nc.Fori(1, rounds):
            nc.all_engine_barrier()
            scatter_again(nc, g)
            load_slots(nc, g)
            add_blocks(nc, g)


def add_high_counts(nc, g, i):
    rounds = nc.values_load(g.rounds[0:1, 0:1], min_val=1, max_val=E // P)
    with nc.If(rounds > 1):
        nc.all_engine_barrier()
        with stage(nc) as (ctx, sem):
            high = ctx.enter_context(nc.sbuf_tensor(unique("high_y"), [P, P], BF16))
            part = ctx.enter_context(nc.sbuf_tensor(unique("part_y"), [P, 3 * C0], BF16))
            v = ctx.enter_context(nc.sbuf_tensor(unique("v_y"), [P, C0], F32))
            total = ctx.enter_context(nc.psum_tensor(unique("total_y"), [P, 512], F32))
            read, taken, summed, used, chain, held = sem("read_y"), sem("taken_y"), sem("summed_y"), sem("used_y"), sem("chain_y"), sem("held_y")

            def blocks(engine, body):
                with engine.Fori(0, T) as d:
                    with engine.Fori(0, T) as s:
                        body(s, d, d * T + s)

            with nc.Block() as block:
                @block.sync
                def _(sp):
                    def body(s, d, n):
                        sp.dma_start(high[:], g.high[bass.ds(s * P, P), bass.ds(d * P, P)]).then_inc(read, 16)
                        sp.wait_ge(used, n + 1)
                        sp.sem_inc(held)
                    blocks(sp, body)

                @block.tensor
                def _(pe):
                    def body(s, d, n):
                        pe.wait_ge(read, (n + 1) * 16)
                        pe.wait_ge(taken, n + 1)
                        nc.tensor.matmul(total[:, 0:3 * C0], high[:], part[:], start=True, stop=True).then_inc(summed, 1)
                    blocks(pe, body)

                @block.vector
                def _(dve):
                    V = nc.vector

                    def body(s, d, n):
                        V.tensor_copy(part[:], g.parts[i % 2][:, bass.ds(s, 1), :, :].rearrange("p a k c -> p (a k c)")
                                      ).then_inc(taken, 1)
                        dve.wait_ge(summed, n + 1)
                        V.tensor_reduce(v[:], total[:, 0:3 * C0].rearrange("p (k c) -> p c k", k=3), AX.X,
                                        ALU.add).then_inc(chain, 1)
                        dve.wait_ge(chain, n * 3 + 1)
                        V.tensor_scalar(v[:], v[:], g.dinv_s[:, bass.ds(d, 1)], 256.0, ALU.mult, ALU.mult).then_inc(chain, 1)
                        dve.wait_ge(chain, n * 3 + 2)
                        row = g.own[:, bass.ds(d, 1), :].rearrange("p a c -> p (a c)")
                        V.tensor_tensor(row, row, v[:], ALU.add).then_inc(chain, 1)
                        dve.wait_ge(chain, n * 3 + 3)
                        dve.sem_inc(used)
                    blocks(dve, body)

NE = 8
CAP = -(-5 * N // (4 * NE))
CT = -(-CAP // P)
CP = CT * P
F1 = 1024
LARGEST = 1e4


def route_first(nc, g):
    with stage(nc) as (ctx, sem):
        sb = lambda n, s, d: ctx.enter_context(nc.sbuf_tensor(unique(n), s, d))
        ps = lambda n: ctx.enter_context(nc.psum_tensor(unique(n), [128, 512], F32))
        rows, xT = sb("rows_r", [P, T, D + 2], F32), sb("xT_r", [128, F, N], F32)
        xn = rows[:, :, 0:D]
        stats, small = sb("stats_r", [P, T, 6], F32), sb("small_r", [P, 4, T], F32)
        zero = sb("zero_r", [P, 1, D + 2], F32)
        gate, gate_b = sb("gate_r", [128, F, NE], F32), sb("gate_b_r", [P, NE], F32)
        tri = sb("tri_r", [P, P], F32)
        number, rev = sb("number_r", [P, NE], F32), sb("rev_r", [P, NE], F32)
        logits, a, b = sb("logits_r", [P, T, NE], F32), sb("a_r", [P, T, NE], F32), sb("b_r", [P, T, NE], F32)
        hot, totals = sb("hot_r", [P, T, NE], F32), sb("totals_r", [P, 2, T, NE], F32)
        top, total, place, kept = (sb(f"{k}_r", [P, T], F32) for k in ("top", "total", "place", "kept"))
        where = sb("where_r", [P, T], F32)
        scatter_at = sb("scatter_at_r", [P, T], U32)
        psum = [ps(f"p_r{k}") for k in range(4)]
        p_gate, p_count, p_total = ps("p_gate"), ps("p_count"), ps("p_total")
        cleared, clear_out, w_in = sem("cleared_r"), sem("clear_out_r"), sem("w_in_r")
        rows_done, var_ready, root_done = sem("rows_done_r"), sem("var_ready_r"), sem("root_done_r")
        dve_step = sem("dve_step_r")
        turned, turn_read, gated = sem("turned_r"), sem("turn_read_r"), sem("gated_r")
        exp_asked, exp_done, hot_ready, counted = sem("exp_asked"), sem("exp_done"), sem("hot_ready_r"), sem("counted_r")
        places_ready, consts, scattered = sem("places_ready"), sem("consts_r"), sem("scattered_r")

        with nc.Block() as block:
            @block.sync
            def _(sp):
                sp.dma_start(gate[:], g.L0_ffn_gate_w.rearrange("(f i) e -> i f e", i=128)).then_inc(w_in, 16)
                sp.dma_start(gate_b[:], g.L0_ffn_gate_b[None, :].to_broadcast([P, NE])).then_inc(w_in, 16)
                sp.wait_ge(cleared, 1)
                sp.dma_start(g.placed.rearrange("(p n) d -> p n d", p=P),
                             zero[:].to_broadcast([P, NE * CP // P, D + 2])).then_inc(clear_out, 16)
                sp.dma_start(g.results.rearrange("(p n) d -> p n d", p=P),
                             zero[:, :, 0:D].to_broadcast([P, T, D])).then_inc(clear_out, 16)

            @block.gpsimd
            def _(pool):
                pool.memset(zero[:], 0.0).then_inc(cleared, 1)
                pool.iota(number[:], pattern=[[1, NE]], base=0, channel_multiplier=0,
                          allow_small_or_imprecise_dtypes=True).then_inc(consts, 1)
                pool.iota(rev[:], pattern=[[-1, NE]], base=NE, channel_multiplier=0,
                          allow_small_or_imprecise_dtypes=True).then_inc(consts, 1)
                pool.affine_select(out=tri[:], in_=g.ones[0:P, 0:P], compare_op=ALU.is_gt, fill=0.0, base=0,
                                   pattern=[[1, P]], channel_multiplier=-1).then_inc(consts, 1)
                pool.iota(rows[:, :, D + 1], pattern=[[P, T]], base=1, channel_multiplier=1,
                          allow_small_or_imprecise_dtypes=True).then_inc(consts, 1)
                bound = pool.to_reg(NE * CP - 1)
                pool.wait_ge(clear_out, 32)
                pool.wait_ge(places_ready, 1)
                for t in range(T):
                    pool.indirect_dma_start(
                        out=g.placed, out_offset=bass.IndirectOffsetOnAxis(ap=scatter_at[:, t:t + 1], axis=0),
                        in_=rows[:, t, :], in_offset=None, bounds_check=bound, oob_is_err=False).then_inc(scattered, 16)
                pool.wait_ge(scattered, 16 * T)

            @block.scalar
            def _(act):
                root(nc, act, small[:, 1, :], small[:, 3, :], var_ready, root_done)
                n = 0
                for t0, k in QUADS:
                    for f in range(F):
                        act.wait_ge(turned, n + 1)
                        nc.scalar.copy(xT[:, f, t0 * P:(t0 + k) * P], psum[n % 4][:, 0:k * P]).then_inc(turn_read, 1)
                        n += 1
                act.wait_ge(exp_asked, 1)
                nc.scalar.activation(b[:], a[:], ACT.Exp).then_inc(exp_done, 1)

            @block.tensor
            def _(pe):
                pe.wait_ge(w_in, 32)

                def gate_quad(q):
                    pe.wait_ge(turn_read, F * (q + 1))
                    t0, k = QUADS[q]
                    for t in range(t0, t0 + k):
                        for f in range(F):
                            mm = nc.tensor.matmul(p_gate[0:P, t * NE:(t + 1) * NE], xT[:, f, t * P:(t + 1) * P],
                                                  gate[:, f, :], start=(f == 0), stop=(f == F - 1))
                    mm.then_inc(gated, 1)

                turn_tiles(nc, pe, xn, D, psum, g.ident, turn_read, turned, rows_done, T, gate_quad)
                pe.wait_ge(hot_ready, 1)
                pe.wait_ge(consts, 4)
                flat = hot[:].rearrange("p t e -> p (t e)")
                nc.tensor.matmul(p_total[0:P, 0:T * NE], g.ones[0:P, 0:P], flat, start=True, stop=True).then_inc(counted, 1)
                nc.tensor.matmul(p_count[0:P, 0:T * NE], tri[:], flat, start=True, stop=True).then_inc(counted, 1)

            @block.vector
            def _(dve):
                step = Step(dve, dve_step)
                bc = lambda v: v[:, :, None].to_broadcast([P, T, NE])
                layer_norm(nc, dve, step, g.xr, xn, stats, small, rows_done, var_ready, root_done)
                dve.wait_ge(gated, len(QUADS))
                dve.wait_ge(w_in, 32)
                dve.wait_ge(consts, 4)
                V = nc.vector
                step(V.tensor_tensor(logits[:], p_gate[0:P, 0:T * NE].rearrange("p (t e) -> p t e", e=NE),
                                     gate_b[:, None, :].to_broadcast([P, T, NE]), ALU.add))
                step(V.tensor_reduce(top[:], logits[:], AX.X, ALU.max))
                V.tensor_tensor(a[:], logits[:], bc(top), ALU.subtract).then_inc(exp_asked, 1)
                step(V.tensor_tensor(hot[:], logits[:], bc(top), ALU.is_equal))
                step(V.tensor_tensor(hot[:], hot[:], rev[:, None, :].to_broadcast([P, T, NE]), ALU.mult))
                step(V.tensor_reduce(top[:], hot[:], AX.X, ALU.max))
                step(V.tensor_tensor(hot[:], hot[:], bc(top), ALU.is_equal))
                dve.sem_inc(hot_ready)
                dve.wait_ge(exp_done, 1)
                step(V.tensor_reduce(total[:], b[:], AX.X, ALU.add))
                step(V.reciprocal(total[:], total[:]))
                step(V.tensor_copy(rows[:, :, D], total[:]))
                step(V.tensor_scalar(top[:], top[:], -float(CP), float(NE * CP), ALU.mult, ALU.add))
                dve.wait_ge(counted, 2)
                step(V.tensor_copy(totals[:, 0], p_total[0:P, 0:T * NE].rearrange("p (t e) -> p t e", e=NE)))
                now, hop = 0, 1
                while hop < T:
                    step(V.tensor_copy(totals[:, 1 - now, 0:hop, :], totals[:, now, 0:hop, :]))
                    step(V.tensor_tensor(totals[:, 1 - now, hop:T, :], totals[:, now, hop:T, :],
                                         totals[:, now, 0:T - hop, :], ALU.add))
                    now, hop = 1 - now, hop * 2
                step(V.tensor_tensor(a[:], totals[:, now], p_total[0:P, 0:T * NE].rearrange("p (t e) -> p t e", e=NE),
                                     ALU.subtract))
                step(V.tensor_tensor(a[:], a[:], p_count[0:P, 0:T * NE].rearrange("p (t e) -> p t e", e=NE), ALU.add))
                step(V.tensor_tensor(a[:], a[:], hot[:], ALU.mult))
                step(V.tensor_reduce(place[:], a[:], AX.X, ALU.add))
                step(V.tensor_scalar(kept[:], place[:], float(CAP), None, ALU.is_lt))
                step(V.tensor_scalar(kept[:], kept[:], -PAST, PAST, ALU.mult, ALU.add))
                step(V.tensor_tensor(where[:], top[:], place[:], ALU.add))
                step(V.tensor_tensor(scatter_at[:], where[:], kept[:], ALU.add))
                dve.sem_inc(places_ready)


def first_experts(nc, g):
    M1 = F1 // 128
    with stage(nc) as (ctx, sem):
        sb = lambda n, s, d: ctx.enter_context(nc.sbuf_tensor(unique(n), s, d))
        ps = lambda n: ctx.enter_context(nc.psum_tensor(unique(n), [128, 512], F32))
        rows = sb("rows_f", [P, 2, CT, D + 2], F32)
        extra = sb("extra_f", [P, 2, CT, 2], F32)
        empty, token = sb("empty_f", [P, CT], F32), sb("token_f", [P, 2, CT], U32)
        xT = sb("xT_f", [128, 2, F, CP], F32)
        w1, w2 = sb("w1_f", [128, 2, F, F1], F32), sb("w2_f", [128, 2, M1, D], F32)
        b1, b2 = sb("b1_f", [128, NE, M1], F32), sb("b2_f", [P, NE, D], F32)
        b1_rows = sb("b1_rows_f", [NE * M1, 128], F32)
        hid = sb("hid_f", [128, 2, M1, CP], F32)
        y, z = sb("y_f", [P, CT, D], F32), sb("z_f", [P, 2, CT, D], F32)
        high, low = sb("high_f", [P, 1, D], F32), sb("low_f", [P, 1, D], F32)
        mask = sb("mask_f", [P, 3, CT, D], U32)
        p_turn = [ps(f"p_turn_f{k}") for k in range(2)]
        p_hid = [ps(f"p_hid_f{k}") for k in range(3)]
        p_out = [ps(f"p_out_f{k}") for k in range(2)]
        biases, rows_in = sem("biases_f"), [sem(f"rows_in_f{k}") for k in range(2)]
        w_in, y_out = [sem(f"w_in_f{k}") for k in range(2)], [sem(f"y_out_f{k}") for k in range(2)]
        turned, turn_read = sem("turned_f"), sem("turn_read_f")
        b1_turned, b1_ready = sem("b1_turned_f"), sem("b1_ready_f")
        hid_done, hid_ready = sem("hid_done_f"), sem("hid_ready_f")
        out_done, out_read = sem("out_done_f"), sem("out_read_f")
        dve_step, z_ready = sem("dve_step_f"), sem("z_ready_f")

        with nc.Block() as block:
            @block.sync
            def _(sp):
                sp.dma_start(b1_rows[:], g.L0_ffn_b1.rearrange("e (m i) -> (e m) i", i=128)).then_inc(biases, 16)
                sp.dma_start(b2[:], g.L0_ffn_b2[None, :, :].to_broadcast([P, NE, D])).then_inc(biases, 16)
                for e in range(NE):
                    k = e % 2
                    if e >= 2:
                        sp.wait_ge(hid_done, (e - 1) * M1)
                    sp.dma_start(rows[:, k], g.placed[e * CP:(e + 1) * CP, :].rearrange("(u p) d -> p u d", p=P)
                                 ).then_inc(rows_in[k], 16)
                    sp.dma_start(w1[:, k], g.L0_ffn_w1[e].rearrange("(f i) o -> i f o", i=128)).then_inc(w_in[k], 16)
                    if e >= 2:
                        sp.wait_ge(out_done, (e - 1) * CT)
                    sp.dma_start(w2[:, k], g.L0_ffn_w2[e].rearrange("(m i) o -> i m o", i=128)).then_inc(w_in[k], 16)

            @block.gpsimd
            def _(pool):
                bound = pool.to_reg(N - 1)
                for e in range(NE):
                    pool.wait_ge(z_ready, e + 1)
                    for u in range(CT):
                        pool.indirect_dma_start(
                            out=g.results, out_offset=bass.IndirectOffsetOnAxis(ap=token[:, e % 2, u:u + 1], axis=0),
                            in_=z[:, e % 2, u, :], in_offset=None, bounds_check=bound,
                            oob_is_err=False).then_inc(y_out[e % 2], 16)
                for k in range(2):
                    pool.wait_ge(y_out[k], 16 * CT * NE // 2)

            @block.tensor
            def _(pe):
                def turn(e):
                    k = e % 2
                    pe.wait_ge(rows_in[k], 16 * (e // 2 + 1))
                    for f in range(F):
                        n = e * F + f
                        if n >= 2:
                            pe.wait_ge(turn_read, n - 1)
                        for u in range(CT):
                            mm = nc.tensor.transpose(p_turn[f][:, u * P:(u + 1) * P],
                                                     rows[:, k, u, f * 128:(f + 1) * 128], g.ident[0:P, 0:P])
                        mm.then_inc(turned, 1)

                pe.wait_ge(biases, 32)
                nc.tensor.transpose(p_hid[0][:, 0:NE * M1], b1_rows[:], g.ident[0:NE * M1, 0:NE * M1]).then_inc(b1_turned, 1)
                turn(0)
                pe.wait_ge(b1_ready, 1)
                for e in range(NE):
                    k = e % 2
                    pe.wait_ge(turn_read, (e + 1) * F)
                    pe.wait_ge(w_in[k], 32 * (e // 2 + 1))
                    for m in range(M1):
                        n = e * M1 + m
                        if n >= 3:
                            pe.wait_ge(hid_ready, n - 2)
                        for f in range(F):
                            mm = nc.tensor.matmul(p_hid[n % 3][:, 0:CP], w1[:, k, f, m * 128:(m + 1) * 128],
                                                  xT[:, k, f, :], start=(f == 0), stop=(f == F - 1))
                        mm.then_inc(hid_done, 1)
                    if e + 1 < NE:
                        turn(e + 1)
                    pe.wait_ge(hid_ready, (e + 1) * M1)
                    for u in range(CT):
                        n = e * CT + u
                        if n >= 2:
                            pe.wait_ge(out_read, n - 1)
                        for m in range(M1):
                            mm = nc.tensor.matmul(p_out[n % 2][0:P, 0:D], hid[:, k, m, u * P:(u + 1) * P],
                                                  w2[:, k, m, :], start=(m == 0), stop=(m == M1 - 1))
                        mm.then_inc(out_done, 1)

            @block.scalar
            def _(act):
                act.wait_ge(b1_turned, 1)
                nc.scalar.copy(b1[:].rearrange("p e m -> p (e m)"), p_hid[0][:, 0:NE * M1]).then_inc(b1_ready, 1)
                act.wait_ge(b1_ready, 1)
                for e in range(NE):
                    k = e % 2
                    if e >= 2:
                        act.wait_ge(out_done, (e - 1) * CT)
                    for m in range(M1):
                        n = e * M1 + m
                        act.wait_ge(hid_done, n + 1)
                        nc.scalar.activation(hid[:, k, m, :], p_hid[n % 3][:, 0:CP], ACT.Relu,
                                             bias=b1[:, e, m:m + 1]).then_inc(hid_ready, 1)

            @block.vector
            def _(dve):
                step = Step(dve, dve_step)
                V = nc.vector
                step(V.memset(high[:], LARGEST))
                step(V.memset(low[:], -LARGEST))
                dve.wait_ge(biases, 32)

                def take_turned(e):
                    k = e % 2
                    if e >= 2:
                        dve.wait_ge(hid_done, (e - 1) * M1)
                    dve.wait_ge(rows_in[k], 16 * (e // 2 + 1))
                    step(V.tensor_copy(extra[:, k], rows[:, k, :, D:D + 2]))
                    for f in range(F):
                        dve.wait_ge(turned, e * F + f + 1)
                        V.tensor_copy(xT[:, k, f, :], p_turn[f][:, 0:CP]).then_inc(turn_read, 1)

                take_turned(0)
                for e in range(NE):
                    k = e % 2
                    if e + 1 < NE:
                        take_turned(e + 1)
                    for u in range(CT):
                        dve.wait_ge(out_done, e * CT + u + 1)
                        V.tensor_tensor(y[:, u, :], p_out[(e * CT + u) % 2][0:P, 0:D], b2[:, e, :],
                                        ALU.add).then_inc(out_read, 1)
                    dve.wait_ge(out_read, (e + 1) * CT)
                    step(V.tensor_tensor(y[:], y[:], extra[:, k, :, 0:1].to_broadcast([P, CT, D]), ALU.mult))
                    if e >= 2:
                        dve.wait_ge(y_out[k], 16 * CT * (e // 2))
                    step(V.tensor_scalar(empty[:], extra[:, k, :, 1], 0.0, PAST + 1, ALU.is_equal, ALU.mult))
                    step(V.scalar_tensor_tensor(out=token[:, k, :], in0=extra[:, k, :, 1], scalar=-1.0, in1=empty[:],
                                                op0=ALU.add, op1=ALU.add))
                    V.memset(z[:, k], 0.0).then_inc(dve_step, 1)
                    V.tensor_tensor(mask[:, 0], y[:], y[:], ALU.is_equal).then_inc(dve_step, 1)
                    V.tensor_scalar(mask[:, 1], y[:], LIMIT, None, ALU.is_gt).then_inc(dve_step, 1)
                    step.count += 3
                    step(V.tensor_scalar(mask[:, 2], y[:], -LIMIT, None, ALU.is_lt))
                    step(V.copy_predicated(z[:, k], mask[:, 0], y[:]))
                    step(V.copy_predicated(z[:, k], mask[:, 1], high[:].to_broadcast([P, CT, D])))
                    V.copy_predicated(z[:, k], mask[:, 2], low[:].to_broadcast([P, CT, D])).then_inc(z_ready, 1)


def combine_first(nc, g):
    FEW = 5
    with stage(nc) as (ctx, sem):
        y = ctx.enter_context(nc.sbuf_tensor(unique("y_c"), [P, T, D], F32))
        loaded, added = [sem(f"loaded_c{m}") for m in range(T // FEW)], sem("added_c")
        with nc.Block() as block:
            @block.sync
            def _(sp):
                for m in range(T // FEW):
                    sp.dma_start(y[:, m * FEW:(m + 1) * FEW, :],
                                 g.results.rearrange("(t p) d -> p t d", p=P)[:, m * FEW:(m + 1) * FEW, :]
                                 ).then_inc(loaded[m], 16)

            @block.vector
            def _(dve):
                for m in range(T // FEW):
                    dve.wait_ge(loaded[m], 16)
                    now = slice(m * FEW, (m + 1) * FEW)
                    nc.vector.tensor_tensor(g.xr[:, now, :], g.xr[:, now, :], y[:, now, :], ALU.add).then_inc(added, 1)
                dve.wait_ge(added, T // FEW)


LIMIT = 3.4028234663852886e38

WINDOWS = [(0, [(0, 4), (4, 4), (8, 4), (12, 4)]), (16, [(16, 4), (20, 4), (24, 1)])]
PAIRS = [(t, min(2, T - t)) for t in range(0, T, 2)]


def second_gnn(nc, g):
    RING = 5
    with stage(nc) as (ctx, sem):
        sb = lambda n, s, d: ctx.enter_context(nc.sbuf_tensor(unique(n), s, d))
        msg = sb("msg_w", [P, T, D], F32)
        xT, outT = sb("xT_w", [128, F, N], F32), sb("outT_w", [128, F, N], F32)
        strips = sb("strips_w", [P, RING, 16 * P], F32)
        msg_now = sb("msg_now", [P, RING, D], F32)
        dinv_row = sb("dinv_row", [128, N], F32)
        stats, small = sb("stats_w", [P, T, 6], F32), sb("small_w", [P, 4, T], F32)
        dinv, rooted, tmp, mask = (sb(f"{k}_w", [P, T], F32) for k in ("dinv", "rooted", "tmp", "mask"))
        dinv_t = sb("dinv_t", [T, P], F32)
        w = [sb(f"w{i}_w", [128, F, D], F32) for i in range(2)]
        cols = sb("cols_w", [128, 4, F], F32)
        bn = sb("bn_w", [128, F, 7, 6], F32)
        agg = sb("agg_w", [128, F, 2], F32)
        norm = sb("norm_w", [128, 4, F], F32)
        bank = [ctx.enter_context(nc.psum_tensor(unique(f"bank_w{k}"), [128, 512], F32)) for k in range(8)]

        w_in, rows_done, var_ready, root_done = sem("w_in_w"), sem("rows_done_w"), sem("var_ready_w"), sem("root_done_w")
        dve_step, turned, turn_read = sem("dve_step_w"), sem("turned_w"), sem("turn_read_w")
        deg_ready, deg_rooted = sem("deg_ready_w"), sem("deg_rooted_w")
        dinv_ready, dinv_turned, dinv_read, dinv_out, row_in = (
            sem(k) for k in ("dinv_ready", "dinv_turned", "dinv_read", "dinv_out", "row_in"))
        multiplied, msg_ready = sem("multiplied_w"), sem("msg_ready")
        strip_in = [sem(f"strip_in{k}") for k in range(RING)]
        now_ready = sem("now_ready")
        strip_used, scaled, out_ready = sem("strip_used"), sem("scaled_w"), sem("out_ready_w")
        bn_ready, bn_rooted, norm_ready = sem("bn_ready"), sem("bn_rooted"), sem("norm_ready")
        mixed, final_ready, back, added = sem("mixed"), sem("final_ready"), sem("back"), sem("added_w")
        NQ, NP, NCH = len(QUADS), len(PAIRS), 7
        BIG = 2 * NCH

        with nc.Block() as block:
            @block.sync
            def _(sp):
                for i, name in enumerate((g.L1_gnn_W1, g.L1_gnn_W2)):
                    sp.dma_start(w[i][:], name.rearrange("(f i) o -> i f o", i=128)).then_inc(w_in, 16)
                for i, name in enumerate((g.L1_gnn_b1, g.L1_gnn_b2, g.L1_gnn_gamma, g.L1_gnn_beta)):
                    for f in range(F):
                        sp.dma_start(cols[:, i, f:f + 1], name[f * 128:(f + 1) * 128, None]).then_inc(w_in, 16)
                sp.wait_ge(dinv_read, 1)
                sp.dma_start(g.dinv.rearrange("(t p) -> t p", p=P), dinv_t[:]).then_inc(dinv_out, 16)
                sp.wait_ge(dinv_out, 16)
                sp.dma_start(dinv_row[:], g.dinv[None, :].to_broadcast([128, N])).then_inc(row_in, 16)
                for i in range(2):
                    for v, (first, chunks) in enumerate(WINDOWS):
                        lo, width = first * P, sum(k for _, k in chunks) * P
                        trip = (i * 2 + v) * (T // RING)

                        def load(m, fresh):
                            for r in range(RING):
                                s = m * RING + r
                                if not fresh:
                                    sp.wait_ge(strip_used, (m + trip - 1) * RING + r + 1)
                                sp.dma_start(strips[:, r, 0:width], g.weights[bass.ds(s * P, P), lo:lo + width]
                                             ).then_inc(strip_in[r], 16)

                        load(0, i == 0 and v == 0)
                        with sp.Fori(1, T // RING) as m:
                            load(m, False)

            @block.scalar
            def _(act):
                root(nc, act, dinv[:], rooted[:], deg_ready, deg_rooted)
                root(nc, act, small[:, 1, :], small[:, 3, :], var_ready, root_done)
                n = 0
                for t0, k in QUADS:
                    for f in range(F):
                        act.wait_ge(turned, n + 1)
                        nc.scalar.copy(xT[:, f, t0 * P:(t0 + k) * P], bank[n % 4][:, 0:k * P]).then_inc(turn_read, 1)
                        n += 1
                act.wait_ge(w_in, 160)
                for i, func in enumerate((ACT.Relu, ACT.Identity)):
                    n = 0
                    act.wait_ge(msg_ready, (i + 1) * NP)
                    for v, (_, chunks) in enumerate(WINDOWS):
                        trip = (i * 2 + v) * (T // RING)

                        def take(m, fresh):
                            for r in range(RING):
                                if not fresh:
                                    act.wait_ge(strip_used, (m + trip - 1) * RING + r + 1)
                                nc.scalar.copy(msg_now[:, r, :], msg[:, bass.ds(m * RING + r, 1), :].rearrange(
                                    "p a c -> p (a c)")).then_inc(now_ready, 1)

                        take(0, i == 0 and v == 0)
                        with act.Fori(1, T // RING) as m:
                            take(m, False)
                        for t0, k in chunks:
                            for f in range(F):
                                act.wait_ge(scaled, i * BIG + n + 1)
                                o = outT[:, f, t0 * P:(t0 + k) * P]
                                nc.scalar.activation(o, o, func, bias=cols[:, i, f:f + 1]).then_inc(out_ready, 1)
                                n += 1
                root(nc, act, norm[:, 0, :], norm[:, 1, :], bn_ready, bn_rooted)
                act.wait_ge(norm_ready, 1)
                n = 0
                for t0, k in QUADS:
                    for f in range(F):
                        act.wait_ge(mixed, n + 1)
                        o = outT[:, f, t0 * P:(t0 + k) * P]
                        nc.scalar.activation(o, o, ACT.Relu, bias=norm[:, 3, f:f + 1]).then_inc(final_ready, 1)
                        n += 1

            @block.tensor
            def _(pe):
                pe.wait_ge(dinv_ready, 1)
                nc.tensor.transpose(bank[7][0:T, 0:P], dinv[:], g.ident[0:P, 0:P]).then_inc(dinv_turned, 1)
                turn_tiles(nc, pe, msg, D, bank[0:4], g.ident, turn_read, turned, rows_done, T)
                pe.wait_ge(w_in, 160)
                pe.wait_ge(turn_read, F * NQ)
                pe.wait_ge(dinv_read, 1)
                for i in range(2):
                    rows = xT if i == 0 else outT
                    for n, (t0, k) in enumerate(PAIRS):
                        if i and n == 0:
                            pe.wait_ge(out_ready, BIG)
                        if n >= 8:
                            pe.wait_ge(msg_ready, i * NP + n - 7)
                        for u in range(k):
                            for f in range(F):
                                mm = nc.tensor.matmul(bank[n % 8][0:P, u * D:(u + 1) * D],
                                                      rows[:, f, (t0 + u) * P:(t0 + u + 1) * P], w[i][:, f, :],
                                                      start=(f == 0), stop=(f == F - 1))
                        mm.then_inc(multiplied, 1)
                    pe.wait_ge(msg_ready, (i + 1) * NP)
                    before = 0
                    for v, (first, chunks) in enumerate(WINDOWS):
                        if v:
                            pe.wait_ge(scaled, i * BIG + before)
                        for c, (t0, k) in enumerate(chunks):
                            for f in range(F):
                                for u in range(k):
                                    nc.tensor.matmul(bank[2 * c + f][:, u * P:(u + 1) * P],
                                                     msg[:, t0 + u, f * 128:(f + 1) * 128], g.ident[0:P, 0:P],
                                                     start=(u == 0), stop=False, skip_group_check=True)

                        trip = (i * 2 + v) * (T // RING)
                        with pe.Fori(0, T // RING) as m:
                            for r in range(RING):
                                pe.wait_ge(strip_in[r], (m + trip + 1) * 16)
                                pe.wait_ge(now_ready, (m + trip) * RING + r + 1)
                                for f in range(F):
                                    for c, (t0, k) in enumerate(chunks):
                                        mm = nc.tensor.matmul(
                                            bank[2 * c + f][:, 0:k * P],
                                            msg_now[:, r, f * 128:(f + 1) * 128],
                                            strips[:, r, (t0 - first) * P:(t0 - first + k) * P], start=False,
                                            stop=True, skip_group_check=True)
                                mm.then_inc(strip_used, 1)
                        before += 2 * len(chunks)
                for n, (t0, k) in enumerate(PAIRS):
                    if n == 0:
                        pe.wait_ge(scaled, 2 * BIG)
                    pe.wait_ge(final_ready, F * ((t0 + k - 1) // 4 + 1))
                    if n >= 8:
                        pe.wait_ge(added, n - 7)
                    for u in range(k):
                        for f in range(F):
                            mm = nc.tensor.transpose(bank[n % 8][0:P, u * D + f * 128:u * D + (f + 1) * 128],
                                                     outT[:, f, (t0 + u) * P:(t0 + u + 1) * P], g.ident[:, :])
                    mm.then_inc(back, 1)

            @block.vector
            def _(dve):
                step = Step(dve, dve_step)
                V = nc.vector
                step(V.tensor_reduce(dinv[:], g.deg[:, :, 1:4], AX.X, ALU.add))
                step(V.tensor_scalar_add(dinv[:], dinv[:], 1.0))
                step(V.tensor_scalar(mask[:], dinv[:], 0.0, None, ALU.is_gt))
                V.tensor_scalar_max(dinv[:], dinv[:], 1e-30).then_inc(deg_ready, 1)
                inverse_root(nc, dve, step, dinv[:], rooted[:], tmp[:], deg_rooted)
                V.tensor_tensor(dinv[:], dinv[:], mask[:], ALU.mult).then_inc(dinv_ready, 1)
                dve.wait_ge(dinv_turned, 1)
                V.tensor_copy(dinv_t[:], bank[7][0:T, 0:P]).then_inc(dinv_read, 1)
                layer_norm(nc, dve, step, g.xr, msg, stats, small, rows_done, var_ready, root_done)
                dve.wait_ge(w_in, 160)
                dve.wait_ge(turned, F * NQ)
                for i in range(2):
                    if i:
                        dve.wait_ge(strip_used, 2 * T)
                    for n, (t0, k) in enumerate(PAIRS):
                        dve.wait_ge(multiplied, i * NP + n + 1)
                        V.tensor_tensor(msg[:, t0:t0 + k, :],
                                        bank[n % 8][0:P, 0:k * D].rearrange("p (u c) -> p u c", u=k),
                                        dinv[:, t0:t0 + k, None].to_broadcast([P, k, D]), ALU.mult).then_inc(msg_ready, 1)
                    if i == 0:
                        dve.wait_ge(row_in, 16)
                    for v, (first, chunks) in enumerate(WINDOWS):
                        dve.wait_ge(strip_used, (i * 2 + v + 1) * T)
                        for c, (t0, k) in enumerate(chunks):
                            for f in range(F):
                                at = slice(t0 * P, (t0 + k) * P)
                                V.tensor_tensor(outT[:, f, at], bank[2 * c + f][:, 0:k * P], dinv_row[:, at],
                                                ALU.mult).then_inc(scaled, 1)
                dve.wait_ge(out_ready, 2 * BIG)
                for f in range(F):
                    for q, (t0, k) in enumerate(QUADS):
                        ins = V.bn_stats(bn[:, f, q, :], outT[:, f, t0 * P:(t0 + k) * P])
                step(ins)
                for f in range(F):
                    step(V.bn_aggr(agg[:, f, :], bn[:, f, :, :].rearrange("p q k -> p (q k)")))
                V.tensor_scalar_add(norm[:, 0, :], agg[:, :, 1], EPS).then_inc(bn_ready, 1)
                inverse_root(nc, dve, step, norm[:, 0, :], norm[:, 1, :], norm[:, 2, :], bn_rooted)
                step(V.tensor_tensor(norm[:, 0, :], norm[:, 0, :], cols[:, 2, :], ALU.mult))
                step(V.tensor_tensor(norm[:, 2, :], norm[:, 0, :], agg[:, :, 0], ALU.mult))
                step(V.tensor_tensor(norm[:, 3, :], cols[:, 3, :], norm[:, 2, :], ALU.subtract))
                dve.sem_inc(norm_ready)
                for t0, k in QUADS:
                    for f in range(F):
                        at = slice(t0 * P, (t0 + k) * P)
                        V.scalar_tensor_tensor(out=outT[:, f, at], in0=outT[:, f, at], scalar=norm[:, 0, f:f + 1],
                                               in1=xT[:, f, at], op0=ALU.mult, op1=ALU.add).then_inc(mixed, 1)
                for n, (t0, k) in enumerate(PAIRS):
                    dve.wait_ge(back, n + 1)
                    V.tensor_tensor(g.xr[:, t0:t0 + k, :], g.xr[:, t0:t0 + k, :],
                                    bank[n % 8][0:P, 0:k * D].rearrange("p (u c) -> p u c", u=k),
                                    ALU.add).then_inc(added, 1)
                dve.wait_ge(added, NP)

F2 = 512
FAR = -1e30
NT = 2 * N // P + NE


def route_second(nc, g, w_all_in):
    with stage(nc) as (ctx, sem):
        sb = lambda n, s, d: ctx.enter_context(nc.sbuf_tensor(unique(n), s, d))
        ps = lambda n: ctx.enter_context(nc.psum_tensor(unique(n), [128, 512], F32))
        rows, xT = sb("rows_z", [P, T, D + 1], F32), sb("xT_z", [128, F, N], F32)
        xn = rows[:, :, 0:D]
        place_at, target = sb("place_at", [P, 2, T], U32), sb("target", [P, 2, T], F32)
        stats, small = sb("stats_z", [P, T, 6], F32), sb("small_z", [P, 4, T], F32)
        zero = sb("zero_z", [P, 1, D + 1], F32)
        gb = sb("gb_z", [P, 2, D], F32)
        wr, br = sb("wr_z", [128, F, NE], F32), sb("br_z", [P, NE], F32)
        rev, tri = sb("rev_z", [P, NE], F32), sb("tri_z", [P, P], F32)
        number = sb("number_z", [P, NT], F32)
        logits, a, share = sb("logits_z", [P, T, NE], F32), sb("a_z", [P, T, NE], F32), sb("share_z", [P, T, NE], F32)
        hot = sb("hot_z", [P, 2, T, NE], F32)
        both, totals = sb("both_z", [P, T, NE], F32), sb("totals_z", [P, 2, T, NE], F32)
        top, pick = sb("top_z", [P, 2, T], F32), sb("pick_z", [P, T], F32)
        ratio, place = sb("ratio_z", [P, T], F32), sb("place_z", [P, T], F32)
        tiles, ends, starts = (sb(f"{k}_z", [P, NE], F32) for k in ("tiles", "ends", "starts"))
        past, owner = sb("past_z", [P, NT, NE - 1], F32), sb("owner_z", [P, NT], F32)
        shareT = sb("shareT_z", [NE, N], F32)
        b2 = sb("b2_z", [NE, D], F32)
        bank = [ps(f"bank_z{k}") for k in range(8)]
        small_in = sem("small_in_z")
        rows_done, var_ready, root_done = sem("rows_done_z"), sem("var_ready_z"), sem("root_done_z")
        dve_step, turned, turn_read = sem("dve_step_z"), sem("turned_z"), sem("turn_read_z")
        consts, gated, asked, answered = sem("consts_z"), sem("gated_z"), sem("asked_z"), sem("answered_z")
        picked, counted, places_ready = sem("picked_z"), sem("counted_z"), sem("places_ready_z")
        share_ready, share_turned, share_read = sem("share_ready"), sem("share_turned"), sem("share_read")
        biased, bias_read = sem("biased"), sem("bias_read")
        cleared, clear_out, scattered = sem("cleared_z"), sem("clear_out_z"), sem("scattered_z")
        target_set, halfway = sem("target_set"), sem("halfway")
        NQ, NP = len(QUADS), len(PAIRS)

        with nc.Block() as block:
            @block.sync
            def _(sp):
                for k, v in enumerate((g.L1_ffn_gamma, g.L1_ffn_beta)):
                    sp.dma_start(gb[:, k, :], v[None, :].to_broadcast([P, D])).then_inc(small_in, 16)
                sp.dma_start(wr[:], g.L1_ffn_Wr.rearrange("(f i) e -> i f e", i=128)).then_inc(small_in, 16)
                sp.dma_start(br[:], g.L1_ffn_br[None, :].to_broadcast([P, NE])).then_inc(small_in, 16)
                sp.dma_start(b2[:], g.L1_ffn_b2).then_inc(small_in, 16)
                sp.wait_ge(cleared, 1)
                sp.dma_start(g.placed2.rearrange("(p n) d -> p n d", p=P), zero[:].to_broadcast([P, NT, D + 1])).then_inc(
                    clear_out, 16)

            @block.gpsimd
            def _(pool):
                pool.memset(zero[:], 0.0).then_inc(cleared, 1)
                pool.iota(rev[:], pattern=[[-1, NE]], base=NE, channel_multiplier=0,
                          allow_small_or_imprecise_dtypes=True).then_inc(consts, 1)
                pool.iota(number[:], pattern=[[1, NT]], base=0, channel_multiplier=0,
                          allow_small_or_imprecise_dtypes=True).then_inc(consts, 1)
                pool.affine_select(out=tri[:], in_=g.ones[0:P, 0:P], compare_op=ALU.is_gt, fill=0.0, base=0,
                                   pattern=[[1, P]], channel_multiplier=-1).then_inc(consts, 1)
                pool.iota(target[:], pattern=[[N, 2], [P, T]], base=1, channel_multiplier=1,
                          allow_small_or_imprecise_dtypes=True).then_inc(consts, 1)
                bound = pool.to_reg(NT * P - 1)
                pool.wait_ge(clear_out, 16)
                for k in range(2):
                    pool.wait_ge(places_ready, k + 1)
                    if k:
                        pool.wait_ge(scattered, 16 * T)
                    nc.gpsimd.tensor_copy(rows[:, :, D], target[:, k, :]).then_inc(target_set, 1)
                    pool.wait_ge(target_set, k + 1)
                    for t in range(T):
                        pool.indirect_dma_start(
                            out=g.placed2, out_offset=bass.IndirectOffsetOnAxis(ap=place_at[:, k, t:t + 1], axis=0),
                            in_=rows[:, t, :], in_offset=None, bounds_check=bound, oob_is_err=False).then_inc(scattered, 16)
                pool.wait_ge(scattered, 2 * 16 * T)

            @block.scalar
            def _(act):
                root(nc, act, small[:, 1, :], small[:, 3, :], var_ready, root_done)
                act.wait_ge(clear_out, 16)
                for e in range(NE):
                    act.dma_start(g.w1_all[:, e], g.L1_ffn_W1[e].rearrange("(f i) o -> i f o", i=128)).then_inc(w_all_in, 16)
                    act.dma_start(g.w2_all[:, e], g.L1_ffn_W2[e].rearrange("(m i) o -> i m o", i=128)).then_inc(w_all_in, 16)
                n = 0
                for t0, k in QUADS:
                    for f in range(F):
                        act.wait_ge(turned, n + 1)
                        nc.scalar.copy(xT[:, f, t0 * P:(t0 + k) * P], bank[n % 4][:, 0:k * P]).then_inc(turn_read, 1)
                        n += 1
                act.wait_ge(asked, 1)
                nc.scalar.activation(ratio[:], ratio[:], ACT.Exp).then_inc(answered, 1)

            @block.tensor
            def _(pe):
                pe.wait_ge(small_in, 80)

                def gate_quad(q):
                    pe.wait_ge(turn_read, F * (q + 1))
                    t0, k = QUADS[q]
                    for t in range(t0, t0 + k):
                        for f in range(F):
                            mm = nc.tensor.matmul(bank[5][0:P, t * NE:(t + 1) * NE], xT[:, f, t * P:(t + 1) * P],
                                                  wr[:, f, :], start=(f == 0), stop=(f == F - 1))
                    mm.then_inc(gated, 1)

                turn_tiles(nc, pe, xn, D, bank[0:4], g.ident, turn_read, turned, rows_done, T, gate_quad)
                pe.wait_ge(picked, 1)
                pe.wait_ge(consts, 4)
                flat = both[:].rearrange("p t e -> p (t e)")
                nc.tensor.matmul(bank[2][0:P, 0:T * NE], g.ones[0:P, 0:P], flat, start=True, stop=True).then_inc(counted, 1)
                nc.tensor.matmul(bank[3][0:P, 0:T * NE], tri[:], flat, start=True, stop=True).then_inc(counted, 1)
                pe.wait_ge(share_ready, 1)
                for q, (t0, k) in enumerate(QUADS):
                    if q >= 2:
                        pe.wait_ge(share_read, q - 1)
                    for u in range(k):
                        mm = nc.tensor.transpose(bank[6 + q % 2][0:NE, u * P:(u + 1) * P], share[:, t0 + u, :],
                                                 g.ident[0:P, 0:P])
                    mm.then_inc(share_turned, 1)
                pe.wait_ge(share_read, NQ)
                for n, (t0, k) in enumerate(PAIRS):
                    if n >= 4:
                        pe.wait_ge(bias_read, n - 3)
                    for u in range(k):
                        mm = nc.tensor.matmul(bank[4 + n % 4][0:P, u * D:(u + 1) * D],
                                              shareT[:, (t0 + u) * P:(t0 + u + 1) * P], b2[:], start=True, stop=True)
                    mm.then_inc(biased, 1)

            @block.vector
            def _(dve):
                step = Step(dve, dve_step)
                V = nc.vector
                bc = lambda v: v[:, :, None].to_broadcast([P, T, NE])
                per_expert = lambda b: b[0:P, 0:T * NE].rearrange("p (t e) -> p t e", e=NE)
                dve.wait_ge(small_in, 80)
                layer_norm(nc, dve, step, g.xr, xn, stats, small, rows_done, var_ready, root_done, gb[:, 0, :], gb[:, 1, :],
                           halfway)
                dve.wait_ge(gated, NQ)
                dve.wait_ge(consts, 4)
                step(V.tensor_tensor(logits[:], per_expert(bank[5]), br[:, None, :].to_broadcast([P, T, NE]), ALU.add))
                for k in range(2):
                    step(V.tensor_reduce(top[:, k, :], logits[:], AX.X, ALU.max))
                    step(V.tensor_tensor(a[:], logits[:], bc(top[:, k, :]), ALU.is_equal))
                    step(V.tensor_tensor(a[:], a[:], rev[:, None, :].to_broadcast([P, T, NE]), ALU.mult))
                    step(V.tensor_reduce(pick[:], a[:], AX.X, ALU.max))
                    step(V.tensor_tensor(hot[:, k], a[:], bc(pick[:]), ALU.is_equal))
                    if k == 0:
                        step(V.scalar_tensor_tensor(out=logits[:], in0=hot[:, 0], scalar=FAR, in1=logits[:],
                                                    op0=ALU.mult, op1=ALU.add))
                V.tensor_tensor(both[:], hot[:, 0], hot[:, 1], ALU.add).then_inc(picked, 1)
                dve.wait_ge(counted, 2)
                step(V.tensor_copy(totals[:, 0], per_expert(bank[2])))
                now, hop = 0, 1
                while hop < T:
                    step(V.tensor_copy(totals[:, 1 - now, 0:hop, :], totals[:, now, 0:hop, :]))
                    step(V.tensor_tensor(totals[:, 1 - now, hop:T, :], totals[:, now, hop:T, :],
                                         totals[:, now, 0:T - hop, :], ALU.add))
                    now, hop = 1 - now, hop * 2
                step(V.tensor_scalar(tiles[:], totals[:, now, T - 1, :], 1.0 / P, (P // 2) / P, ALU.mult, ALU.add))
                step(V.tensor_scalar_add(ends[:], tiles[:], ROUND))
                step(V.tensor_scalar_add(tiles[:], ends[:], -ROUND))
                step(V.tensor_copy(ends[:], tiles[:]))
                for e in range(1, NE):
                    step(V.tensor_tensor(ends[:, e:e + 1], ends[:, e:e + 1], ends[:, e - 1:e], ALU.add))
                step(V.tensor_tensor(starts[:], ends[:], tiles[:], ALU.subtract))
                step(V.tensor_tensor(a[:], totals[:, now], per_expert(bank[2]), ALU.subtract))
                step(V.tensor_tensor(a[:], a[:], per_expert(bank[3]), ALU.add))
                step(V.tensor_scalar_mul(starts[:], starts[:], float(P)))
                step(V.tensor_tensor(a[:], a[:], starts[:, None, :].to_broadcast([P, T, NE]), ALU.add))
                for k in range(2):
                    step(V.tensor_tensor(totals[:, 0], hot[:, k], a[:], ALU.mult))
                    step(V.tensor_reduce(place[:], totals[:, 0], AX.X, ALU.add))
                    step(V.tensor_copy(place_at[:, k, :], place[:]))
                    dve.sem_inc(places_ready)
                step(V.tensor_tensor(past[:], number[:, :, None].to_broadcast([P, NT, NE - 1]),
                                     ends[:, None, 0:NE - 1].to_broadcast([P, NT, NE - 1]), ALU.is_ge))
                step(V.tensor_reduce(owner[:], past[:], AX.X, ALU.add))
                step(V.tensor_copy(g.expert_of[:], owner[0:1, :]))
                V.tensor_tensor(ratio[:], top[:, 1, :], top[:, 0, :], ALU.subtract).then_inc(asked, 1)
                dve.wait_ge(answered, 1)
                step(V.tensor_scalar_add(g.shares[:, 0, :], ratio[:], 1.0))
                step(V.reciprocal(g.shares[:, 0, :], g.shares[:, 0, :]))
                step(V.tensor_tensor(g.shares[:, 1, :], ratio[:], g.shares[:, 0, :], ALU.mult))
                step(V.tensor_tensor(share[:], hot[:, 0], bc(g.shares[:, 0, :]), ALU.mult))
                step(V.tensor_tensor(a[:], hot[:, 1], bc(g.shares[:, 1, :]), ALU.mult))
                V.tensor_tensor(share[:], share[:], a[:], ALU.add).then_inc(share_ready, 1)
                for q, (t0, k) in enumerate(QUADS):
                    dve.wait_ge(share_turned, q + 1)
                    V.tensor_copy(shareT[:, t0 * P:(t0 + k) * P], bank[6 + q % 2][0:NE, 0:k * P]).then_inc(share_read, 1)
                for n, (t0, k) in enumerate(PAIRS):
                    dve.wait_ge(biased, n + 1)
                    V.tensor_tensor(g.xr[:, t0:t0 + k, :], g.xr[:, t0:t0 + k, :],
                                    bank[4 + n % 4][0:P, 0:k * D].rearrange("p (u c) -> p u c", u=k),
                                    ALU.add).then_inc(bias_read, 1)
                dve.wait_ge(bias_read, NP)


def second_experts(nc, g):
    M2 = F2 // 128
    with stage(nc) as (ctx, sem):
        sb = lambda n, s, d: ctx.enter_context(nc.sbuf_tensor(unique(n), s, d))
        ps = lambda n: [ctx.enter_context(nc.psum_tensor(unique(f"{n}{k}"), [128, 512], F32)) for k in range(2)]
        rows, xT = sb("rows_v", [P, 2, D + 1], F32), sb("xT_v", [128, 2, F, P], F32)
        empty, target = sb("empty_v", [P, 2], F32), sb("target_v", [P, 2, 1], U32)
        before, hidT = sb("before_v", [P, 2, F2], F32), sb("hidT_v", [128, 2, M2, P], F32)
        y, wanted = sb("y_v", [P, 2, D], F32), sb("wanted", [P, 2, 2], F32)
        b1_rows, b1 = sb("b1_rows_v", [NE * M2, 128], F32), sb("b1_v", [128, NE, M2], F32)
        p_x, p_up, p_h, p_y = ps("p_x_v"), ps("p_up_v"), ps("p_h_v"), ps("p_y_v")
        b1_in, b1_turned, b1_ready, tile_held = sem("b1_in_v"), sem("b1_turned_v"), sem("b1_ready_v"), sem("tile_held")
        rows_in, y_out = [sem(f"rows_in_v{k}") for k in range(2)], [sem(f"y_out_v{k}") for k in range(2)]
        x_turned, x_ready, up_done, up_read = sem("x_turned_v"), sem("x_ready_v"), sem("up_done_v"), sem("up_read_v")
        target_step, wanted_clear = sem("target_step"), sem("wanted_clear")
        h_turned, h_ready, down_done, y_ready = sem("h_turned_v"), sem("h_ready_v"), sem("down_done_v"), sem("y_ready_v")

        def in_pairs(engine, first, last, body):
            with engine.Fori(first // 2, last // 2) as m:
                body(m * 2 + 1, 1, m)
                body(m * 2 + 2, 0, m + 1)

        with nc.Block() as block:
            @block.sync
            def _(sp):
                def load(i, b):
                    sp.dma_start(rows[:, b], g.placed2[bass.ds(i * P, P), :]).then_inc(rows_in[b], 16)

                sp.dma_start(b1_rows[:], g.L1_ffn_b1.rearrange("e (m i) -> (e m) i", i=128)).then_inc(b1_in, 16)
                load(0, 0)
                load(1, 1)
                with sp.Fori(1, NT // 2) as m:
                    for b in range(2):
                        sp.wait_ge(x_ready, m * 2 + b - 1)
                        load(m * 2 + b, b)

            @block.gpsimd
            def _(pool):
                bound = pool.to_reg(2 * N - 1)
                with pool.Fori(0, NT // 2) as m:
                    for b in range(2):
                        pool.wait_ge(y_ready, m * 2 + b + 1)
                        pool.sem_inc(tile_held)
                        pool.indirect_dma_start(
                            out=g.results2, out_offset=bass.IndirectOffsetOnAxis(ap=target[:, b, 0:1], axis=0),
                            in_=y[:, b], in_offset=None, bounds_check=bound, oob_is_err=False).then_inc(y_out[b], 16)
                for b in range(2):
                    pool.wait_ge(y_out[b], 16 * (NT // 2))

            @block.tensor
            def _(pe):
                def turn_rows(i, b, m, first):
                    pe.wait_ge(rows_in[b], m * 16 + 16)
                    if not first:
                        pe.wait_ge(x_ready, i - 1)
                    for f in range(F):
                        mm = nc.tensor.transpose(p_x[b][:, f * P:(f + 1) * P], rows[:, b, f * 128:(f + 1) * 128],
                                                 g.ident[0:P, 0:P])
                    mm.then_inc(x_turned, 1)

                def up(i, b, first):
                    e = pe.value_load(g.expert_of[0:1, bass.ds(i, 1)], min_val=0, max_val=NE - 1)
                    pe.wait_ge(x_ready, i + 1)
                    if not first:
                        pe.wait_ge(up_read, i - 1)
                    for f in range(F):
                        mm = nc.tensor.matmul(p_up[b][0:P, :], xT[:, b, f, :],
                                              g.w1_all[:, bass.ds(e, 1), f, :].rearrange("p a o -> p (a o)"),
                                              start=(f == 0), stop=(f == F - 1))
                    mm.then_inc(up_done, 1)

                def turn_hidden(i, b, first):
                    pe.wait_ge(up_read, i + 1)
                    if not first:
                        pe.wait_ge(h_ready, i - 1)
                    for m in range(M2):
                        mm = nc.tensor.transpose(p_h[b][:, m * P:(m + 1) * P], before[:, b, m * 128:(m + 1) * 128],
                                                 g.ident[0:P, 0:P])
                    mm.then_inc(h_turned, 1)

                def down(i, b, first):
                    e = pe.value_load(g.expert_of[0:1, bass.ds(i, 1)], min_val=0, max_val=NE - 1)
                    pe.wait_ge(h_ready, i + 1)
                    if not first:
                        pe.wait_ge(y_ready, i - 1)
                    for m in range(M2):
                        mm = nc.tensor.matmul(p_y[b][0:P, 0:D], hidT[:, b, m, :],
                                              g.w2_all[:, bass.ds(e, 1), m, :].rearrange("p a o -> p (a o)"),
                                              start=(m == 0), stop=(m == M2 - 1))
                    mm.then_inc(down_done, 1)

                pe.wait_ge(b1_in, 16)
                nc.tensor.transpose(p_h[1][:, 0:NE * M2], b1_rows[:], g.ident[0:NE * M2, 0:NE * M2]).then_inc(b1_turned, 1)
                turn_rows(0, 0, 0, True)
                up(0, 0, True)
                turn_rows(1, 1, 0, True)
                turn_hidden(0, 0, True)
                pe.wait_ge(b1_ready, 1)
                up(1, 1, True)
                turn_rows(2, 0, 1, False)
                down(0, 0, True)
                turn_hidden(1, 1, True)
                up(2, 0, False)
                turn_rows(3, 1, 1, False)
                down(1, 1, True)
                turn_hidden(2, 0, False)

                def both(i, b, m):
                    up(i, b, False)
                    turn_rows(i + 1, 1 - b, m + b, False)
                    down(i - 1, 1 - b, False)
                    turn_hidden(i, b, False)

                in_pairs(pe, 3, NT - 1, both)
                up(NT - 1, 1, False)
                down(NT - 2, 0, False)
                turn_hidden(NT - 1, 1, False)
                down(NT - 1, 1, False)

            @block.scalar
            def _(act):
                act.wait_ge(b1_turned, 1)
                nc.scalar.copy(b1[:].rearrange("p e m -> p (e m)"), p_h[1][:, 0:NE * M2]).then_inc(b1_ready, 1)
                act.wait_ge(b1_ready, 1)

                def gelu(i, b, first):
                    e = act.value_load(g.expert_of[0:1, bass.ds(i, 1)], min_val=0, max_val=NE - 1)
                    act.wait_ge(h_turned, i + 1)
                    if not first:
                        act.wait_ge(down_done, i - 1)
                    for m in range(M2):
                        ins = nc.scalar.activation(hidT[:, b, m, :], p_h[b][:, m * P:(m + 1) * P], ACT.Gelu,
                                                   bias=b1[:, bass.ds(e, 1), m])
                    ins.then_inc(h_ready, 1)

                gelu(0, 0, True)
                gelu(1, 1, True)
                with act.Fori(1, NT // 2) as m:
                    for b in range(2):
                        gelu(m * 2 + b, b, False)

            @block.vector
            def _(dve):
                V = nc.vector

                def chain(before, ins):
                    ins.then_inc(target_step, 1)
                    dve.wait_ge(target_step, before + 1)

                def take_rows(i, b, first, i_from_2=True):
                    dve.wait_ge(x_turned, i + 1)
                    if not first:
                        dve.wait_ge(up_done, i - 1)
                    chain(4 * i - 4 if i_from_2 else 2 * i, V.tensor_copy(wanted[:, 1, b:b + 1], wanted[:, 0, b:b + 1]))
                    V.tensor_copy(wanted[:, 0, b:b + 1], rows[:, b, D:D + 1]).then_inc(target_step, 1)
                    V.tensor_copy(xT[:, b].rearrange("p f e -> p (f e)"), p_x[b][:, 0:F * P]).then_inc(x_ready, 1)

                def take_up(i, b, first):
                    dve.wait_ge(up_done, i + 1)
                    if not first:
                        dve.wait_ge(h_turned, i - 1)
                    V.tensor_copy(before[:, b], p_up[b][0:P, :]).then_inc(up_read, 1)

                def take_y(i, b, m, first, age=1):
                    dve.wait_ge(down_done, i + 1)
                    if not first:
                        dve.wait_ge(y_out[b], m * 16)
                    to = wanted[:, age, b:b + 1]
                    steps = 4 * i + 6 if age else 4 * NT - 4 + 2 * (i - NT + 2)
                    dve.wait_ge(target_step, steps)
                    chain(steps, V.tensor_scalar(empty[:, b:b + 1], to, 0.0, PAST + 1, ALU.is_equal, ALU.mult))
                    V.scalar_tensor_tensor(out=target[:, b, 0:1], in0=to, scalar=-1.0, in1=empty[:, b:b + 1],
                                           op0=ALU.add, op1=ALU.add).then_inc(target_step, 1)
                    V.tensor_copy(y[:, b], p_y[b][0:P, 0:D]).then_inc(y_ready, 1)

                V.memset(wanted[:], 0.0).then_inc(wanted_clear, 1)
                dve.wait_ge(wanted_clear, 1)
                take_rows(0, 0, True, i_from_2=False)
                take_up(0, 0, True)
                dve.wait_ge(target_step, 2)
                take_rows(1, 1, True, i_from_2=False)
                take_up(1, 1, True)
                take_rows(2, 0, False)
                take_y(0, 0, 0, True)
                take_up(2, 0, False)
                take_rows(3, 1, False)
                take_y(1, 1, 0, True)

                def both(i, b, m):
                    take_up(i, b, False)
                    take_rows(i + 1, 1 - b, False)
                    take_y(i - 1, 1 - b, m if b else m - 1, False)

                in_pairs(dve, 3, NT - 1, both)
                take_up(NT - 1, 1, False)
                take_y(NT - 2, 0, NT // 2 - 1, False, age=0)
                take_y(NT - 1, 1, NT // 2 - 1, False, age=0)


def combine_second(nc, g):
    FEW = 5
    with stage(nc) as (ctx, sem):
        y = ctx.enter_context(nc.sbuf_tensor(unique("y_u"), [P, 2, T, D], F32))
        loaded = [sem(f"loaded_u{m}") for m in range(T // FEW)]
        first_added, summed, x_out = sem("first_added"), sem("summed_u"), sem("x_out_u")
        by_tile = lambda a: a.rearrange("(t p) d -> p t d", p=P)
        with nc.Block() as block:
            @block.sync
            def _(sp):
                for m in range(T // FEW):
                    now = slice(m * FEW, (m + 1) * FEW)
                    for k in range(2):
                        sp.dma_start(y[:, k, now, :], by_tile(g.results2[k * N:(k + 1) * N, :])[:, now, :]).then_inc(
                            loaded[m], 16)

            @block.vector
            def _(dve):
                for t in range(T):
                    dve.wait_ge(loaded[t // FEW], 32)
                    for k in range(2):
                        if k:
                            dve.wait_ge(first_added, t + 1)
                        nc.vector.scalar_tensor_tensor(
                            out=g.xr[:, t, :], in0=y[:, k, t, :], scalar=g.shares[:, k, t:t + 1], in1=g.xr[:, t, :],
                            op0=ALU.mult, op1=ALU.add).then_inc(summed if k else first_added, 1)

            @block.scalar
            def _(act):
                for m in range(T // FEW):
                    now = slice(m * FEW, (m + 1) * FEW)
                    act.wait_ge(summed, (m + 1) * FEW)
                    act.dma_start(by_tile(g.out)[:, now, :], g.xr[:, now, :]).then_inc(x_out, 16)
                act.wait_ge(x_out, T // FEW * 16)


def second_ffn(nc, g):
    with ExitStack() as ctx:
        sb = lambda n, s, d: ctx.enter_context(nc.sbuf_tensor(unique(n), s, d))
        g.shares = sb("shares", [P, 2, T], F32)
        g.expert_of = sb("expert_of", [1, NT], I32)
        g.w1_all, g.w2_all = sb("w1_all", [128, NE, F, F2], F32), sb("w2_all", [128, NE, F2 // 128, D], F32)
        w_all_in = nc.alloc_semaphore(name=unique("w_all_in"))
        route_second(nc, g, w_all_in)
        with nc.Block() as block:
            @block.tensor
            def _(pe):
                pe.wait_ge(w_all_in, NE * 32)
        second_experts(nc, g)
        nc.clear_and_free_semaphores([w_all_in])
        nc.all_engine_barrier()
        combine_second(nc, g)


def prepare(nc, g):
    with stage(nc) as (_, sem):
        ones_ready, ready = sem("ones_ready"), sem("consts_ready")
        with nc.Block() as block:
            @block.gpsimd
            def _(pool):
                pool.iota(g.iota[:], pattern=[[1, 128]], base=0, channel_multiplier=0,
                          allow_small_or_imprecise_dtypes=True).then_inc(ready, 1)
                pool.memset(g.ones[:], 1.0).then_inc(ones_ready, 1)
                pool.wait_ge(ones_ready, 1)
                pool.affine_select(out=g.ident[:], in_=g.ones[:], compare_op=ALU.is_equal, fill=0.0, base=0,
                                   pattern=[[-1, 128]], channel_multiplier=1).then_inc(ready, 1)
                pool.wait_ge(ready, 2)


def program(nc, g):
    dram = lambda n, s: nc.dram_tensor(n, s, F32).ap()
    g.slots = dram("slots", (NB * P, 2))
    g.xn, g.weights, g.dinv = dram("xn_dram", (N, D)), dram("weights_dram", (N, N)), dram("dinv_dram", (N,))
    g.edge_rec, g.edge_key, g.edge_rank = dram("edge_rec", (P, 2 * EC)), dram("edge_key", (P, EC)), dram("edge_rank", (P, EC))
    g.high = nc.dram_tensor("high_counts", (N, N), BF16).ap()
    g.placed, g.results = dram("placed_dram", (NE * CP, D + 2)), dram("results_dram", (N, D))
    g.placed2, g.results2 = dram("placed2_dram", (NT * P, D + 1)), dram("results2_dram", (2 * N, D))
    with ExitStack() as whole:
        keep = lambda ctx, n, s, d: ctx.enter_context(nc.sbuf_tensor(unique(n), s, d))
        g.spare = keep(whole, "spare", [128, 4], F32)
        g.ident, g.ones = keep(whole, "ident", [128, 128], F32), keep(whole, "ones", [128, 128], F32)
        g.iota = keep(whole, "iota", [128, 128], BF16)
        g.rounds, g.offset = keep(whole, "rounds", [1, 1], I32), keep(whole, "offset", [P, 1], F32)
        g.deg = keep(whole, "deg", [P, T, 4], F32)
        prepare(nc, g)
        g.dyn, g.h = keep(whole, "dyn", [P, T, C0], F32), keep(whole, "h", [P, T, C0], F32)
        with ExitStack() as graph:
            g.xparts = keep(graph, "xparts", [P, T, 3, C0], BF16)
            with ExitStack() as ctx:
                g.x_in = keep(ctx, "x_in", [P, T, D], F32)
                g.ranks = keep(ctx, "ranks", [P, EC], F32)
                sort_edges(nc, g)
                count_rounds(nc, g)
                normalise_input(nc, g)
            g.counts = keep(graph, "counts", [P, T, N], BF16)
            with ExitStack() as build:
                g.slot_w, g.slot_ids = keep(build, "slot_w", [P, NB], F32), keep(build, "slot_ids", [P, 2, NB], F32)
                g.slot_deg = keep(build, "slot_deg", [P, NB, 4], BF16)
                load_slots(nc, g)
                build_blocks(nc, g)
                further_rounds(nc, g)
            g.parts, g.own = (g.xparts, keep(graph, "parts", [P, T, 3, C0], BF16)), keep(graph, "own", [P, T, C0], F32)
            g.w_static, g.b_static = keep(graph, "w_static", [C0, 3, C0], F32), keep(graph, "b_static", [P, 3, C0], F32)
            g.dinv_s = keep(graph, "dinv_s", [P, T], F32)
            static_degrees(nc, g)
            static_messages(nc, g)
            for i in range(3):
                add_high_counts(nc, g, i)
                static_sums(nc, g, i)
        g.xr = keep(whole, "xr", [P, T, D], F32)
        first_gnn_out(nc, g)
        route_first(nc, g)
        first_experts(nc, g)
        combine_first(nc, g)
        second_gnn(nc, g)
        second_ffn(nc, g)


_INS = ["x", "src", "dst", "edge_weight", "L0_gnn_W_static", "L0_gnn_b_static", "L0_gnn_W1", "L0_gnn_b1", "L0_gnn_W2",
        "L0_gnn_b2", "L0_gnn_W_aggr", "L0_gnn_b_aggr", "L0_ffn_gate_w", "L0_ffn_gate_b", "L0_ffn_w1", "L0_ffn_b1",
        "L0_ffn_w2", "L0_ffn_b2", "L1_gnn_W1", "L1_gnn_b1", "L1_gnn_W2", "L1_gnn_b2", "L1_gnn_gamma", "L1_gnn_beta",
        "L1_ffn_gamma", "L1_ffn_beta", "L1_ffn_Wr", "L1_ffn_br", "L1_ffn_W1", "L1_ffn_b1", "L1_ffn_W2", "L1_ffn_b2"]


class Tensors:
    pass


def kernel(**inputs):
    import numpy as _np
    import concourse.bacc as _bacc
    from concourse import mybir as _mybir
    from concourse.bass_utils import run_bass_kernel_spmd as _run

    nc = _bacc.Bacc("TRN2", target_bir_lowering=False, num_devices=1)
    arrays, g = {}, Tensors()
    for name in _INS:
        a = _np.ascontiguousarray(inputs[name])
        arrays[f"in_{name}_dram"] = a
        g.__dict__[name] = nc.dram_tensor(f"in_{name}_dram", a.shape, _mybir.dt.from_np(a.dtype),
                                          kind="ExternalInput").ap()
    g.out = nc.dram_tensor("out_0_dram", (N, D), _mybir.dt.float32, kind="ExternalOutput").ap()
    program(nc, g)
    r = _run(nc, [arrays], core_ids=[0])
    return r.results[0]["out_0_dram"]
```
